# Optimizing a Trainium2 kernel written in Bass

```python
import numpy as np
import jax
import jax.numpy as jnp

def _softmax(x, axis=-1):
    return jax.nn.softmax(x, axis=axis)

def _gelu(x):
    return jax.nn.gelu(x, approximate=True)

def _silu(x):
    return jax.nn.silu(x)

def _sigmoid(x):
    return jax.nn.sigmoid(x)

def _layernorm(x, axis=-1, eps=1e-05):
    m = jnp.mean(x, axis=axis, keepdims=True)
    v = jnp.var(x, axis=axis, keepdims=True)
    return (x - m) / jnp.sqrt(v + eps)

def _scatter_add(tgt, idx, src, axis=0):
    return tgt.at[idx].add(src)

def _segment_sum(src, seg, n):
    return jax.ops.segment_sum(src, seg, n)
kernel_name = 'mk_conv_seq_d4_conv_nchw256_r4_854a8d'

def setup_inputs(seed: int=0):
    np.random.seed(seed)
    _w = jnp.asarray

    def _rec_inputs():
        import jax
        import jax.numpy as jnp
        _gk = jax.random.key(seed)
        x = -0.000125 + 0.9999 * jax.random.normal(jax.random.fold_in(_gk, 1), (8, 64, 32, 32), jnp.float32)
        return x
    x = _rec_inputs()

    def _L0_conv_setup():
        import jax, jax.numpy as jnp
        import numpy as np
        WS = 8
        HEADS = 8
        EPS = 1e-05

        def _rel_pos_index(ws):
            coords = np.stack(np.meshgrid(np.arange(ws), np.arange(ws), indexing='ij')).reshape(2, -1)
            rel = coords[:, :, None] - coords[:, None, :]
            rel = rel.transpose(1, 2, 0).astype(np.int64)
            rel[..., 0] += ws - 1
            rel[..., 1] += ws - 1
            rel[..., 0] *= 2 * ws - 1
            return jnp.asarray(rel.sum(-1))
        REL_IDX = _rel_pos_index(WS)

        def _layernorm(x, scale, bias):
            mu = jnp.mean(x, axis=-1, keepdims=True)
            var = jnp.mean(jnp.square(x - mu), axis=-1, keepdims=True)
            return (x - mu) * jax.lax.rsqrt(var + EPS) * scale + bias

        def _window_attention(xw, w_qkv, b_qkv, w_proj, b_proj, rel_bias_table):
            Bn, N, C = xw.shape
            d = C // HEADS
            scale = d ** (-0.5)
            qkv = xw @ w_qkv + b_qkv
            qkv = qkv.reshape(Bn, N, 3, HEADS, d)
            q, k, v = (qkv[:, :, 0], qkv[:, :, 1], qkv[:, :, 2])
            attn = jnp.einsum('bnhd,bmhd->bhnm', q * scale, k)
            bias = rel_bias_table[REL_IDX.reshape(-1)].reshape(N, N, HEADS)
            attn = attn + bias.transpose(2, 0, 1)[None]
            attn = jax.nn.softmax(attn, axis=-1)
            out = jnp.einsum('bhnm,bmhd->bnhd', attn, v).reshape(Bn, N, C)
            return out @ w_proj + b_proj
        key = jax.random.key(seed)
        ks = jax.random.split(key, 8)
        B, C, H, W = (8, 64, 32, 32)
        hid = 4 * C
        nb = (2 * WS - 1) ** 2
        return {'x': jax.random.normal(ks[0], (B, C, H, W), jnp.float32), 'ln1_scale': jnp.ones((C,), jnp.float32), 'ln1_bias': jnp.zeros((C,), jnp.float32), 'w_qkv': jax.random.normal(ks[1], (C, 3 * C), jnp.float32) * 0.02, 'b_qkv': jnp.zeros((3 * C,), jnp.float32), 'w_proj': jax.random.normal(ks[2], (C, C), jnp.float32) * 0.02, 'b_proj': jnp.zeros((C,), jnp.float32), 'rel_bias_table': jax.random.normal(ks[3], (nb, HEADS), jnp.float32) * 0.02, 'ln2_scale': jnp.ones((C,), jnp.float32), 'ln2_bias': jnp.zeros((C,), jnp.float32), 'w_mlp1': jax.random.normal(ks[4], (C, hid), jnp.float32) * 0.02, 'b_mlp1': jnp.zeros((hid,), jnp.float32), 'w_mlp2': jax.random.normal(ks[5], (hid, C), jnp.float32) * 0.02, 'b_mlp2': jnp.zeros((C,), jnp.float32)}
    _L0_conv_all = _L0_conv_setup()
    _L0_conv_in = {k: v for k, v in _L0_conv_all.items() if k in ('ln1_scale', 'ln1_bias', 'w_qkv', 'b_qkv', 'w_proj', 'b_proj', 'rel_bias_table', 'ln2_scale', 'ln2_bias', 'w_mlp1', 'b_mlp1', 'w_mlp2', 'b_mlp2')}
    del _L0_conv_all

    def _L1_conv_setup():
        import jax, jax.numpy as jnp
        import numpy as np
        UP, DOWN = (2, 2)
        PAD = (11, 11, 11, 11)
        NEG_SLOPE = 0.2
        CLAMP = 256.0
        GAIN = float(np.sqrt(2.0))

        def _depthwise_fir(x, f, up, down, pad):
            C = x.shape[1]
            k = jnp.broadcast_to(f[None, None], (C, 1, f.shape[0], f.shape[1]))
            return jax.lax.conv_general_dilated(x, k, window_strides=(down, down), padding=((pad[0], pad[1]), (pad[2], pad[3])), lhs_dilation=(up, up), dimension_numbers=('NCHW', 'OIHW', 'NCHW'), feature_group_count=C)

        def _make_kaiser_filter(taps=12, beta=6.0):
            t = np.kaiser(taps, beta)
            f = np.outer(t, t)
            return (f / f.sum()).astype(np.float32)
        key = jax.random.key(seed)
        k1, k2 = jax.random.split(key)
        B, C, H, W = (8, 64, 32, 32)
        x = jax.random.normal(k1, (B, C, H, W), dtype=jnp.float32)
        bias = jax.random.normal(k2, (C,), dtype=jnp.float32) * 0.1
        f = _make_kaiser_filter(12, 6.0)
        up_filter = jnp.asarray(f * (UP * UP))
        down_filter = jnp.asarray(f)
        return {'input': x, 'bias': bias, 'up_filter': up_filter, 'down_filter': down_filter}
    _L1_conv_all = _L1_conv_setup()
    _L1_conv_in = {k: v for k, v in _L1_conv_all.items() if k in ('bias', 'up_filter', 'down_filter')}
    del _L1_conv_all

    def _L2_conv_setup():
        import jax, jax.numpy as jnp
        from jax import lax
        import numpy as np
        import math
        B, CH, H, W = (4, 64, 16, 16)
        TOK = 8
        GCN = math.ceil(CH / TOK)
        PAD = TOK * GCN
        DIN = 2 * GCN
        DSTATE = 16
        DTR = math.ceil(GCN / 16)
        GROUPS = 4
        EPS = 1e-05

        def _forward(x, W_in, W_x, W_dt, b_dt, A_logs, Ds, W_out, gn_w, gn_b):
            b, c, h, w = x.shape
            M = b * h * w
            xf = jnp.transpose(x, (0, 2, 3, 1)).reshape(M, TOK, GCN)
            xz = xf @ W_in
            xp, z = (xz[..., :DIN], xz[..., DIN:])
            xs = jnp.concatenate([xp, xp[:, ::-1]], axis=0)
            x_dbl = xs @ W_x
            dts = x_dbl[..., :DTR]
            Bs = x_dbl[..., DTR:DTR + DSTATE]
            Cs = x_dbl[..., DTR + DSTATE:]
            dts = dts @ W_dt + b_dt
            A = -jnp.exp(A_logs)
            delta = jax.nn.softplus(dts + b_dt)

            def step(hst, inp):
                d_t, u_t, B_t, C_t = inp
                dA = jnp.exp(d_t[:, :, None] * A)
                hst = dA * hst + (d_t * u_t)[:, :, None] * B_t[:, None, :]
                y_t = jnp.einsum('bdn,bn->bd', hst, C_t)
                return (hst, y_t)
            h0 = jnp.zeros((2 * M, DIN, DSTATE), dtype=x.dtype)
            scan_in = (jnp.swapaxes(delta, 0, 1), jnp.swapaxes(xs, 0, 1), jnp.swapaxes(Bs, 0, 1), jnp.swapaxes(Cs, 0, 1))
            _, ys = lax.scan(step, h0, scan_in)
            ys = jnp.swapaxes(ys, 0, 1) + xs * Ds
            y1, y2 = (ys[:M], ys[M:])
            y = y1 + y2[:, ::-1]
            y = y * jax.nn.gelu(z, approximate=False)
            y = y @ W_out
            y = y.reshape(b, h, w, PAD).transpose(0, 3, 1, 2)
            yg = y.reshape(b, GROUPS, -1)
            mu = yg.mean(-1, keepdims=True)
            var = yg.var(-1, keepdims=True)
            yg = (yg - mu) * lax.rsqrt(var + EPS)
            y = yg.reshape(b, PAD, h, w) * gn_w[None, :, None, None] + gn_b[None, :, None, None]
            return x + y[:, :c]
        key = jax.random.key(seed)
        ks = jax.random.split(key, 8)
        x = jax.random.normal(ks[0], (B, CH, H, W), dtype=jnp.float32)
        W_in = jax.random.normal(ks[1], (GCN, 2 * DIN), dtype=jnp.float32) * 0.05
        W_x = jax.random.normal(ks[2], (DIN, DTR + 2 * DSTATE), dtype=jnp.float32) * 0.05
        dt_init_std = DTR ** (-0.5)
        W_dt = jax.random.uniform(ks[3], (DTR, DIN), dtype=jnp.float32, minval=-dt_init_std, maxval=dt_init_std)
        dt = jnp.exp(jax.random.uniform(ks[4], (DIN,), dtype=jnp.float32) * (math.log(0.1) - math.log(0.001)) + math.log(0.001))
        dt = jnp.clip(dt, 0.0001)
        b_dt = dt + jnp.log(-jnp.expm1(-dt))
        A_logs = jnp.log(jnp.broadcast_to(jnp.arange(1, DSTATE + 1, dtype=jnp.float32), (DIN, DSTATE)))
        Ds = jnp.ones((DIN,), dtype=jnp.float32)
        W_out = jax.random.normal(ks[5], (DIN, GCN), dtype=jnp.float32) * 0.05
        gn_w = jnp.ones((PAD,), dtype=jnp.float32)
        gn_b = jnp.zeros((PAD,), dtype=jnp.float32)
        return {'x': x, 'W_in': W_in, 'W_x': W_x, 'W_dt': W_dt, 'b_dt': b_dt, 'A_logs': A_logs, 'Ds': Ds, 'W_out': W_out, 'gn_w': gn_w, 'gn_b': gn_b}
    _L2_conv_all = _L2_conv_setup()
    _L2_conv_in = {k: v for k, v in _L2_conv_all.items() if k in ('W_in', 'W_x', 'W_dt', 'b_dt', 'A_logs', 'Ds', 'W_out', 'gn_w', 'gn_b')}
    del _L2_conv_all

    def _L3_conv_setup():
        import jax, jax.numpy as jnp
        import numpy as np
        from jax import lax

        def layer_norm(x, w, b, eps=1e-05):
            mu = x.mean(-1, keepdims=True)
            var = ((x - mu) ** 2).mean(-1, keepdims=True)
            return (x - mu) / jnp.sqrt(var + eps) * w + b

        def mamba_fwd(x, in_w, conv_w, conv_b, xproj_w, dt_w, dt_b, A_log, Dp, out_w):
            Bb, L, dm = x.shape
            di = in_w.shape[0] // 2
            ds = A_log.shape[1]
            dr = dt_w.shape[1]
            xz = x @ in_w.T
            xi, z = (xz[..., :di], xz[..., di:])
            xc = lax.conv_general_dilated(xi.transpose(0, 2, 1), conv_w, (1,), [(conv_w.shape[-1] - 1, 0)], feature_group_count=di, dimension_numbers=('NCH', 'OIH', 'NCH'))
            xc = jax.nn.silu(xc + conv_b[None, :, None]).transpose(0, 2, 1)
            dbl = xc @ xproj_w.T
            dtr = dbl[..., :dr]
            Bs = dbl[..., dr:dr + ds]
            Cs = dbl[..., dr + ds:]
            dt = jax.nn.softplus(dtr @ dt_w.T + dt_b)
            A = -jnp.exp(A_log)

            def step(h, inp):
                dt_t, B_t, C_t, x_t = inp
                dA = jnp.exp(dt_t[..., None] * A)
                h = dA * h + (dt_t * x_t)[..., None] * B_t[:, None, :]
                y = jnp.einsum('bds,bs->bd', h, C_t)
                return (h, y)
            h0 = jnp.zeros((Bb, di, ds), x.dtype)
            _, ys = lax.scan(step, h0, (dt.transpose(1, 0, 2), Bs.transpose(1, 0, 2), Cs.transpose(1, 0, 2), xc.transpose(1, 0, 2)))
            y = ys.transpose(1, 0, 2) + xc * Dp
            y = y * jax.nn.silu(z)
            return y @ out_w.T

        def forward(x, ln_w, ln_b, skip_scale, proj_w, proj_b, in_w, conv_w, conv_b, xproj_w, dt_w, dt_b, A_log, Dp, out_w, fc1_w, fc1_b, fc2_w, fc2_b):
            B, C, H, W = x.shape
            L = H * W
            dm = C // 4
            xf = x.reshape(B, C, L).transpose(0, 2, 1)
            xn = layer_norm(xf, ln_w, ln_b)
            chunks = xn.reshape(B, L, 4, dm).transpose(2, 0, 1, 3).reshape(4 * B, L, dm)
            ym = mamba_fwd(chunks, in_w, conv_w, conv_b, xproj_w, dt_w, dt_b, A_log, Dp, out_w)
            ym = ym + skip_scale * chunks
            ym = ym.reshape(4, B, L, dm).transpose(1, 2, 0, 3).reshape(B, L, C)
            ym = layer_norm(ym, ln_w, ln_b)
            ym = ym @ proj_w.T + proj_b
            tm = ym.transpose(0, 2, 1).reshape(B, C, H, W)
            out = x + tm
            h = jnp.einsum('bchw,oc->bohw', out, fc1_w) + fc1_b[None, :, None, None]
            h = jax.nn.gelu(h, approximate=False)
            m = jnp.einsum('bchw,oc->bohw', h, fc2_w) + fc2_b[None, :, None, None]
            return out + m + x
        key = jax.random.key(seed)
        ks = jax.random.split(key, 10)
        B, C, H, W = (4, 64, 16, 16)
        dm, di, ds, dr, dc = (16, 32, 16, 4, 4)
        s = 0.02
        return {'x': jax.random.normal(ks[0], (B, C, H, W), jnp.float32), 'ln_w': jnp.ones((C,), jnp.float32), 'ln_b': jnp.zeros((C,), jnp.float32), 'skip_scale': jnp.ones((1,), jnp.float32), 'proj_w': jax.random.normal(ks[1], (C, C), jnp.float32) * s, 'proj_b': jnp.zeros((C,), jnp.float32), 'in_w': jax.random.normal(ks[2], (2 * di, dm), jnp.float32) * s, 'conv_w': jax.random.normal(ks[3], (di, 1, dc), jnp.float32) * s, 'conv_b': jnp.zeros((di,), jnp.float32), 'xproj_w': jax.random.normal(ks[4], (dr + 2 * ds, di), jnp.float32) * s, 'dt_w': jax.random.normal(ks[5], (di, dr), jnp.float32) * s, 'dt_b': jnp.full((di,), -4.6, jnp.float32), 'A_log': jnp.log(jnp.broadcast_to(jnp.arange(1, ds + 1, dtype=jnp.float32), (di, ds))), 'Dp': jnp.ones((di,), jnp.float32), 'out_w': jax.random.normal(ks[6], (dm, di), jnp.float32) * s, 'fc1_w': jax.random.normal(ks[7], (4 * C, C), jnp.float32) * s, 'fc1_b': jnp.zeros((4 * C,), jnp.float32), 'fc2_w': jax.random.normal(ks[8], (C, 4 * C), jnp.float32) * s, 'fc2_b': jnp.zeros((C,), jnp.float32)}
    _L3_conv_all = _L3_conv_setup()
    _L3_conv_in = {k: v for k, v in _L3_conv_all.items() if k in ('ln_w', 'ln_b', 'skip_scale', 'proj_w', 'proj_b', 'in_w', 'conv_w', 'conv_b', 'xproj_w', 'dt_w', 'dt_b', 'A_log', 'Dp', 'out_w', 'fc1_w', 'fc1_b', 'fc2_w', 'fc2_b')}
    del _L3_conv_all
    return {'x': x, 'L0_conv_ln1_scale': _L0_conv_in['ln1_scale'], 'L0_conv_ln1_bias': _L0_conv_in['ln1_bias'], 'L0_conv_w_qkv': _L0_conv_in['w_qkv'], 'L0_conv_b_qkv': _L0_conv_in['b_qkv'], 'L0_conv_w_proj': _L0_conv_in['w_proj'], 'L0_conv_b_proj': _L0_conv_in['b_proj'], 'L0_conv_rel_bias_table': _L0_conv_in['rel_bias_table'], 'L0_conv_ln2_scale': _L0_conv_in['ln2_scale'], 'L0_conv_ln2_bias': _L0_conv_in['ln2_bias'], 'L0_conv_w_mlp1': _L0_conv_in['w_mlp1'], 'L0_conv_b_mlp1': _L0_conv_in['b_mlp1'], 'L0_conv_w_mlp2': _L0_conv_in['w_mlp2'], 'L0_conv_b_mlp2': _L0_conv_in['b_mlp2'], 'L1_conv_bias': _L1_conv_in['bias'], 'L1_conv_up_filter': _L1_conv_in['up_filter'], 'L1_conv_down_filter': _L1_conv_in['down_filter'], 'L2_conv_W_in': _L2_conv_in['W_in'], 'L2_conv_W_x': _L2_conv_in['W_x'], 'L2_conv_W_dt': _L2_conv_in['W_dt'], 'L2_conv_b_dt': _L2_conv_in['b_dt'], 'L2_conv_A_logs': _L2_conv_in['A_logs'], 'L2_conv_Ds': _L2_conv_in['Ds'], 'L2_conv_W_out': _L2_conv_in['W_out'], 'L2_conv_gn_w': _L2_conv_in['gn_w'], 'L2_conv_gn_b': _L2_conv_in['gn_b'], 'L3_conv_ln_w': _L3_conv_in['ln_w'], 'L3_conv_ln_b': _L3_conv_in['ln_b'], 'L3_conv_skip_scale': _L3_conv_in['skip_scale'], 'L3_conv_proj_w': _L3_conv_in['proj_w'], 'L3_conv_proj_b': _L3_conv_in['proj_b'], 'L3_conv_in_w': _L3_conv_in['in_w'], 'L3_conv_conv_w': _L3_conv_in['conv_w'], 'L3_conv_conv_b': _L3_conv_in['conv_b'], 'L3_conv_xproj_w': _L3_conv_in['xproj_w'], 'L3_conv_dt_w': _L3_conv_in['dt_w'], 'L3_conv_dt_b': _L3_conv_in['dt_b'], 'L3_conv_A_log': _L3_conv_in['A_log'], 'L3_conv_Dp': _L3_conv_in['Dp'], 'L3_conv_out_w': _L3_conv_in['out_w'], 'L3_conv_fc1_w': _L3_conv_in['fc1_w'], 'L3_conv_fc1_b': _L3_conv_in['fc1_b'], 'L3_conv_fc2_w': _L3_conv_in['fc2_w'], 'L3_conv_fc2_b': _L3_conv_in['fc2_b']}

def reference(x, L0_conv_ln1_scale, L0_conv_ln1_bias, L0_conv_w_qkv, L0_conv_b_qkv, L0_conv_w_proj, L0_conv_b_proj, L0_conv_rel_bias_table, L0_conv_ln2_scale, L0_conv_ln2_bias, L0_conv_w_mlp1, L0_conv_b_mlp1, L0_conv_w_mlp2, L0_conv_b_mlp2, L1_conv_bias, L1_conv_up_filter, L1_conv_down_filter, L2_conv_W_in, L2_conv_W_x, L2_conv_W_dt, L2_conv_b_dt, L2_conv_A_logs, L2_conv_Ds, L2_conv_W_out, L2_conv_gn_w, L2_conv_gn_b, L3_conv_ln_w, L3_conv_ln_b, L3_conv_skip_scale, L3_conv_proj_w, L3_conv_proj_b, L3_conv_in_w, L3_conv_conv_w, L3_conv_conv_b, L3_conv_xproj_w, L3_conv_dt_w, L3_conv_dt_b, L3_conv_A_log, L3_conv_Dp, L3_conv_out_w, L3_conv_fc1_w, L3_conv_fc1_b, L3_conv_fc2_w, L3_conv_fc2_b):
    import jax
    import jax.numpy as jnp

    def _L0_conv_ref(x, ln1_scale, ln1_bias, w_qkv, b_qkv, w_proj, b_proj, rel_bias_table, ln2_scale, ln2_bias, w_mlp1, b_mlp1, w_mlp2, b_mlp2):
        import jax, jax.numpy as jnp
        import numpy as np
        WS = 8
        HEADS = 8
        EPS = 1e-05

        def _rel_pos_index(ws):
            coords = np.stack(np.meshgrid(np.arange(ws), np.arange(ws), indexing='ij')).reshape(2, -1)
            rel = coords[:, :, None] - coords[:, None, :]
            rel = rel.transpose(1, 2, 0).astype(np.int64)
            rel[..., 0] += ws - 1
            rel[..., 1] += ws - 1
            rel[..., 0] *= 2 * ws - 1
            return jnp.asarray(rel.sum(-1))
        REL_IDX = _rel_pos_index(WS)

        def _layernorm(x, scale, bias):
            mu = jnp.mean(x, axis=-1, keepdims=True)
            var = jnp.mean(jnp.square(x - mu), axis=-1, keepdims=True)
            return (x - mu) * jax.lax.rsqrt(var + EPS) * scale + bias

        def _window_attention(xw, w_qkv, b_qkv, w_proj, b_proj, rel_bias_table):
            Bn, N, C = xw.shape
            d = C // HEADS
            scale = d ** (-0.5)
            qkv = xw @ w_qkv + b_qkv
            qkv = qkv.reshape(Bn, N, 3, HEADS, d)
            q, k, v = (qkv[:, :, 0], qkv[:, :, 1], qkv[:, :, 2])
            attn = jnp.einsum('bnhd,bmhd->bhnm', q * scale, k)
            bias = rel_bias_table[REL_IDX.reshape(-1)].reshape(N, N, HEADS)
            attn = attn + bias.transpose(2, 0, 1)[None]
            attn = jax.nn.softmax(attn, axis=-1)
            out = jnp.einsum('bhnm,bmhd->bnhd', attn, v).reshape(Bn, N, C)
            return out @ w_proj + b_proj
        B, C, H, W = x.shape
        xc = jnp.transpose(x, (0, 2, 3, 1))
        xn = _layernorm(xc, ln1_scale, ln1_bias)
        nh, nw = (H // WS, W // WS)
        win = xn.reshape(B, nh, WS, nw, WS, C).transpose(0, 1, 3, 2, 4, 5)
        win = win.reshape(B * nh * nw, WS * WS, C)
        aw = _window_attention(win, w_qkv, b_qkv, w_proj, b_proj, rel_bias_table)
        x_attn = aw.reshape(B, nh, nw, WS, WS, C).transpose(0, 1, 3, 2, 4, 5).reshape(B, H, W, C)
        xc = xc + x_attn
        h = _layernorm(xc, ln2_scale, ln2_bias)
        h = jax.nn.gelu(h @ w_mlp1 + b_mlp1, approximate=False) @ w_mlp2 + b_mlp2
        xc = xc + h
        return jnp.transpose(xc, (0, 3, 1, 2))

    def _L1_conv_ref(input, bias, up_filter, down_filter):
        import jax, jax.numpy as jnp
        import numpy as np
        UP, DOWN = (2, 2)
        PAD = (11, 11, 11, 11)
        NEG_SLOPE = 0.2
        CLAMP = 256.0
        GAIN = float(np.sqrt(2.0))

        def _depthwise_fir(x, f, up, down, pad):
            C = x.shape[1]
            k = jnp.broadcast_to(f[None, None], (C, 1, f.shape[0], f.shape[1]))
            return jax.lax.conv_general_dilated(x, k, window_strides=(down, down), padding=((pad[0], pad[1]), (pad[2], pad[3])), lhs_dilation=(up, up), dimension_numbers=('NCHW', 'OIHW', 'NCHW'), feature_group_count=C)

        def _make_kaiser_filter(taps=12, beta=6.0):
            t = np.kaiser(taps, beta)
            f = np.outer(t, t)
            return (f / f.sum()).astype(np.float32)
        x = input + bias[None, :, None, None]
        x = _depthwise_fir(x, up_filter, UP, 1, PAD)
        x = jnp.where(x >= 0, x, NEG_SLOPE * x) * GAIN
        x = jnp.clip(x, -CLAMP, CLAMP)
        x = _depthwise_fir(x, down_filter, 1, DOWN, (0, 0, 0, 0))
        return x

    def _L2_conv_ref(x, W_in, W_x, W_dt, b_dt, A_logs, Ds, W_out, gn_w, gn_b):
        import jax, jax.numpy as jnp
        from jax import lax
        import numpy as np
        import math
        B, CH, H, W = (4, 64, 16, 16)
        TOK = 8
        GCN = math.ceil(CH / TOK)
        PAD = TOK * GCN
        DIN = 2 * GCN
        DSTATE = 16
        DTR = math.ceil(GCN / 16)
        GROUPS = 4
        EPS = 1e-05

        def _forward(x, W_in, W_x, W_dt, b_dt, A_logs, Ds, W_out, gn_w, gn_b):
            b, c, h, w = x.shape
            M = b * h * w
            xf = jnp.transpose(x, (0, 2, 3, 1)).reshape(M, TOK, GCN)
            xz = xf @ W_in
            xp, z = (xz[..., :DIN], xz[..., DIN:])
            xs = jnp.concatenate([xp, xp[:, ::-1]], axis=0)
            x_dbl = xs @ W_x
            dts = x_dbl[..., :DTR]
            Bs = x_dbl[..., DTR:DTR + DSTATE]
            Cs = x_dbl[..., DTR + DSTATE:]
            dts = dts @ W_dt + b_dt
            A = -jnp.exp(A_logs)
            delta = jax.nn.softplus(dts + b_dt)

            def step(hst, inp):
                d_t, u_t, B_t, C_t = inp
                dA = jnp.exp(d_t[:, :, None] * A)
                hst = dA * hst + (d_t * u_t)[:, :, None] * B_t[:, None, :]
                y_t = jnp.einsum('bdn,bn->bd', hst, C_t)
                return (hst, y_t)
            h0 = jnp.zeros((2 * M, DIN, DSTATE), dtype=x.dtype)
            scan_in = (jnp.swapaxes(delta, 0, 1), jnp.swapaxes(xs, 0, 1), jnp.swapaxes(Bs, 0, 1), jnp.swapaxes(Cs, 0, 1))
            _, ys = lax.scan(step, h0, scan_in)
            ys = jnp.swapaxes(ys, 0, 1) + xs * Ds
            y1, y2 = (ys[:M], ys[M:])
            y = y1 + y2[:, ::-1]
            y = y * jax.nn.gelu(z, approximate=False)
            y = y @ W_out
            y = y.reshape(b, h, w, PAD).transpose(0, 3, 1, 2)
            yg = y.reshape(b, GROUPS, -1)
            mu = yg.mean(-1, keepdims=True)
            var = yg.var(-1, keepdims=True)
            yg = (yg - mu) * lax.rsqrt(var + EPS)
            y = yg.reshape(b, PAD, h, w) * gn_w[None, :, None, None] + gn_b[None, :, None, None]
            return x + y[:, :c]
        return _forward(x, W_in, W_x, W_dt, b_dt, A_logs, Ds, W_out, gn_w, gn_b)

    def _L3_conv_ref(x, ln_w, ln_b, skip_scale, proj_w, proj_b, in_w, conv_w, conv_b, xproj_w, dt_w, dt_b, A_log, Dp, out_w, fc1_w, fc1_b, fc2_w, fc2_b):
        import jax, jax.numpy as jnp
        import numpy as np
        from jax import lax

        def layer_norm(x, w, b, eps=1e-05):
            mu = x.mean(-1, keepdims=True)
            var = ((x - mu) ** 2).mean(-1, keepdims=True)
            return (x - mu) / jnp.sqrt(var + eps) * w + b

        def mamba_fwd(x, in_w, conv_w, conv_b, xproj_w, dt_w, dt_b, A_log, Dp, out_w):
            Bb, L, dm = x.shape
            di = in_w.shape[0] // 2
            ds = A_log.shape[1]
            dr = dt_w.shape[1]
            xz = x @ in_w.T
            xi, z = (xz[..., :di], xz[..., di:])
            xc = lax.conv_general_dilated(xi.transpose(0, 2, 1), conv_w, (1,), [(conv_w.shape[-1] - 1, 0)], feature_group_count=di, dimension_numbers=('NCH', 'OIH', 'NCH'))
            xc = jax.nn.silu(xc + conv_b[None, :, None]).transpose(0, 2, 1)
            dbl = xc @ xproj_w.T
            dtr = dbl[..., :dr]
            Bs = dbl[..., dr:dr + ds]
            Cs = dbl[..., dr + ds:]
            dt = jax.nn.softplus(dtr @ dt_w.T + dt_b)
            A = -jnp.exp(A_log)

            def step(h, inp):
                dt_t, B_t, C_t, x_t = inp
                dA = jnp.exp(dt_t[..., None] * A)
                h = dA * h + (dt_t * x_t)[..., None] * B_t[:, None, :]
                y = jnp.einsum('bds,bs->bd', h, C_t)
                return (h, y)
            h0 = jnp.zeros((Bb, di, ds), x.dtype)
            _, ys = lax.scan(step, h0, (dt.transpose(1, 0, 2), Bs.transpose(1, 0, 2), Cs.transpose(1, 0, 2), xc.transpose(1, 0, 2)))
            y = ys.transpose(1, 0, 2) + xc * Dp
            y = y * jax.nn.silu(z)
            return y @ out_w.T

        def forward(x, ln_w, ln_b, skip_scale, proj_w, proj_b, in_w, conv_w, conv_b, xproj_w, dt_w, dt_b, A_log, Dp, out_w, fc1_w, fc1_b, fc2_w, fc2_b):
            B, C, H, W = x.shape
            L = H * W
            dm = C // 4
            xf = x.reshape(B, C, L).transpose(0, 2, 1)
            xn = layer_norm(xf, ln_w, ln_b)
            chunks = xn.reshape(B, L, 4, dm).transpose(2, 0, 1, 3).reshape(4 * B, L, dm)
            ym = mamba_fwd(chunks, in_w, conv_w, conv_b, xproj_w, dt_w, dt_b, A_log, Dp, out_w)
            ym = ym + skip_scale * chunks
            ym = ym.reshape(4, B, L, dm).transpose(1, 2, 0, 3).reshape(B, L, C)
            ym = layer_norm(ym, ln_w, ln_b)
            ym = ym @ proj_w.T + proj_b
            tm = ym.transpose(0, 2, 1).reshape(B, C, H, W)
            out = x + tm
            h = jnp.einsum('bchw,oc->bohw', out, fc1_w) + fc1_b[None, :, None, None]
            h = jax.nn.gelu(h, approximate=False)
            m = jnp.einsum('bchw,oc->bohw', h, fc2_w) + fc2_b[None, :, None, None]
            return out + m + x
        return forward(x, ln_w, ln_b, skip_scale, proj_w, proj_b, in_w, conv_w, conv_b, xproj_w, dt_w, dt_b, A_log, Dp, out_w, fc1_w, fc1_b, fc2_w, fc2_b)

    def _gn(v, G=32, eps=1e-05):
        B_, C_, H_, W_ = v.shape
        g = v.reshape(B_, G, C_ // G, H_, W_)
        m = jnp.mean(g, axis=(2, 3, 4), keepdims=True)
        s = jnp.var(g, axis=(2, 3, 4), keepdims=True)
        return ((g - m) / jnp.sqrt(s + eps)).reshape(v.shape)

    def _ln_c(v, eps=1e-06):
        m = jnp.mean(v, axis=1, keepdims=True)
        s = jnp.var(v, axis=1, keepdims=True)
        return (v - m) / jnp.sqrt(s + eps)

    def _ln_t(v, eps=1e-05):
        m = jnp.mean(v, axis=-1, keepdims=True)
        s = jnp.var(v, axis=-1, keepdims=True)
        return (v - m) / jnp.sqrt(s + eps)

    def _to_tokens(v):
        B_, C_, H_, W_ = v.shape
        return v.reshape(B_, C_, H_ * W_).transpose(0, 2, 1)

    def _from_tokens(t, like):
        B_, C_, H_, W_ = like.shape
        return t.transpose(0, 2, 1).reshape(B_, C_, H_, W_)
    x = _L0_conv_ref(x, L0_conv_ln1_scale, L0_conv_ln1_bias, L0_conv_w_qkv, L0_conv_b_qkv, L0_conv_w_proj, L0_conv_b_proj, L0_conv_rel_bias_table, L0_conv_ln2_scale, L0_conv_ln2_bias, L0_conv_w_mlp1, L0_conv_b_mlp1, L0_conv_w_mlp2, L0_conv_b_mlp2)
    x = _L1_conv_ref(x, L1_conv_bias, L1_conv_up_filter, L1_conv_down_filter)
    x = _L2_conv_ref(x, L2_conv_W_in, L2_conv_W_x, L2_conv_W_dt, L2_conv_b_dt, L2_conv_A_logs, L2_conv_Ds, L2_conv_W_out, L2_conv_gn_w, L2_conv_gn_b)
    x = _L3_conv_ref(x, L3_conv_ln_w, L3_conv_ln_b, L3_conv_skip_scale, L3_conv_proj_w, L3_conv_proj_b, L3_conv_in_w, L3_conv_conv_w, L3_conv_conv_b, L3_conv_xproj_w, L3_conv_dt_w, L3_conv_dt_b, L3_conv_A_log, L3_conv_Dp, L3_conv_out_w, L3_conv_fc1_w, L3_conv_fc1_b, L3_conv_fc2_w, L3_conv_fc2_b)
    return x

_drawn_inputs = setup_inputs


def setup_inputs(seed=0):
    import zlib

    import numpy as np

    out = dict(_drawn_inputs(seed))
    spreads = {'L0_conv_ln1_scale': (1.0, 0.6),
     'L0_conv_ln1_bias': (0.0, 0.743),
     'L0_conv_b_qkv': (0.0, 0.1),
     'L0_conv_b_proj': (0.0, 0.1),
     'L0_conv_ln2_scale': (1.0, 0.6),
     'L0_conv_ln2_bias': (0.0, 0.8),
     'L0_conv_b_mlp1': (0.0, 0.1),
     'L0_conv_b_mlp2': (0.0, 0.1),
     'L2_conv_Ds': (1.0, 0.2),
     'L2_conv_gn_w': (1.0, 0.2),
     'L2_conv_gn_b': (0.0, 0.1),
     'L3_conv_ln_w': (1.0, 0.2),
     'L3_conv_ln_b': (0.0, 0.1),
     'L3_conv_proj_b': (0.0, 0.1),
     'L3_conv_conv_b': (0.0, 0.8),
     'L3_conv_dt_b': (-4.599999904632568, 0.6),
     'L3_conv_Dp': (1.0, 0.6),
     'L3_conv_fc1_b': (0.0, 0.277),
     'L3_conv_fc2_b': (0.0, 0.1)}
    factors = {'L0_conv_w_qkv': 4.274,
     'L0_conv_rel_bias_table': 64.0,
     'L2_conv_W_x': 8.0,
     'L2_conv_W_dt': 8.0,
     'L2_conv_b_dt': 8.0,
     'L2_conv_A_logs': 8.0,
     'L3_conv_in_w': 8.0,
     'L3_conv_conv_w': 8.0,
     'L3_conv_xproj_w': 64.0,
     'L3_conv_A_log': 64.0,
     'L3_conv_out_w': 8.0,
     'L3_conv_fc1_w': 4.14,
     'L3_conv_dt_w': 8.0}
    for name, (base, spread) in spreads.items():
        noise = np.random.default_rng([zlib.crc32(name.encode()), seed]).standard_normal(out[name].shape)
        drawn = base * np.exp(spread * noise) if base else spread * noise
        out[name] = jnp.asarray(drawn.astype(out[name].dtype))
    for name, factor in factors.items():
        out[name] = (out[name] * factor).astype(out[name].dtype)
    return out
```

```python
from contextlib import ExitStack

import numpy as np

import concourse.bass as bass
from concourse import mybir

F32 = mybir.dt.float32
F32R = mybir.dt.float32r
ALU = mybir.AluOpType
ACT = mybir.ActivationFunctionType
AX = mybir.AxisListType
ds = bass.ds

B, C, H, W = 8, 64, 32, 32
P = 128
HALVES = P // C
BL = B // HALVES
HW = H * W
COLS = BL * HW
N = 512
CHUNKS = COLS // N
WS = 8
HEADS = 8
HD = C // HEADS
WIN = WS * WS
PAIRS = COLS // WIN
ROWCOLS = WS * W
WROW = W // WS
HPAIRS = HEADS // 2
REL = 2 * WS - 1
LN_EPS = 1e-5
TAPS = 12
UPW = 74
PITCH = 80
RB = 4
TILES = H // RB
KM = 12
BLK = 2 * RB * PITCH // P
UPB = BLK * (TILES - 1) + KM
GAIN = float(np.sqrt(2.0))
SLOPE = 0.2
CLAMP = 256.0
NS = 16
D8 = P // NS
TOK = 8
GCN = C // TOK
DIN = 2 * GCN
SLOT = TOK + 1
N2 = 256
DM = C // 4
DI = 2 * DM
Q4 = 4
AMAX = 88.0


def wait(eng, sem, value):
    if isinstance(value, int) and value <= 0:
        return
    eng.wait_ge(sem, value)


def live(p, n):
    return not isinstance(p, int) or 0 <= p < n


def skewed(eng, n, unroll, peel, body):
    for s in range(peel):
        body(s, s % unroll)
    with eng.Fori(0, (n - peel) // unroll) as r:
        for u in range(unroll):
            body(r * unroll + (peel + u), u)
    for s in range(n, n + peel):
        body(s, s % unroll)


def layout(groups):
    at, out = 0, {}
    for name, width in groups:
        out[name] = (at, at + width)
        at += width
    return out, at


CONST = {
    "ln": [("center", P), ("mean", P), ("ln1_scale", 1), ("ln1_bias", 1), ("ln2_scale", 1), ("ln2_bias", 1),
           ("lnw", 1), ("lnb", 1)],
    "attn": [("wq", P), ("wk", P), ("wv", P), ("wp", P), ("ident", P), ("kmask", HEADS), ("vmask", 2 * 32),
             ("bq", 1), ("bk", 1), ("bv", 1), ("bp", 1)],
    "mlp0": [("w1", 4 * P), ("w2", 4 * P), ("b1", 2), ("b2", 1), ("l1b", 1)],
    "fir": [("ident", P)],
    "scan": [("sel", 16 * P), ("seln", 8 * P), ("ysel", 4 * 32)],
    "l2": [("wxp", 2 * P), ("wdt", P), ("wx0", 1), ("wb", P), ("wc", P), ("bdt", 1), ("alog", 2), ("dsk", 1)],
    "l2post": [("wz", 2 * P), ("wo", 2 * P), ("gavg", P), ("gnw", 1), ("gnb", 1)],
    "l3conv": [("wxi", 2 * P), ("convw", 4 * P), ("convb", 1)],
    "l3": [("xpr", P), ("dtw", P), ("wbc", P), ("dtb", 1),
           ("alog", 4), ("dp", 1)],
    "l3post": [("wz", 2 * P), ("wo", 2 * P), ("skip", 1), ("wpj", P), ("pjb", 1)],
    "mlp3": [("w1", 4 * P), ("w2", 4 * P), ("b1", 2), ("b2", 1), ("l1b", 1)],
}


def blocks(n, m):
    r, c = m.shape
    out = np.zeros((n, r, n, c), np.float32)
    for i in range(n):
        out[i, :, i, :] = m
    return out.reshape(n * r, n * c)


def halves(m, rows):
    out = np.zeros((HALVES, P, P), np.float32)
    for h in range(HALVES):
        if rows:
            out[h, h * C:(h + 1) * C, :] = m
        else:
            out[h, :, h * C:(h + 1) * C] = m
    return out.transpose(1, 0, 2).reshape(P, HALVES * P)


def mlp_pack(w1, b1, w2, b2, l1b):
    a = np.zeros((P, 2, 2, P), np.float32)
    z = np.zeros((P, 2, 2, P), np.float32)
    for h in range(2):
        for k in range(2):
            a[h * C:(h + 1) * C, h, k] = w1[:, k * P:(k + 1) * P]
            z[:, h, k, h * C:(h + 1) * C] = w2[k * P:(k + 1) * P]
    return {"w1": a.reshape(P, -1), "w2": z.reshape(P, -1), "b1": b1.reshape(2, P).T,
            "b2": np.tile(b2, 2)[:, None], "l1b": np.tile(l1b, 2)[:, None]}


def pack(i):
    def two(v):
        return np.tile(np.asarray(v), 2)[:, None]

    def rep(v, n):
        return np.tile(np.asarray(v), n)[:, None]

    eye = np.eye(P, dtype=np.float32)
    wqkv, bqkv = i["L0_conv_w_qkv"], i["L0_conv_b_qkv"]
    part = np.arange(P)
    kmask = ((part % C)[:, None] // HD == np.arange(HEADS)).astype(np.float32)
    c32 = np.arange(32)
    vmask = (c32[None, None, :] // HD == 2 * np.arange(2)[None, :, None] + (part // C)[:, None, None])
    v = {}
    v["ln"] = {"center": eye - blocks(2, np.full((C, C), 1.0 / C, np.float32)),
               "mean": blocks(2, np.full((C, C), 1.0 / C, np.float32)),
               "ln1_scale": two(i["L0_conv_ln1_scale"]), "ln1_bias": two(i["L0_conv_ln1_bias"]),
               "ln2_scale": two(i["L0_conv_ln2_scale"]), "ln2_bias": two(i["L0_conv_ln2_bias"]),
               "lnw": two(i["L3_conv_ln_w"]), "lnb": two(i["L3_conv_ln_b"])}
    v["attn"] = {"wq": blocks(2, wqkv[:, :C]), "wk": blocks(2, wqkv[:, C:2 * C]), "wv": blocks(2, wqkv[:, 2 * C:]),
                 "wp": blocks(2, i["L0_conv_w_proj"]), "ident": eye, "kmask": kmask,
                 "vmask": vmask.astype(np.float32).reshape(P, -1), "bq": two(bqkv[:C]), "bk": two(bqkv[C:2 * C]),
                 "bv": two(bqkv[2 * C:]), "bp": two(i["L0_conv_b_proj"])}
    v["mlp0"] = mlp_pack(i["L0_conv_w_mlp1"], i["L0_conv_b_mlp1"], i["L0_conv_w_mlp2"], i["L0_conv_b_mlp2"],
                         i["L1_conv_bias"])
    v["fir"] = {"ident": eye}
    d8n = np.arange(P)
    sel = np.zeros((P, 16, P), np.float32)
    seln = np.zeros((P, 8, P), np.float32)
    ysel = np.zeros((P, 4, 32), np.float32)
    for k in range(16):
        sel[8 * k + d8n // NS, k, d8n] = 1.0
    for t in range(8):
        seln[NS * t + d8n % NS, t, d8n] = 1.0
    for j in range(4):
        ysel[d8n, j, 8 * j + d8n // NS] = 1.0
    v["scan"] = {"sel": sel.reshape(P, -1), "seln": seln.reshape(P, -1), "ysel": ysel.reshape(P, -1)}
    wi, wx, wdt = i["L2_conv_W_in"], i["L2_conv_W_x"], i["L2_conv_W_dt"]
    v["l2"] = {"wxp": halves(blocks(TOK, wi[:, :DIN]), True),
               "wdt": blocks(TOK, np.repeat(wdt, DIN, axis=0)), "wx0": rep(wx[:, 0], TOK),
               "wb": blocks(TOK, wx[:, 1:1 + NS]), "wc": blocks(TOK, wx[:, 1 + NS:]),
               "bdt": rep(i["L2_conv_b_dt"], TOK), "alog": i["L2_conv_A_logs"].reshape(2, P).T,
               "dsk": rep(i["L2_conv_Ds"], TOK)}
    v["l2post"] = {"wz": halves(blocks(TOK, wi[:, DIN:]), True), "wo": halves(blocks(TOK, i["L2_conv_W_out"]), False),
                   "gavg": blocks(8, np.full((16, 16), 1.0 / 16, np.float32)),
                   "gnw": two(i["L2_conv_gn_w"]), "gnb": two(i["L2_conv_gn_b"])}
    inw, xp, cw = i["L3_conv_in_w"], i["L3_conv_xproj_w"], i["L3_conv_conv_w"]
    xpr = np.zeros((P, P), np.float32)
    dtw = np.zeros((P, P), np.float32)
    xpr[:16] = blocks(Q4, xp[:4])
    dtw[:16] = blocks(Q4, i["L3_conv_dt_w"].T)
    v["l3conv"] = {"wxi": halves(blocks(Q4, inw[:DI].T), True),
               "convw": np.broadcast_to(np.tile(cw[:, 0].T[:, None, :], (1, Q4, 1)).reshape(1, -1), (P, 4 * P)),
                   "convb": rep(i["L3_conv_conv_b"], Q4)}
    v["l3"] = {"xpr": xpr, "dtw": dtw, "wbc": blocks(Q4, xp[4:].T),
               "dtb": rep(i["L3_conv_dt_b"], Q4), "alog": i["L3_conv_A_log"].reshape(4, P).T,
               "dp": rep(i["L3_conv_Dp"], Q4)}
    v["l3post"] = {"wz": halves(blocks(Q4, inw[DI:].T), True), "wo": halves(blocks(Q4, i["L3_conv_out_w"].T), False),
                   "skip": np.broadcast_to(i["L3_conv_skip_scale"], (P,))[:, None],
                   "wpj": blocks(2, i["L3_conv_proj_w"].T), "pjb": two(i["L3_conv_proj_b"])}
    v["mlp3"] = mlp_pack(i["L3_conv_fc1_w"].T, i["L3_conv_fc1_b"], i["L3_conv_fc2_w"].T, i["L3_conv_fc2_b"],
                         np.zeros(C, np.float32))
    out = {}
    for group, names in CONST.items():
        at, width = layout(names)
        a = np.zeros((P, width), np.float32)
        for name, (lo, hi) in at.items():
            a[:, lo:hi] = v[group][name]
        out["pack_" + group] = a
    for name, f in (("up", i["L1_conv_up_filter"][::-1, ::-1]), ("down", i["L1_conv_down_filter"])):
        band = np.zeros((RB, W, KM * P // PITCH + 1, PITCH), np.float32)
        for r in range(RB):
            for ix in range(W):
                band[r, ix, 2 * r:2 * r + TAPS, 2 * ix:2 * ix + TAPS] = f
        band = band.reshape(P, -1)[:, :KM * P]
        if name == "down":
            band = band.reshape(P, KM, P).transpose(2, 1, 0).reshape(P, -1)
        out["fir_" + name] = band
    return out


class Scope:

    def __init__(self, nc, ctx):
        self.nc, self.ctx = nc, ctx

    def sb(self, name, shape, dt=F32):
        return self.ctx.enter_context(self.nc.sbuf_tensor(name, shape, dt))

    def banks(self, name, n, shape=(P, N), dt=F32):
        return [self.ctx.enter_context(self.nc.psum_tensor(f"{name}{k}", list(shape), dt)) for k in range(n)]

    def sem(self, name):
        return self.nc.alloc_semaphore(name=name)

    def consts(self, group, tag):
        at, width = layout(CONST[group])
        t = self.sb(f"{tag}_{group}", [P, width])
        return t, {name: t[:, lo:hi] for name, (lo, hi) in at.items()}


def layernorm(nc, dram, tag, src, dst, scale_name, bias_name):
    with ExitStack() as ctx:
        m = Scope(nc, ctx)
        consts, c = m.consts("ln", tag)
        center, square, normed = m.banks(tag + "cen", 2), m.sb(tag + "sq", [P, 2, N]), m.sb(tag + "nrm", [P, 2, N])
        var, rstd, lnv = m.banks(tag + "var", 2), m.sb(tag + "rstd", [P, 2, N]), m.sb(tag + "lnv", [P, 2, N])
        const_in, centered, squared, var_done, logged, rstd_done, norm_done, out_done = (
            m.sem(tag + x) for x in ("const", "centered", "squared", "var", "logged", "rstd", "norm", "out"))
        block = ctx.enter_context(nc.Block())

        @block.sync
        def _(sp):
            sp.dma_start(consts[:], dram["pack_ln"]).then_inc(const_in, 16)

        @block.tensor
        def _(pe):
            pe.wait_ge(const_in, 16)
            for n in range(CHUNKS + 1):
                if n < CHUNKS:
                    wait(pe, norm_done, n - 1)
                    pe.matmul(center[n % 2][:], c["center"], src[:, n * N:(n + 1) * N], start=True,
                              stop=True).then_inc(centered, 1)
                if n >= 1:
                    k = n - 1
                    pe.wait_ge(squared, k + 1)
                    wait(pe, logged, k - 1)
                    pe.matmul(var[k % 2][:], c["mean"], square[:, k % 2], start=True, stop=True).then_inc(var_done, 1)

        @block.scalar
        def _(act):
            act.preload_act_table_set("natural_log_exp_and_others")
            for n in range(CHUNKS + 1):
                if n < CHUNKS:
                    act.wait_ge(centered, n + 1)
                    wait(act, var_done, n - 1)
                    act.activation(square[:, n % 2], center[n % 2][:], ACT.Square).then_inc(squared, 1)
                if n >= 1:
                    k = n - 1
                    act.wait_ge(var_done, k + 1)
                    act.activation(lnv[:, k % 2], var[k % 2][:], ACT.Ln, bias=LN_EPS).then_inc(logged, 1)
                    act.wait_ge(logged, k + 1)
                    wait(act, norm_done, k - 1)
                    act.activation(rstd[:, k % 2], lnv[:, k % 2], ACT.Exp, scale=-0.5).then_inc(rstd_done, 1)

        @block.vector
        def _(dve):
            for n in range(CHUNKS):
                dve.wait_ge(rstd_done, n + 1)
                dve.wait_ge(squared, n + 1)
                dve.tensor_tensor(normed[:, n % 2], center[n % 2][:], rstd[:, n % 2], ALU.mult).then_inc(norm_done, 1)
                dve.wait_ge(norm_done, n + 1)
                dve.tensor_scalar(dst[:, n * N:(n + 1) * N], normed[:, n % 2], c[scale_name], c[bias_name],
                                  ALU.mult, ALU.add).then_inc(out_done, 1)


def mlp(nc, dram, tag, group, src, resid, dst, out=None):
    with ExitStack() as ctx:
        m = Scope(nc, ctx)
        consts, c = m.consts(group, tag)
        hidden, act_out, total = m.banks(tag + "hid", 4), m.sb(tag + "gelu", [P, 2, 4, N]), m.banks(tag + "tot", 2)
        bias = m.sb(tag + "bias", [P, 1])
        const_in, hid_done, gelu_done, tot_done, bias_done, res_done, stored = (
            m.sem(tag + x) for x in ("const", "hid", "gelu", "tot", "bias", "res", "stored"))
        w1 = c["w1"].rearrange("p (k n) -> p k n", n=P)
        w2 = c["w2"].rearrange("p (k n) -> p k n", n=P)
        block = ctx.enter_context(nc.Block())

        @block.sync
        def _(sp):
            sp.dma_start(consts[:], dram["pack_" + group]).then_inc(const_in, 16)
            if out is not None:
                for n in range(CHUNKS):
                    sp.wait_ge(res_done, n + 1)
                    bl, at = n * N // HW, n * N % HW
                    for h in range(HALVES):
                        sp.dma_start(out[h * BL + bl, :, at:at + N],
                                     dst[h * C:(h + 1) * C, n * N:(n + 1) * N]).then_inc(stored, 16)
                sp.wait_ge(stored, 16 * HALVES * CHUNKS)

        @block.tensor
        def _(pe):
            pe.wait_ge(const_in, 16)
            for n in range(CHUNKS + 1):
                if n < CHUNKS:
                    for k in range(4):
                        wait(pe, gelu_done, 4 * (n - 1) + k + 1)
                        pe.matmul(hidden[k][:], w1[:, k], src[:, n * N:(n + 1) * N], start=True,
                                  stop=True).then_inc(hid_done, 1)
                if n >= 1:
                    j = n - 1
                    wait(pe, res_done, j - 1)
                    for k in range(4):
                        pe.wait_ge(gelu_done, 4 * j + k + 1)
                        mm = pe.matmul(total[j % 2][:], w2[:, k], act_out[:, j % 2, k], start=(k == 0), stop=(k == 3))
                    mm.then_inc(tot_done, 1)

        @block.scalar
        def _(act):
            act.wait_ge(const_in, 16)
            for n in range(CHUNKS):
                wait(act, tot_done, n - 1)
                for k in range(4):
                    act.wait_ge(hid_done, 4 * n + k + 1)
                    act.activation(act_out[:, n % 2, k], hidden[k][:], ACT.Gelu,
                                   bias=c["b1"][:, k % 2:k % 2 + 1]).then_inc(gelu_done, 1)

        @block.vector
        def _(dve):
            dve.wait_ge(const_in, 16)
            dve.tensor_tensor(bias[:], c["b2"], c["l1b"], ALU.add).then_inc(bias_done, 1)
            dve.wait_ge(bias_done, 1)
            for n in range(CHUNKS):
                dve.wait_ge(tot_done, n + 1)
                cols = slice(n * N, (n + 1) * N)
                dve.scalar_tensor_tensor(out=dst[:, cols], in0=total[n % 2][:], scalar=bias[:, 0:1],
                                         in1=resid[:, cols], op0=ALU.add, op1=ALU.add).then_inc(res_done, 1)


def attention(nc, dram, xn, x):
    with ExitStack() as ctx:
        m = Scope(nc, ctx)
        consts, c = m.consts("attn", "a")
        rel = m.sb("relrow", [P, WIN, HEADS])
        bias = m.sb("relbias", [P, HEADS, WIN])
        win = m.sb("win", [P, 2, WROW, 2, WIN])
        qs, ks = m.sb("qs", [P, 2, ROWCOLS]), m.sb("ks", [P, 2, ROWCOLS])
        keys = m.sb("keys", [P, 2, HEADS, WIN])
        vals = m.sb("vals", [P, 2, WROW * HALVES, HPAIRS, 32])
        logit, prob, pnorm = (m.sb(x, [P, 2, HEADS, WIN]) for x in ("logit", "prob", "pnorm"))
        top, total, inv = (m.sb(x, [P, 2, HEADS]) for x in ("top", "total", "inv"))
        probt = m.sb("probt", [P, 2, HPAIRS, P])
        mixed = m.sb("mixed", [P, 2, ROWCOLS])
        ps_qk, ps_v, ps_o, ps_y = (m.banks(x, 1)[0] for x in ("psqk", "psv", "pso", "psy"))
        ps_s, ps_t = m.banks("pss", 2), m.banks("pst", 2)
        const_in, rel_in, bias_done = (m.sem("a_" + x) for x in ("const", "rel", "bias"))
        win_done, qk_done, v_done, q_out, k_out, v_out, y_done, x_done, mix_done = (
            m.sem("a_" + x) for x in ("win", "qk", "v", "qout", "kout", "vout", "y", "x", "mix"))
        keys_done, s_done, added, top_done, shifted, exp_done, sum_done, inv_done, norm_done, t_done, t_out, o_done = (
            m.sem("a_" + x) for x in ("keys", "s", "added", "top", "shifted", "exp", "sum", "inv", "norm", "t",
                                      "tout", "o"))
        R = WROW
        LAG_V, LAG_K, LAG_S, LAG_E, LAG_T, LAG_TO, LAG_O, LAG_Y = 3, 3, 4, 5, 6, 6, 7, 8
        UN, PEEL = 8, 16
        block = ctx.enter_context(nc.Block())

        def image(t, base):
            return t[:, ds(base, ROWCOLS)].rearrange("p (y w x) -> p w y x", y=WS, w=R)

        @block.sync
        def _(sp):
            sp.dma_start(consts[:], dram["pack_attn"]).then_inc(const_in, 16)
            for half in range(HALVES):
                for ny in range(WS):
                    at = half * WIN + ny * WS
                    src = dram["rel"][0:1, 0:1]
                    src = bass.AP(src.tensor, ny * REL * HEADS, [[HEADS, WS], [REL * HEADS, WS], [1, WS * HEADS]])
                    sp.dma_start(rel[at:at + WS].rearrange("p (a b) h -> p a (b h)", a=WS), src).then_inc(rel_in, 16)

        @block.scalar
        def _(act):
            act.preload_act_table_set("natural_log_exp_and_others")
            act.wait_ge(const_in, 16)

            def body(s, u):
                if u % R == 0 and live(s, PAIRS):
                    par = u // R
                    wait(act, v_done, s - R)
                    wait(act, qk_done, s - R)
                    for twice in range(2):
                        act.activation(win[:, par, :, twice].rearrange("p w (y x) -> p w y x", y=WS),
                                       image(xn, s * WIN), ACT.Copy).then_inc(win_done, R // 2)
                p = s - LAG_E
                if live(p, PAIRS):
                    b = (u - LAG_E) % 2
                    act.wait_ge(shifted, p + 1)
                    wait(act, norm_done, p - 1)
                    wait(act, sum_done, p - 1)
                    act.activation(prob[:, b], logit[:, b], ACT.Exp).then_inc(exp_done, 1)
                p = s - LAG_TO
                if live(p, PAIRS):
                    b = (u - LAG_TO) % 2
                    act.wait_ge(t_done, p + 1)
                    wait(act, o_done, p - 1)
                    act.activation(probt[:, b].rearrange("p a b -> p (a b)"), ps_t[b][:], ACT.Copy).then_inc(t_out, 1)
                p = s - LAG_Y
                if (u - LAG_Y) % R == R - 1 and live(p, PAIRS):
                    par = (u - LAG_Y) % UN // R
                    act.wait_ge(o_done, p + 1)
                    wait(act, y_done, p + 1 - 2 * R)
                    act.activation(mixed[:, par], ps_o[:, 0:ROWCOLS], ACT.Identity,
                                   bias=c["bv"]).then_inc(mix_done, R)

            skewed(act, PAIRS, UN, PEEL, body)

        @block.tensor
        def _(pe):
            pe.wait_ge(const_in, 16)

            def body(s, u):
                if u % R == 0 and live(s, PAIRS):
                    par = u // R
                    pe.wait_ge(win_done, s + R)
                    wait(pe, q_out, s)
                    wait(pe, k_out, s)
                    once = win[:, par, :, 0]
                    pe.matmul(ps_qk[:, 0:ROWCOLS], c["wq"], once, start=True, stop=True)
                    pe.matmul(ps_qk[:, ROWCOLS:2 * ROWCOLS], c["wk"], once, start=True, stop=True).then_inc(qk_done, R)
                p = s - LAG_V
                if u % R == LAG_V and live(p, PAIRS):
                    par = u // R
                    wait(pe, v_out, p)
                    for w in range(R):
                        mm = pe.matmul(ps_v[:, w * P:(w + 1) * P], win[:, par, w].rearrange("p a b -> p (a b)"), c["wv"], start=True, stop=True)
                    mm.then_inc(v_done, R)
                p = s - LAG_S
                if live(p, PAIRS):
                    b, w, par = (u - LAG_S) % 2, (u - LAG_S) % R, (u - LAG_S) % UN // R
                    pe.wait_ge(keys_done, p + 1)
                    pe.wait_ge(q_out, p - w + R)
                    wait(pe, added, p - 1)
                    pe.matmul(ps_s[b][:, 0:1], c["ident"], c["kmask"][:, 0:1], start=True, stop=True)
                    for h in range(HALVES):
                        r = slice(h * C, (h + 1) * C)
                        mm = pe.matmul(ps_s[b][r, :], qs[r, par, w * WIN:(w + 1) * WIN],
                                       keys[r, b].rearrange("p a b -> p (a b)"), start=True, stop=True)
                    mm.then_inc(s_done, 1)
                p = s - LAG_T
                if live(p, PAIRS):
                    b = (u - LAG_T) % 2
                    pe.wait_ge(norm_done, p + 1)
                    wait(pe, t_out, p - 1)
                    for k in range(HPAIRS):
                        mm = pe.transpose(ps_t[b][:, k * P:(k + 1) * P],
                                          pnorm[:, b, 2 * k:2 * k + 2].rearrange("p a b -> p (a b)"), c["ident"])
                    mm.then_inc(t_done, 1)
                p = s - LAG_O
                if live(p, PAIRS):
                    b, w, par = (u - LAG_O) % 2, (u - LAG_O) % R, (u - LAG_O) % UN // R
                    pe.wait_ge(t_out, p + 1)
                    pe.wait_ge(v_out, p - w + R)
                    if w == 0:
                        wait(pe, mix_done, p)
                    for first in (0, 1):
                        for h in range(HALVES):
                            for k2 in range(2):
                                quad = 2 * h + k2
                                k = 2 * k2 + first
                                mm = pe.matmul(ps_o[quad * 32:(quad + 1) * 32, w * WIN:(w + 1) * WIN],
                                               vals[:, par, w * HALVES + h, k], probt[:, b, k, h * WIN:(h + 1) * WIN],
                                               start=(first == 0), stop=(first == 1), tile_position=(0, quad * 32))
                    mm.then_inc(o_done, 1)
                p = s - LAG_Y
                if (u - LAG_Y) % R == R - 1 and live(p, PAIRS):
                    par = (u - LAG_Y) % UN // R
                    pe.wait_ge(mix_done, p + 1)
                    wait(pe, x_done, p + 1 - R)
                    pe.matmul(ps_y[:, 0:ROWCOLS], c["wp"],
                              mixed[:, par].rearrange("p (w y x) -> p y w x", w=R, y=WS),
                              start=True, stop=True).then_inc(y_done, R)

            skewed(pe, PAIRS, UN, PEEL, body)

        @block.vector
        def _(dve):
            dve.wait_ge(const_in, 16)
            dve.wait_ge(rel_in, 16 * HALVES * WS)
            dve.tensor_copy(bias[:], rel[:, ::-1, :].rearrange("p j h -> p h j")).then_inc(bias_done, 1)
            dve.wait_ge(bias_done, 1)

            def body(s, u):
                if u % R == 0 and live(s, PAIRS):
                    par = u // R
                    dve.wait_ge(qk_done, s + R)
                    wait(dve, s_done, s - R)
                    dve.tensor_scalar(qs[:, par], ps_qk[:, 0:ROWCOLS], c["bq"], float(HD) ** -0.5, ALU.add,
                                      ALU.mult).then_inc(q_out, R)
                    wait(dve, keys_done, s - R)
                    dve.tensor_scalar(ks[:, par], ps_qk[:, ROWCOLS:2 * ROWCOLS], c["bk"], None,
                                      ALU.add).then_inc(k_out, R)
                p = s - LAG_V
                if u % R == LAG_V and live(p, PAIRS):
                    par = u // R
                    dve.wait_ge(v_done, p + R)
                    wait(dve, o_done, p - R)
                    v = ps_v[:].rearrange("p (a b) -> p a b", b=C)
                    mask = c["vmask"].rearrange("p (a b) -> p a b", a=2)
                    for k2 in range(2):
                        dve.tensor_tensor(vals[:, par, :, 2 * k2:2 * k2 + 2],
                                          v[:, :, None, 32 * k2:32 * k2 + 32].to_broadcast([P, R * HALVES, 2, 32]),
                                          mask[:, None].to_broadcast([P, R * HALVES, 2, 32]),
                                          ALU.mult).then_inc(v_out, R // 2)
                p = s - LAG_S
                if live(p, PAIRS):
                    b = (u - LAG_S) % 2
                    dve.wait_ge(s_done, p + 1)
                    wait(dve, exp_done, p - 1)
                    dve.tensor_tensor(logit[:, b].rearrange("p a b -> p (a b)"), ps_s[b][:],
                                      bias[:].rearrange("p a b -> p (a b)"), ALU.add).then_inc(added, 1)
                    dve.wait_ge(added, p + 1)
                    dve.tensor_reduce(top[:, b], logit[:, b], AX.X, ALU.max).then_inc(top_done, 1)
                    dve.wait_ge(top_done, p + 1)
                    dve.tensor_tensor(logit[:, b], logit[:, b], top[:, b, :, None].to_broadcast([P, HEADS, WIN]),
                                      ALU.subtract).then_inc(shifted, 1)
                p = s - LAG_E
                if live(p, PAIRS):
                    b = (u - LAG_E) % 2
                    dve.wait_ge(exp_done, p + 1)
                    dve.tensor_reduce(total[:, b], prob[:, b], AX.X, ALU.add).then_inc(sum_done, 1)
                    dve.wait_ge(sum_done, p + 1)
                    wait(dve, norm_done, p - 1)
                    dve.reciprocal(inv[:, b], total[:, b]).then_inc(inv_done, 1)
                p = s - LAG_Y
                if (u - LAG_Y) % R == R - 1 and live(p, PAIRS):
                    dve.wait_ge(y_done, p + 1)
                    cols = ds((p + 1 - R) * WIN, ROWCOLS)
                    dve.scalar_tensor_tensor(out=x[:, cols], in0=ps_y[:, 0:ROWCOLS], scalar=c["bp"], in1=x[:, cols],
                                             op0=ALU.add, op1=ALU.add).then_inc(x_done, R)

            skewed(dve, PAIRS, UN, PEEL, body)

        @block.gpsimd
        def _(pool):
            pool.wait_ge(const_in, 16)

            def body(s, u):
                p = s - LAG_K
                if live(p, PAIRS):
                    b, w, par = (u - LAG_K) % 2, (u - LAG_K) % R, (u - LAG_K) % UN // R
                    pool.wait_ge(k_out, p - w + R)
                    wait(pool, s_done, p - 1)
                    pool.tensor_tensor(keys[:, b],
                                       ks[:, par, None, w * WIN:(w + 1) * WIN].to_broadcast([P, HEADS, WIN]),
                                       c["kmask"][:, :, None].to_broadcast([P, HEADS, WIN]),
                                       ALU.mult).then_inc(keys_done, 1)
                p = s - LAG_E
                if live(p, PAIRS):
                    b = (u - LAG_E) % 2
                    pool.wait_ge(inv_done, p + 1)
                    wait(pool, t_done, p - 1)
                    pool.tensor_tensor(pnorm[:, b], prob[:, b], inv[:, b, :, None].to_broadcast([P, HEADS, WIN]),
                                       ALU.mult).then_inc(norm_done, 1)

            skewed(pool, PAIRS, UN, PEEL, body)


def antialiased(nc, dram, x):
    with ExitStack() as ctx:
        m = Scope(nc, ctx)
        consts, c = m.consts("fir", "f")
        upm = m.sb("upm", [P, KM * P])
        downt = m.sb("downt", [P, KM, P])
        pos = m.sb("pos", [P, TILES, N])
        lin, rect, act_y = (m.sb(t, [P, 2, N]) for t in ("lin", "rect", "acty"))
        tile_out = m.sb("tileout", [P, 2, N])
        ps_up, ps_down, ps_t = m.banks("psup", 3), m.banks("psdown", 3), m.banks("pstr", 2)
        const_in, band_in, tp_done, tp_out = (m.sem("f_" + t) for t in ("const", "band", "tp", "tpout"))
        up_done, lin_done, rect_done, act_done, acc_done, tile_done, back_done, x_done = (
            m.sem("f_" + t) for t in ("up", "lin", "rect", "act", "acc", "tile", "back", "x"))

        def sources(j):
            return [(t, j - BLK * t) for t in range(TILES) if 0 <= j - BLK * t < KM]

        block = ctx.enter_context(nc.Block())

        @block.sync
        def _(sp):
            sp.dma_start(consts[:], dram["pack_fir"]).then_inc(const_in, 16)
            sp.dma_start(upm[:], dram["fir_up"]).then_inc(band_in, 16)
            sp.dma_start(downt[:], dram["fir_down"].rearrange("p (k n) -> p k n", n=P)).then_inc(band_in, 16)

        @block.tensor
        def _(pe):
            pe.wait_ge(const_in, 16)
            for t in range(TILES):
                wait(pe, tp_out, t - 1)
                for bl in range(BL):
                    mm = pe.transpose(ps_t[t % 2][:, bl * P:(bl + 1) * P],
                                      x[:, bl * HW + t * P:bl * HW + (t + 1) * P], c["ident"])
                mm.then_inc(tp_done, 1)
            pe.wait_ge(band_in, 16 * 2)

            def up(j):
                pe.wait_ge(tp_out, sources(j)[-1][0] + 1)
                wait(pe, lin_done, j - 2)
                src = sources(j)
                for n, (t, k) in enumerate(src):
                    mm = pe.matmul(ps_up[j % 3][:], upm[:, k * P:(k + 1) * P], pos[:, t], start=(n == 0),
                                   stop=(n == len(src) - 1))
                mm.then_inc(up_done, 1)

            def down(j):
                pe.wait_ge(act_done, j + 1)
                for t, k in sources(j):
                    if k == 0:
                        wait(pe, tile_done, t - 2)
                    mm = pe.matmul(ps_down[t % 3][:], downt[:, k], act_y[:, j % 2], start=(k == 0), stop=(k == KM - 1))
                mm.then_inc(acc_done, 1)

            def back(t):
                pe.wait_ge(tile_done, t + 1)
                wait(pe, x_done, t - 1)
                pe.wait_ge(tp_out, TILES)
                for bl in range(BL):
                    mm = pe.transpose(ps_t[t % 2][:, bl * P:(bl + 1) * P], tile_out[:, t % 2, bl * P:(bl + 1) * P],
                                      c["ident"])
                mm.then_inc(back_done, 1)

            for j in range(UPB + 4):
                if j < UPB:
                    up(j)
                if 2 <= j < UPB + 2:
                    down(j - 2)
                t, rest = divmod(j - 3 - KM, BLK)
                if rest == 0 and 0 <= t < TILES:
                    back(t)

        @block.scalar
        def _(act):
            for t in range(TILES):
                act.wait_ge(tp_done, t + 1)
                act.activation(pos[:, t], ps_t[t % 2][:], ACT.Copy).then_inc(tp_out, 1)
            def finish(t):
                act.wait_ge(acc_done, BLK * t + KM)
                wait(act, back_done, t - 1)
                act.activation(tile_out[:, t % 2], ps_down[t % 3][:], ACT.Copy).then_inc(tile_done, 1)

            for j in range(UPB):
                act.wait_ge(up_done, j + 1)
                wait(act, rect_done, j - 1)
                act.activation(lin[:, j % 2], ps_up[j % 3][:], ACT.Copy, scale=GAIN).then_inc(lin_done, 1)
                t, rest = divmod(j - KM - 1, BLK)
                if rest == 0 and t >= 0:
                    finish(t)
            finish(TILES - 1)

        @block.vector
        def _(dve):
            def put(t):
                dve.wait_ge(back_done, t + 1)
                dve.tensor_copy(x.rearrange("p (b t n) -> p t b n", b=BL, n=P)[:, t],
                                ps_t[t % 2][:].rearrange("p (b n) -> p b n", b=BL)).then_inc(x_done, 1)

            for j in range(UPB):
                dve.wait_ge(lin_done, j + 1)
                dve.scalar_tensor_tensor(out=rect[:, j % 2], in0=lin[:, j % 2], scalar=SLOPE, in1=lin[:, j % 2],
                                         op0=ALU.mult, op1=ALU.max).then_inc(rect_done, 1)
                dve.wait_ge(rect_done, j + 1)
                wait(dve, acc_done, j - 1)
                dve.tensor_scalar(act_y[:, j % 2], rect[:, j % 2], CLAMP, -CLAMP, ALU.min,
                                  ALU.max).then_inc(act_done, 1)
                t, rest = divmod(j - KM - 5, BLK)
                if rest == 0 and t >= 0:
                    put(t)
            for t in range((UPB - 1 - KM - 5) // BLK + 1, TILES):
                put(t)


STEPS = 64
UNROLL, PEEL = 8, 8


def selectors(nc, dram, selr, ysel):
    with ExitStack() as ctx:
        m = Scope(nc, ctx)
        consts, c = m.consts("scan", "z")
        const_in, copied = m.sem("z_const"), m.sem("z_copied")
        block = ctx.enter_context(nc.Block())

        @block.sync
        def _(sp):
            sp.dma_start(consts[:], dram["pack_scan"]).then_inc(const_in, 16)

        @block.vector
        def _(dve):
            dve.wait_ge(const_in, 16)
            dve.tensor_copy(selr[:], consts[:, 0:24 * P]).then_inc(copied, 1)
            dve.tensor_copy(ysel[:], c["ysel"]).then_inc(copied, 1)


def prepare_a(m, tag, c, consts_in, blocks_of_a):
    low, grown, neg = (m.sb(tag + t, [P, blocks_of_a]) for t in ("alow", "agrown", "aneg"))
    low_done, grown_done, neg_done = (m.sem(tag + t) for t in ("alowd", "agrownd", "anegd"))

    def on_vector(dve):
        dve.tensor_scalar(low[:], c["alog"], AMAX, None, ALU.min).then_inc(low_done, 1)
        dve.wait_ge(grown_done, 1)
        dve.tensor_scalar(neg[:], grown[:], -1.0, None, ALU.mult).then_inc(neg_done, 1)

    def on_scalar(act):
        act.wait_ge(low_done, 1)
        act.activation(grown[:], low[:], ACT.Exp).then_inc(grown_done, 1)
        act.wait_ge(neg_done, 1)

    return neg, on_vector, on_scalar


def scan2(nc, dram, x, y, selr, ysel):
    with ExitStack() as ctx:
        m = Scope(nc, ctx)
        consts, c = m.consts("l2", "s")
        wdt, bdt2, dsk2 = m.sb("s_wdtb", [P, P]), m.sb("s_bdt2", [P, 1]), m.sb("s_dsk2", [P, 1])
        xp = m.sb("s_xp", [P, 2, N])
        delta, du, rest = m.sb("s_delta", [P, N]), m.sb("s_du", [P, N]), m.sb("s_rest", [P, N])
        away, relu, ex, one, ln, lost = (m.sb("s_" + t, [P, N]) for t in ("away", "relu", "ex", "one", "ln", "lost"))
        parts = m.sb("s_parts", [P, 2, 4, 2, N], F32R)
        decay, feed = m.sb("s_decay", [P, 2, N2, SLOT]), m.sb("s_feed", [P, N2, SLOT])
        ahead, back = m.sb("s_ahead", [P, 2, N2, SLOT]), m.sb("s_back", [P, 2, N2, SLOT])
        brep = m.sb("s_brep", [P, 2, 2, N2])
        prod = m.sb("s_prod", [P, 2, TOK, N2])
        ps_in, ps_dt, ps_y = (m.banks("s_p" + t, 1)[0] for t in ("in", "dt", "y"))
        ps_d, ps_r = m.banks("s_pd", 2), m.banks("s_pr", 3)
        const_in, ready, zeroed = (m.sem("s_" + t) for t in ("const", "ready", "zeroed"))
        xp_ps, xp_done, skip_done, dt_ps, b_ps, c_ps, away_done, relu_done, ex_done, one_done, ln_done, lost_done, \
            rest_done, delta_done, du_done = (m.sem("s_" + t) for t in (
                "xpps", "xpd", "skipd", "dtps", "bps", "cps", "awayd", "relud", "exd", "oned", "lnd", "lostd",
                "restd", "deltad", "dud"))
        hi_d, hi_u, hi_b, hi_c, lo_d, lo_u, lo_b, lo_c = (
            m.sem("s_" + t) for t in ("hid", "hiu", "hib", "hic", "lod", "lou", "lob", "loc"))
        d_ps, decayed, b_rep, b_copied, u_rep, fed, c_rep, multiplied, ahead_done, back_done, summed, y_part, y_done = (
            m.sem("s_" + t) for t in ("dps", "decayed", "brepd", "bcop", "urep", "fed", "crep", "mult", "aheadd",
                                      "backd", "summed", "ypart", "ydone"))
        aneg, a_on_vector, a_on_scalar = prepare_a(m, "s_", c, const_in, 2)
        LAG_A, LAG_C, LAG_Y = 4, 5, 6
        DT, DU, BB, CC = range(4)
        RING = [(BB, 0), (DU, 0), (BB, 1), (DU, 1), (BB, 2), (DU, 2), (BB, 3), (DU, 3)] + [(CC, t) for t in range(4)]
        READER = {BB: b_copied, DU: fed, CC: multiplied}
        LAG = {BB: LAG_A, DU: LAG_A, CC: LAG_C}
        block = ctx.enter_context(nc.Block())

        def place(u):
            u %= UNROLL
            return u // 4, slice(u % 4 // 2 * N2, (u % 4 // 2 + 1) * N2), u % 2

        @block.sync
        def _(sp):
            sp.dma_start(consts[:], dram["pack_l2"]).then_inc(const_in, 16)

        @block.tensor
        def _(pe):
            pe.wait_ge(ready, 3)

            def spread(bank, sel, which, par, cols):
                for i in range(2):
                    for part in range(2):
                        mm = pe.matmul(bank[:, i * N2:(i + 1) * N2], selr[:, sel[i] * P:(sel[i] + 1) * P],
                                       parts[:, par, which, part, cols], start=(part == 0), stop=(part == 1))
                return mm

            def ring_free(s, r):
                for k in range(r - 3, r - 25, -3):
                    kind, tp = RING[k % 12]
                    p = s + k // 12 - LAG[kind]
                    if live(p, STEPS):
                        pe.wait_ge(READER[kind], 4 * p + tp + 1)
                        return

            def body(s, u):
                par = u // 4
                if u % 4 == 0 and live(s, STEPS):
                    wait(pe, lo_b, s)
                    pe.matmul(ps_in[:], c["wxp"][:, par * P:(par + 1) * P], x[:, ds((s - u) * (N // UNROLL), N)],
                              start=True, stop=True).then_inc(xp_ps, 4)
                if u % 4 == 1 and live(s, STEPS):
                    pe.wait_ge(xp_done, s + 3)
                    pe.wait_ge(skip_done, s + 3)
                    wait(pe, lo_c, s - 1)
                    pe.matmul(ps_dt[:], wdt[:], xp[:, par], start=True, stop=True).then_inc(dt_ps, 4)
                    pe.matmul(ps_in[:], c["wb"], xp[:, par], start=True, stop=True).then_inc(b_ps, 4)
                if u % 4 == 2 and live(s, STEPS):
                    pe.wait_ge(relu_done, s + 2)
                    pe.matmul(ps_dt[:], c["wc"], xp[:, par], start=True, stop=True).then_inc(c_ps, 4)
                p = s - LAG_A
                if live(p, STEPS):
                    par, cols, g = place(u - LAG_A)
                    if (u - LAG_A) % 4 == 0:
                        for done in (lo_d, lo_u, lo_b):
                            pe.wait_ge(done, p + 4)
                    for tp in range(4):
                        wait(pe, decayed, 4 * p + tp - 1)
                        spread(ps_d[tp % 2], [2 * (2 * tp + i) + g for i in range(2)], DT, par, cols).then_inc(d_ps, 1)
                    for tp in range(4):
                        ring_free(s, 2 * tp)
                        spread(ps_r[2 * tp % 3], [16 + 2 * tp + i for i in range(2)], BB, par, cols).then_inc(b_rep, 1)
                        ring_free(s, 2 * tp + 1)
                        spread(ps_r[(2 * tp + 1) % 3], [2 * (2 * tp + i) + g for i in range(2)], DU, par,
                               cols).then_inc(u_rep, 1)
                p = s - LAG_C
                if live(p, STEPS):
                    par, cols, g = place(u - LAG_C)
                    if (u - LAG_C) % 4 == 0:
                        pe.wait_ge(lo_c, p + 4)
                    for tp in range(4):
                        ring_free(s, 8 + tp)
                        spread(ps_r[(8 + tp) % 3], [16 + 2 * tp + i for i in range(2)], CC, par, cols).then_inc(c_rep, 1)
                p = s - LAG_Y
                if live(p, STEPS):
                    _, cols, g = place(u - LAG_Y)
                    if (u - LAG_Y) % 4 == 0:
                        wait(pe, y_done, p)
                    pe.wait_ge(multiplied, 4 * p + 4)
                    for odd in range(2):
                        for quad in range(4):
                            mm = pe.matmul(ps_y[quad * 32:(quad + 1) * 32, cols],
                                           ysel[:, (2 * odd + g) * 32:(2 * odd + g + 1) * 32],
                                           prod[:, u % 2, 2 * quad + odd], start=(odd == 0 and g == 0),
                                           stop=(odd == 1 and g == 1), tile_position=(0, quad * 32))
                    mm.then_inc(y_part, 1)

            skewed(pe, STEPS, UNROLL, PEEL, body)

        @block.scalar
        def _(act):
            act.preload_act_table_set("natural_log_exp_and_others")
            a_on_scalar(act)
            act.wait_ge(ready, 3)
            act.wait_ge(zeroed, 3)

            def body(s, u):
                p = s - LAG_A
                if live(p, STEPS):
                    b, (_, _, g) = u % 2, place(u - LAG_A)
                    wait(act, back_done, p - 1)
                    wait(act, ahead_done, p - 1)
                    for tp in range(4):
                        act.wait_ge(d_ps, 4 * p + tp + 1)
                        act.activation(decay[:, b, :, 2 * tp:2 * tp + 2].rearrange("p n t -> p t n"),
                                       ps_d[tp % 2][:].rearrange("p (t n) -> p t n", t=2), ACT.Exp,
                                       scale=aneg[:, g:g + 1]).then_inc(decayed, 1)
                    for tp in range(4):
                        act.wait_ge(b_rep, 4 * p + tp + 1)
                        wait(act, fed, 4 * p + tp - 1)
                        act.activation(brep[:, tp % 2].rearrange("p t n -> p (t n)"), ps_r[2 * tp % 3][:],
                                       ACT.Copy).then_inc(b_copied, 1)
                if not live(s, STEPS):
                    return
                par, gi = u // 4, s - u % 4
                if u % 4 == 0:
                    act.wait_ge(xp_ps, gi + 4)
                    wait(act, c_ps, gi - 4)
                    wait(act, du_done, gi - 4)
                    act.activation(xp[:, par], ps_in[:], ACT.Copy).then_inc(xp_done, 4)
                    act.activation(y[:, par, ds((s - u) * (N // UNROLL), N)], ps_in[:], ACT.Copy,
                                   scale=dsk2[:, 0:1]).then_inc(skip_done, 4)
                if u % 4 == 1:
                    act.wait_ge(dt_ps, gi + 4)
                    act.activation(away[:], ps_dt[:], ACT.Abs, bias=bdt2[:, 0:1]).then_inc(away_done, 4)
                    wait(act, delta_done, gi)
                    act.activation(relu[:], ps_dt[:], ACT.Relu, bias=bdt2[:, 0:1]).then_inc(relu_done, 4)
                    act.wait_ge(away_done, gi + 4)
                    wait(act, lost_done, gi)
                    act.activation(ex[:], away[:], ACT.Exp, scale=-1.0).then_inc(ex_done, 4)
                    act.wait_ge(b_ps, gi + 4)
                    wait(act, b_rep, 4 * (gi - 4))
                    act.activation(parts[:, par, BB, 0], ps_in[:], ACT.Copy).then_inc(hi_b, 4)
                if u % 4 == 2:
                    act.wait_ge(one_done, gi + 4)
                    wait(act, rest_done, gi)
                    act.activation(ln[:], one[:], ACT.Ln).then_inc(ln_done, 4)
                    act.wait_ge(c_ps, gi + 4)
                    wait(act, c_rep, 4 * (gi - 4))
                    act.activation(parts[:, par, CC, 0], ps_dt[:], ACT.Copy).then_inc(hi_c, 4)
                if u % 4 == 3:
                    act.wait_ge(delta_done, gi + 4)
                    wait(act, d_ps, 4 * (gi - 4))
                    act.activation(parts[:, par, DT, 0], delta[:], ACT.Copy).then_inc(hi_d, 4)
                    act.wait_ge(du_done, gi + 4)
                    wait(act, u_rep, 4 * (gi - 4))
                    act.activation(parts[:, par, DU, 0], du[:], ACT.Copy).then_inc(hi_u, 4)

            skewed(act, STEPS, UNROLL, PEEL, body)

        @block.vector
        def _(dve):
            dve.wait_ge(const_in, 16)
            dve.tensor_scalar(wdt[:], c["wdt"], c["wx0"], None, ALU.mult).then_inc(ready, 1)
            dve.tensor_scalar(bdt2[:], c["bdt"], 2.0, None, ALU.mult).then_inc(ready, 1)
            dve.tensor_scalar(dsk2[:], c["dsk"], 2.0, None, ALU.mult).then_inc(ready, 1)
            a_on_vector(dve)
            dve.wait_ge(zeroed, 3)

            def body(s, u):
                p = s - LAG_A
                if live(p, STEPS):
                    b = u % 2
                    for tp in range(4):
                        dve.wait_ge(u_rep, 4 * p + tp + 1)
                        dve.wait_ge(b_copied, 4 * p + tp + 1)
                        wait(dve, back_done, p)
                        dve.tensor_tensor(feed[:, :, 2 * tp:2 * tp + 2].rearrange("p n t -> p t n"),
                                          ps_r[(2 * tp + 1) % 3][:].rearrange("p (t n) -> p t n", t=2),
                                          brep[:, tp % 2], ALU.mult).then_inc(fed, 1)
                    dve.wait_ge(decayed, 4 * p + 4)
                    dve.wait_ge(fed, 4 * p + 4)
                    a, f = (t.rearrange("p n t -> p (n t)") for t in (decay[:, b], feed[:]))
                    wait(dve, multiplied, 4 * (p - 1))
                    dve.tensor_tensor_scan(ahead[:, b].rearrange("p n t -> p (n t)"), a, f, 0.0, ALU.mult,
                                           ALU.add).then_inc(ahead_done, 1)
                    wait(dve, summed, p - 1)
                    dve.tensor_tensor_scan(back[:, b].rearrange("p n t -> p (n t)")[:, ::-1], a[:, ::-1], f[:, ::-1],
                                           0.0, ALU.mult, ALU.add).then_inc(back_done, 1)
                p = s - LAG_C
                if live(p, STEPS):
                    b = (u - LAG_C) % 2
                    dve.wait_ge(summed, p + 1)
                    wait(dve, y_part, p - 1)
                    for tp in range(4):
                        dve.wait_ge(c_rep, 4 * p + tp + 1)
                        dve.tensor_tensor(prod[:, b, 2 * tp:2 * tp + 2],
                                          ps_r[(8 + tp) % 3][:].rearrange("p (t n) -> p t n", t=2),
                                          ahead[:, b, :, 2 * tp:2 * tp + 2].rearrange("p n t -> p t n"),
                                          ALU.mult).then_inc(multiplied, 1)
                p = s - LAG_Y
                if (u - LAG_Y) % 4 == 3 and live(p, STEPS):
                    half = place(u - LAG_Y)[0]
                    dve.wait_ge(y_part, p + 1)
                    dve.wait_ge(skip_done, p + 1)
                    cols = ds((p - (u - LAG_Y) % UNROLL) * (N // UNROLL), N)
                    dve.tensor_tensor(y[:, half, cols], ps_y[:], y[:, half, cols], ALU.add).then_inc(y_done, 4)
                if not live(s, STEPS):
                    return
                par, gi = u // 4, s - u % 4
                if u % 4 == 1:
                    dve.wait_ge(ex_done, gi + 4)
                    wait(dve, ln_done, gi)
                    dve.tensor_scalar(one[:], ex[:], 1.0, None, ALU.add).then_inc(one_done, 4)
                    dve.wait_ge(one_done, gi + 4)
                    wait(dve, rest_done, gi)
                    dve.scalar_tensor_tensor(out=lost[:], in0=one[:], scalar=-1.0, in1=ex[:], op0=ALU.add,
                                             op1=ALU.subtract).then_inc(lost_done, 4)
                    dve.wait_ge(hi_b, gi + 4)
                    wait(dve, b_rep, 4 * (gi - 4))
                    dve.tensor_tensor(parts[:, par, BB, 1], ps_in[:], parts[:, par, BB, 0].bitcast(F32),
                                      ALU.subtract).then_inc(lo_b, 4)
                if u % 4 == 2:
                    dve.wait_ge(hi_c, gi + 4)
                    wait(dve, c_rep, 4 * (gi - 4))
                    dve.tensor_tensor(parts[:, par, CC, 1], ps_dt[:], parts[:, par, CC, 0].bitcast(F32),
                                      ALU.subtract).then_inc(lo_c, 4)

            skewed(dve, STEPS, UNROLL, PEEL, body)

        @block.gpsimd
        def _(pool):
            for t in (decay[:, 0], decay[:, 1], feed[:]):
                pool.memset(t, 0.0).then_inc(zeroed, 1)

            def body(s, u):
                p = s - LAG_A
                if live(p, STEPS):
                    b = u % 2
                    pool.wait_ge(ahead_done, p + 1)
                    pool.wait_ge(back_done, p + 1)
                    pool.tensor_tensor(ahead[:, b, :, 0:TOK], ahead[:, b, :, 0:TOK], back[:, b, :, 0:TOK],
                                       ALU.add).then_inc(summed, 1)
                if not live(s, STEPS):
                    return
                par, gi = u // 4, s - u % 4
                if u % 4 == 2:
                    pool.wait_ge(ln_done, gi + 4)
                    pool.wait_ge(lost_done, gi + 4)
                    pool.tensor_tensor(rest[:], ln[:], lost[:], ALU.subtract).then_inc(rest_done, 4)
                    pool.wait_ge(rest_done, gi + 4)
                    pool.wait_ge(relu_done, gi + 4)
                    wait(pool, hi_d, gi)
                    wait(pool, lo_d, gi)
                    pool.tensor_tensor(delta[:], relu[:], rest[:], ALU.add).then_inc(delta_done, 4)
                    pool.wait_ge(delta_done, gi + 4)
                    wait(pool, hi_u, gi)
                    wait(pool, lo_u, gi)
                    pool.wait_ge(xp_done, gi + 4)
                    pool.tensor_tensor(du[:], delta[:], xp[:, par], ALU.mult).then_inc(du_done, 4)
                if u % 4 == 3:
                    pool.wait_ge(hi_d, gi + 4)
                    wait(pool, d_ps, 4 * (gi - 4))
                    pool.tensor_tensor(parts[:, par, DT, 1], delta[:], parts[:, par, DT, 0].bitcast(F32),
                                       ALU.subtract).then_inc(lo_d, 4)
                    pool.wait_ge(hi_u, gi + 4)
                    wait(pool, u_rep, 4 * (gi - 4))
                    pool.tensor_tensor(parts[:, par, DU, 1], du[:], parts[:, par, DU, 0].bitcast(F32),
                                       ALU.subtract).then_inc(lo_u, 4)

            skewed(pool, STEPS, UNROLL, PEEL, body)


def gated(nc, dram, tag, group, src, y, func, dst, sums=None):
    with ExitStack() as ctx:
        m = Scope(nc, ctx)
        consts, c = m.consts(group, tag)
        gate, gated_y = m.sb(tag + "gate", [P, 2, N]), m.sb(tag + "gy", [P, 2, N])
        ps_z, ps_o = m.banks(tag + "psz", 3), m.banks(tag + "pso", 2)
        const_in, z_done, gate_done, gy_done, o_done, dst_done = (
            m.sem(tag + t) for t in ("const", "zd", "gated", "gyd", "od", "dstd"))
        block = ctx.enter_context(nc.Block())
        units = [(n, h) for n in range(CHUNKS) for h in range(HALVES)]

        @block.sync
        def _(sp):
            sp.dma_start(consts[:], dram["pack_" + group]).then_inc(const_in, 16)

        @block.tensor
        def _(pe):
            pe.wait_ge(const_in, 16)
            for k in range(len(units) + 2):
                if k < len(units):
                    n, h = units[k]
                    wait(pe, gate_done, k - 2)
                    pe.matmul(ps_z[k % 3][:], c["wz"][:, h * P:(h + 1) * P], src[:, n * N:(n + 1) * N], start=True,
                              stop=True).then_inc(z_done, 1)
                if k >= 2:
                    n, h = units[k - 2]
                    pe.wait_ge(gy_done, k - 1)
                    if h == 0:
                        wait(pe, dst_done, n - 1)
                    pe.matmul(ps_o[n % 2][:], c["wo"][:, h * P:(h + 1) * P], gated_y[:, k % 2], start=(h == 0),
                              stop=(h == 1)).then_inc(o_done, 1)

        @block.scalar
        def _(act):
            for k in range(len(units)):
                act.wait_ge(z_done, k + 1)
                wait(act, gy_done, k - 1)
                act.activation(gate[:, k % 2], ps_z[k % 3][:], func).then_inc(gate_done, 1)

        @block.vector
        def _(dve):
            dve.wait_ge(const_in, 16)

            def finish(n):
                dve.wait_ge(o_done, 2 * n + 2)
                cols = slice(n * N, (n + 1) * N)
                if sums is None:
                    dve.scalar_tensor_tensor(out=dst[:, cols], in0=src[:, cols], scalar=c["skip"],
                                             in1=ps_o[n % 2][:], op0=ALU.mult, op1=ALU.add).then_inc(dst_done, 1)
                else:
                    dve.tensor_scalar(dst[:, cols], ps_o[n % 2][:], 1.0, 0.0, ALU.mult, ALU.add,
                                      accum_out=sums[:, n:n + 1]).then_inc(dst_done, 1)

            for k, (n, h) in enumerate(units):
                dve.wait_ge(gate_done, k + 1)
                wait(dve, o_done, k - 1)
                dve.tensor_tensor(gated_y[:, k % 2], y[:, h, n * N:(n + 1) * N], gate[:, k % 2],
                                  ALU.mult).then_inc(gy_done, 1)
                if h == 1 and n >= 1:
                    finish(n - 1)
            finish(CHUNKS - 1)


def groupnorm(nc, dram, src, sums, x):
    with ExitStack() as ctx:
        m = Scope(nc, ctx)
        consts, c = m.consts("l2post", "g")
        spread, total, scaled = m.sb("g_spread", [P, HW]), m.sb("g_total", [P, BL]), m.sb("g_scaled", [P, 2, HW])
        means, square, lnv, rstd, gain, shift, offset = (m.sb("g_" + t, [P, BL]) for t in (
            "means", "square", "lnv", "rstd", "gain", "shift", "offset"))
        ps_m, ps_v = m.banks("g_psm", 1, (P, BL))[0], m.banks("g_psv", 1, (P, BL))[0]
        const_in, total_done, mean_ps, mean_done, square_done, var_ps, logged, rstd_done, gain_done, shift_done, \
            offset_done, scaled_done, x_done = (m.sem("g_" + t) for t in (
                "const", "totald", "meanps", "meand", "squared", "varps", "logged", "rstdd", "gaind", "shiftd",
                "offsetd", "scaledd", "xd"))
        block = ctx.enter_context(nc.Block())

        @block.sync
        def _(sp):
            sp.dma_start(consts[:], dram["pack_l2post"]).then_inc(const_in, 16)

        @block.tensor
        def _(pe):
            pe.wait_ge(const_in, 16)
            pe.wait_ge(total_done, 1)
            pe.matmul(ps_m[:], c["gavg"], total[:], start=True, stop=True).then_inc(mean_ps, 1)
            pe.wait_ge(square_done, BL)
            pe.matmul(ps_v[:], c["gavg"], square[:], start=True, stop=True).then_inc(var_ps, 1)

        @block.scalar
        def _(act):
            act.preload_act_table_set("natural_log_exp_and_others")
            act.wait_ge(mean_done, 1)
            for bl in range(BL):
                wait(act, square_done, bl)
                act.activation(spread[:], src[:, bl * HW:(bl + 1) * HW], ACT.Square, bias=means[:, bl:bl + 1],
                               accum_out=square[:, bl:bl + 1]).then_inc(square_done, 1)
            act.wait_ge(var_ps, 1)
            act.activation(lnv[:], ps_v[:], ACT.Ln, scale=1.0 / HW, bias=LN_EPS).then_inc(logged, 1)
            act.wait_ge(logged, 1)
            act.activation(rstd[:], lnv[:], ACT.Exp, scale=-0.5).then_inc(rstd_done, 1)
            act.wait_ge(gain_done, 1)
            act.wait_ge(offset_done, 1)
            for bl in range(BL):
                wait(act, x_done, bl - 1)
                act.activation(scaled[:, bl % 2], src[:, bl * HW:(bl + 1) * HW], ACT.Identity,
                               scale=gain[:, bl:bl + 1], bias=offset[:, bl:bl + 1]).then_inc(scaled_done, 1)

        @block.vector
        def _(dve):
            pairs = sums.rearrange("p (b k) -> p k b", k=HW // N)
            dve.tensor_tensor(total[:], pairs[:, 0], pairs[:, 1], ALU.add).then_inc(total_done, 1)
            dve.wait_ge(mean_ps, 1)
            dve.tensor_scalar(means[:], ps_m[:], -1.0 / HW, None, ALU.mult).then_inc(mean_done, 1)
            dve.wait_ge(const_in, 16)
            dve.wait_ge(rstd_done, 1)
            dve.tensor_scalar(gain[:], rstd[:], c["gnw"], None, ALU.mult).then_inc(gain_done, 1)
            dve.wait_ge(mean_done, 1)
            dve.wait_ge(gain_done, 1)
            dve.tensor_tensor(shift[:], means[:], gain[:], ALU.mult).then_inc(shift_done, 1)
            dve.wait_ge(shift_done, 1)
            dve.tensor_scalar(offset[:], shift[:], c["gnb"], None, ALU.add).then_inc(offset_done, 1)
            for bl in range(BL):
                dve.wait_ge(scaled_done, bl + 1)
                cols = slice(bl * HW, (bl + 1) * HW)
                dve.tensor_tensor(x[:, cols], x[:, cols], scaled[:, bl % 2], ALU.add).then_inc(x_done, 1)


def convolve3(nc, dram, xn, xc):
    with ExitStack() as ctx:
        m = Scope(nc, ctx)
        consts, c = m.consts("l3conv", "c")
        taps = 4
        folded = m.sb("c_folded", [P, taps, HALVES, P])
        banks = m.banks("c_ps", 4)
        const_in, folded_done, conv_done, silu_done = (m.sem("c_" + t) for t in ("const", "foldedd", "convd", "silud"))
        block = ctx.enter_context(nc.Block())

        @block.sync
        def _(sp):
            sp.dma_start(consts[:], dram["pack_l3conv"]).then_inc(const_in, 16)

        @block.vector
        def _(dve):
            dve.wait_ge(const_in, 16)
            for k in range(taps):
                for h in range(HALVES):
                    dve.tensor_tensor(folded[:, k, h], c["wxi"][:, h * P:(h + 1) * P],
                                      c["convw"][:, k * P:(k + 1) * P], ALU.mult).then_inc(folded_done, 1)

        @block.tensor
        def _(pe):
            pe.wait_ge(folded_done, taps * HALVES)
            for u in range(HALVES * CHUNKS):
                h, n = divmod(u, CHUNKS)
                wait(pe, silu_done, u - 3)
                for back in range(taps):
                    lost = back if n * N % HW == 0 else 0
                    mm = pe.matmul(banks[u % 4][:, lost:N], folded[:, taps - 1 - back, h],
                                   xn[:, n * N + lost - back:(n + 1) * N - back], start=(back == 0),
                                   stop=(back == taps - 1))
                mm.then_inc(conv_done, 1)

        @block.scalar
        def _(act):
            act.wait_ge(const_in, 16)
            for u in range(HALVES * CHUNKS):
                h, n = divmod(u, CHUNKS)
                act.wait_ge(conv_done, u + 1)
                act.activation(xc[:, h, n * N:(n + 1) * N], banks[u % 4][:], ACT.Silu,
                               bias=c["convb"]).then_inc(silu_done, 1)


def project3(nc, dram, src, x, out, resid):
    with ExitStack() as ctx:
        m = Scope(nc, ctx)
        consts, c = m.consts("l3post", "j")
        banks = m.banks("j_ps", 3)
        const_in, proj_done, out_done, resid_done = (m.sem("j_" + t) for t in ("const", "projd", "outd", "residd"))
        block = ctx.enter_context(nc.Block())

        @block.sync
        def _(sp):
            sp.dma_start(consts[:], dram["pack_l3post"]).then_inc(const_in, 16)

        @block.tensor
        def _(pe):
            pe.wait_ge(const_in, 16)
            for n in range(CHUNKS):
                wait(pe, out_done, n - 2)
                pe.matmul(banks[n % 3][:], c["wpj"], src[:, n * N:(n + 1) * N], start=True,
                          stop=True).then_inc(proj_done, 1)

        @block.vector
        def _(dve):
            dve.wait_ge(const_in, 16)
            for n in range(CHUNKS):
                cols = slice(n * N, (n + 1) * N)
                dve.wait_ge(proj_done, n + 1)
                dve.scalar_tensor_tensor(out=out[:, cols], in0=banks[n % 3][:], scalar=c["pjb"], in1=x[:, cols],
                                         op0=ALU.add, op1=ALU.add).then_inc(out_done, 1)

        @block.gpsimd
        def _(pool):
            for n in range(CHUNKS):
                cols = slice(n * N, (n + 1) * N)
                pool.wait_ge(out_done, n + 1)
                pool.tensor_tensor(resid[:, cols], out[:, cols], x[:, cols], ALU.add).then_inc(resid_done, 1)


def scan3(nc, dram, xc, selr, ysel):
    with ExitStack() as ctx:
        m = Scope(nc, ctx)
        consts, c = m.consts("l3", "r")
        wdt = m.sb("r_wdtb", [P, P])
        delta, du, rest = m.sb("r_delta", [P, N]), m.sb("r_du", [P, N]), m.sb("r_rest", [P, N])
        relu, ex, one, ln, lost = (m.sb("r_" + t, [P, N]) for t in ("relu", "ex", "one", "ln", "lost"))
        parts = m.sb("r_parts", [P, 2, 3, 2, N], F32R)
        decay, feed = m.sb("r_decay", [P, 2, Q4, N]), m.sb("r_feed", [P, Q4, N])
        state, prod = m.sb("r_state", [P, 2, Q4, N]), m.sb("r_prod", [P, 2, Q4, N])
        carry = m.sb("r_carry", [P, Q4, Q4])
        bs, cs = m.sb("r_bs", [P, 2, Q4, N]), m.sb("r_cs", [P, 2, Q4, N])
        ps_bc, ps_dt, ps_y = (m.banks("r_p" + t, 1)[0] for t in ("bc", "dt", "y"))
        ps_d, ps_r = m.banks("r_pd", 2), m.banks("r_pr", 3)
        const_in, w_ps, w_done = (m.sem("r_" + t) for t in ("const", "wps", "wd"))
        dt_ps, bc_ps, away_done, relu_done, ex_done, one_done, ln_done, lost_done, rest_done, delta_done, \
            du_done = (m.sem("r_" + t) for t in (
                "dtps", "bcps", "awayd", "relud", "exd", "oned", "lnd", "lostd", "restd", "deltad", "dud"))
        hi_d, hi_u, hi_bc, lo_d, lo_u, lo_bc = (m.sem("r_" + t) for t in ("hid", "hiu", "hibc", "lod", "lou", "lobc"))
        d_ps, decayed, u_rep, fed, scanned, multiplied, b_rep, c_rep, b_copied, c_copied, carried, y_part, y_done = (
            m.sem("r_" + t) for t in ("dps", "decayed", "urep", "fed", "scanned", "mult", "brepd", "crepd", "bcop",
                                      "ccop", "carried", "ypart", "ydone"))
        aneg, a_on_vector, a_on_scalar = prepare_a(m, "r_", c, const_in, 4)
        LAG_B, LAG_D, LAG_U, LAG_Y = 2, 5, 6, 7
        DT, DU, BC = range(3)
        block = ctx.enter_context(nc.Block())

        def columns(s, u):
            if isinstance(s, int):
                return slice(s // 4 * N, (s // 4 + 1) * N)
            return ds((s - u % UNROLL) * (N // 4) + u % UNROLL // 4 * N, N)

        @block.sync
        def _(sp):
            sp.dma_start(consts[:], dram["pack_l3"]).then_inc(const_in, 16)

        @block.tensor
        def _(pe):
            pe.wait_ge(const_in, 16)
            pe.matmul(ps_dt[:, 0:P], c["xpr"][0:16], c["dtw"][0:16], start=True, stop=True).then_inc(w_ps, 1)
            pe.wait_ge(w_done, 1)

            def spread(bank, sel, which, par):
                for part in range(2):
                    mm = pe.matmul(bank[:], selr[:, sel * P:(sel + 1) * P], parts[:, par, which, part],
                                   start=(part == 0), stop=(part == 1))
                return mm

            def body(s, u):
                par = u // 4
                if u % 4 == 0 and live(s, STEPS):
                    cols = columns(s, u)
                    wait(pe, relu_done, s)
                    pe.matmul(ps_dt[:], wdt[:], xc[:, cols], start=True, stop=True).then_inc(dt_ps, 4)
                    wait(pe, lo_bc, s)
                    pe.matmul(ps_bc[:], c["wbc"], xc[:, cols], start=True, stop=True).then_inc(bc_ps, 4)

                def decays(qs):
                    p, v = s - LAG_D, u - LAG_D
                    if not live(p, STEPS):
                        return
                    for q in qs:
                        if v % 4 == 0 and q == 0:
                            pe.wait_ge(lo_d, p + 4)
                        wait(pe, decayed, 4 * p + q - 1)
                        spread(ps_d[q % 2], 4 * q + v % 4, DT, v % UNROLL // 4).then_inc(d_ps, 1)

                def states(which):
                    p, v = s - LAG_B, u - LAG_B
                    if not live(p, STEPS):
                        return
                    if which == 0 and v % 4 == 0:
                        pe.wait_ge(lo_bc, p + 4)
                    if isinstance(s, int) and s <= LAG_U:
                        wait(pe, (b_copied, c_copied)[which], p)
                    else:
                        pe.wait_ge(fed, 4 * (s - 1 - LAG_U) + 2 + which)
                    spread(ps_r[which], 16 + 2 * (v % 4) + which, BC, v % UNROLL // 4)\
                        .then_inc((b_rep, c_rep)[which], 1)

                decays((0, 1))
                states(0)
                decays((2,))
                states(1)
                decays((3,))
                p, v = s - LAG_U, u - LAG_U
                if live(p, STEPS):
                    if v % 4 == 0:
                        pe.wait_ge(lo_u, p + 4)
                    for q in range(Q4):
                        if q == 0:
                            wait(pe, fed, 4 * (p - 1) + 4)
                        elif q == 1:
                            copied_p = s - LAG_B
                            if live(copied_p, STEPS):
                                pe.wait_ge(b_copied, copied_p + 1)
                            else:
                                pe.wait_ge(fed, 4 * (p - 1) + 2)
                        elif q == 2:
                            copied_p = s - LAG_B
                            if live(copied_p, STEPS):
                                pe.wait_ge(c_copied, copied_p + 1)
                            else:
                                pe.wait_ge(fed, 4 * (p - 1) + 3)
                        else:
                            pe.wait_ge(fed, 4 * p + 1)
                        spread(ps_r[(2 + q) % 3], 4 * q + v % 4, DU, v % UNROLL // 4).then_inc(u_rep, 1)
                p, v = s - LAG_Y, u - LAG_Y
                if live(p, STEPS):
                    if v % 4 == 0:
                        wait(pe, y_done, p)
                    pe.wait_ge(multiplied, 4 * p + 4)
                    for q in range(Q4):
                        mm = pe.matmul(ps_y[q * 32:(q + 1) * 32], ysel[:, v % 4 * 32:(v % 4 + 1) * 32],
                                       prod[:, v % 2, q], start=(v % 4 == 0), stop=(v % 4 == 3),
                                       tile_position=(0, q * 32))
                    mm.then_inc(y_part, 1)

            skewed(pe, STEPS, UNROLL, PEEL, body)

        @block.scalar
        def _(act):
            act.preload_act_table_set("natural_log_exp_and_others")
            act.wait_ge(const_in, 16)
            act.wait_ge(w_ps, 1)
            act.activation(wdt[:], ps_dt[:, 0:P], ACT.Copy).then_inc(w_done, 1)
            a_on_scalar(act)

            def body(s, u):
                def decays(qs):
                    p, v = s - LAG_D, u - LAG_D
                    if not live(p, STEPS):
                        return
                    for q in qs:
                        act.wait_ge(d_ps, 4 * p + q + 1)
                        wait(act, scanned, 4 * (p - 2) + q + 1)
                        act.activation(decay[:, v % 2, q], ps_d[q % 2][:], ACT.Exp,
                                       scale=aneg[:, v % 4:v % 4 + 1]).then_inc(decayed, 1)

                def states(which):
                    p, v = s - LAG_B, u - LAG_B
                    if not live(p, STEPS):
                        return
                    act.wait_ge((b_rep, c_rep)[which], p + 1)
                    wait(act, (fed, multiplied)[which], 4 * (p - 5) + v % 4 + 1)
                    act.activation((bs, cs)[which][:, v % UNROLL // 4, v % 4], ps_r[which][:],
                                   ACT.Copy).then_inc((b_copied, c_copied)[which], 1)

                decays((0, 1))
                states(0)
                decays((2,))
                states(1)
                decays((3,))
                if not live(s, STEPS):
                    return
                par, gi = u // 4, s - u % 4
                if u % 4 == 0:
                    act.wait_ge(dt_ps, gi + 4)
                    wait(act, lost_done, gi)
                    act.activation(ex[:], ps_dt[:], ACT.Abs, bias=c["dtb"]).then_inc(away_done, 4)
                    wait(act, delta_done, gi)
                    act.activation(relu[:], ps_dt[:], ACT.Relu, bias=c["dtb"]).then_inc(relu_done, 4)
                    act.wait_ge(away_done, gi + 4)
                    act.activation(ex[:], ex[:], ACT.Exp, scale=-1.0).then_inc(ex_done, 4)
                if u % 4 == 1:
                    act.wait_ge(bc_ps, gi + 4)
                    wait(act, c_rep, gi - 4)
                    act.activation(parts[:, par, BC, 0], ps_bc[:], ACT.Copy).then_inc(hi_bc, 4)
                    act.wait_ge(one_done, gi + 4)
                    wait(act, rest_done, gi)
                    act.activation(ln[:], one[:], ACT.Ln).then_inc(ln_done, 4)
                if u % 4 == 3:
                    act.wait_ge(delta_done, gi + 4)
                    wait(act, d_ps, 4 * (gi - 4))
                    act.activation(parts[:, par, DT, 0], delta[:], ACT.Copy).then_inc(hi_d, 4)
                    act.wait_ge(du_done, gi + 4)
                    wait(act, u_rep, 4 * (gi - 4))
                    act.activation(parts[:, par, DU, 0], du[:], ACT.Copy).then_inc(hi_u, 4)

            skewed(act, STEPS, UNROLL, PEEL, body)

        @block.vector
        def _(dve):
            dve.wait_ge(const_in, 16)
            a_on_vector(dve)

            def body(s, u):
                p, v = s - LAG_U, u - LAG_U
                if live(p, STEPS):
                    b, g, lc = v % 2, v % 4, v % UNROLL // 4
                    for q in range(Q4):
                        dve.wait_ge(u_rep, 4 * p + q + 1)
                        if g == 0:
                            dve.wait_ge(b_copied, p + q + 1)
                        wait(dve, scanned, 4 * (p - 1) + q + 1)
                        dve.tensor_tensor(feed[:, q], ps_r[(2 + q) % 3][:], bs[:, lc, q], ALU.mult).then_inc(fed, 1)
                    for q in range(Q4):
                        dve.wait_ge(decayed, 4 * p + q + 1)
                        dve.wait_ge(fed, 4 * p + q + 1)
                        wait(dve, multiplied, 4 * (p - 2) + q + 1)
                        if lc == 1:
                            dve.wait_ge(carried, p - 2 + g)
                            start = carry[:, g, q:q + 1]
                        else:
                            start = 0.0
                        dve.tensor_tensor_scan(state[:, b, q], decay[:, b, q], feed[:, q], start, ALU.mult,
                                               ALU.add).then_inc(scanned, 1)
                    if lc == 0:
                        dve.wait_ge(scanned, 4 * p + 4)
                        dve.tensor_copy(carry[:, g], state[:, b, :, N - 1]).then_inc(carried, 2)
                p, v = s - LAG_Y, u - LAG_Y
                if v % 4 == 3 and live(p, STEPS):
                    dve.wait_ge(y_part, p + 1)
                    cols = columns(p, v)
                    dve.wait_ge(du_done, p + 1)
                    dve.scalar_tensor_tensor(out=xc[:, cols], in0=xc[:, cols], scalar=c["dp"], in1=ps_y[:],
                                             op0=ALU.mult, op1=ALU.add).then_inc(y_done, 4)
                if not live(s, STEPS):
                    return
                par, gi = u // 4, s - u % 4
                if u % 4 == 1:
                    dve.wait_ge(ex_done, gi + 4)
                    wait(dve, ln_done, gi)
                    dve.tensor_scalar(one[:], ex[:], 1.0, None, ALU.add).then_inc(one_done, 4)
                    dve.wait_ge(one_done, gi + 4)
                    wait(dve, rest_done, gi)
                    dve.scalar_tensor_tensor(out=lost[:], in0=one[:], scalar=-1.0, in1=ex[:], op0=ALU.add,
                                             op1=ALU.subtract).then_inc(lost_done, 4)
                    dve.wait_ge(hi_bc, gi + 4)
                    wait(dve, c_rep, gi - 4)
                    dve.tensor_tensor(parts[:, par, BC, 1], ps_bc[:], parts[:, par, BC, 0].bitcast(F32),
                                      ALU.subtract).then_inc(lo_bc, 4)

            skewed(dve, STEPS, UNROLL, PEEL, body)

        @block.gpsimd
        def _(pool):
            def body(s, u):
                p, v = s - LAG_U, u - LAG_U
                if live(p, STEPS):
                    wait(pool, y_part, p - 1)
                    for q in range(Q4):
                        pool.wait_ge(scanned, 4 * p + q + 1)
                        if v % 4 == 0:
                            pool.wait_ge(c_copied, p + q + 1)
                        pool.tensor_tensor(prod[:, v % 2, q], state[:, v % 2, q], cs[:, v % UNROLL // 4, q],
                                           ALU.mult).then_inc(multiplied, 1)
                if not live(s, STEPS):
                    return
                par, gi = u // 4, s - u % 4
                if u % 4 == 2:
                    pool.wait_ge(ln_done, gi + 4)
                    pool.wait_ge(lost_done, gi + 4)
                    pool.tensor_tensor(rest[:], ln[:], lost[:], ALU.subtract).then_inc(rest_done, 4)
                    pool.wait_ge(rest_done, gi + 4)
                    pool.wait_ge(relu_done, gi + 4)
                    wait(pool, hi_d, gi)
                    wait(pool, lo_d, gi)
                    pool.tensor_tensor(delta[:], relu[:], rest[:], ALU.add).then_inc(delta_done, 4)
                    pool.wait_ge(delta_done, gi + 4)
                    wait(pool, hi_u, gi)
                    wait(pool, lo_u, gi)
                    pool.tensor_tensor(du[:], delta[:], xc[:, columns(gi, u - u % 4)], ALU.mult).then_inc(du_done, 4)
                if u % 4 == 3:
                    pool.wait_ge(hi_d, gi + 4)
                    wait(pool, d_ps, 4 * (gi - 4))
                    pool.tensor_tensor(parts[:, par, DT, 1], delta[:], parts[:, par, DT, 0].bitcast(F32),
                                       ALU.subtract).then_inc(lo_d, 4)
                    pool.wait_ge(hi_u, gi + 4)
                    wait(pool, u_rep, 4 * (gi - 4))
                    pool.tensor_tensor(parts[:, par, DU, 1], du[:], parts[:, par, DU, 0].bitcast(F32),
                                       ALU.subtract).then_inc(lo_u, 4)

            skewed(pool, STEPS, UNROLL, PEEL, body)


def load(nc, dram, x):
    x_in = nc.alloc_semaphore(name="x_in")
    with nc.Block() as block:
        @block.sync
        def _(sp):
            for h in range(HALVES):
                sp.dma_start(x[h * C:(h + 1) * C].rearrange("c (b n) -> c b n", b=BL),
                             dram["x"][h * BL:(h + 1) * BL].rearrange("b c n -> c b n")).then_inc(x_in, 16)
            sp.wait_ge(x_in, 16 * HALVES)


def program(nc, dram, out):
    with ExitStack() as kept:
        m = Scope(nc, kept)
        x = m.sb("x_act", [P, COLS])
        with nc.cleanup_on_exit(), ExitStack() as layer:
            xn = Scope(nc, layer).sb("x_norm0", [P, COLS])
            load(nc, dram, x)
            layernorm(nc, dram, "n1", x, xn, "ln1_scale", "ln1_bias")
            attention(nc, dram, xn, x)
            layernorm(nc, dram, "n2", x, xn, "ln2_scale", "ln2_bias")
            mlp(nc, dram, "m0", "mlp0", xn, x, x)
        selr, ysel = m.sb("selr", [P, 24 * P], F32R), m.sb("ysel", [P, 4 * 32])
        with nc.cleanup_on_exit():
            antialiased(nc, dram, x)
            selectors(nc, dram, selr, ysel)
        y = m.sb("y_inner", [P, HALVES, COLS])
        with nc.cleanup_on_exit():
            scan2(nc, dram, x, y, selr, ysel)
            with ExitStack() as layer:
                mem = Scope(nc, layer)
                mixed, sums = mem.sb("mixed2", [P, COLS]), mem.sb("chunk_sums", [P, CHUNKS])
                gated(nc, dram, "o2", "l2post", x, y, ACT.Gelu, mixed, sums)
                groupnorm(nc, dram, mixed, sums, x)
        xn = m.sb("x_norm3", [P, COLS])
        layernorm(nc, dram, "n3", x, xn, "lnw", "lnb")
        convolve3(nc, dram, xn, y)
        scan3(nc, dram, y[:].rearrange("p h n -> p (h n)"), selr, ysel)
        mixed = m.sb("mixed3", [P, COLS])
        gated(nc, dram, "o3", "l3post", xn, y, ACT.Silu, mixed)
        layernorm(nc, dram, "n4", mixed, xn, "lnw", "lnb")
        project3(nc, dram, xn, x, mixed, x)
        mlp(nc, dram, "m3", "mlp3", mixed, x, x, out)


def kernel(**inputs):
    import concourse.bacc as _bacc
    from concourse import mybir as _mybir
    from concourse.bass_utils import run_bass_kernel_spmd as _run

    host = {k: np.asarray(v) for k, v in inputs.items()}
    data = pack(host)
    data["x"] = host["x"].reshape(B, C, HW)
    data["rel"] = host["L0_conv_rel_bias_table"].reshape(1, -1)
    nc = _bacc.Bacc("TRN2", target_bir_lowering=False, num_devices=1)
    arrays, dram = {}, {}
    for name, a in data.items():
        a = np.ascontiguousarray(a)
        arrays[f"in_{name}_dram"] = a
        dram[name] = nc.dram_tensor(f"in_{name}_dram", a.shape, _mybir.dt.from_np(a.dtype),
                                    kind="ExternalInput").ap()
    out = nc.dram_tensor("out_0_dram", (B, C, HW), F32, kind="ExternalOutput").ap()
    program(nc, dram, out)
    r = _run(nc, [arrays], core_ids=[0])
    return r.results[0]["out_0_dram"].reshape(B, C, H, W)
```

```python
from contextlib import ExitStack

import numpy as np

import concourse.bass as bass
from concourse import mybir

F32 = mybir.dt.float32
F32R = mybir.dt.float32r
ALU = mybir.AluOpType
ACT = mybir.ActivationFunctionType
AX = mybir.AxisListType
ds = bass.ds

B, C, H, W = 8, 64, 32, 32
P = 128
HALVES = P // C
BL = B // HALVES
HW = H * W
COLS = BL * HW
N = 512
CHUNKS = COLS // N
WS = 8
HEADS = 8
HD = C // HEADS
WIN = WS * WS
PAIRS = COLS // WIN
ROWCOLS = WS * W
WROW = W // WS
HPAIRS = HEADS // 2
REL = 2 * WS - 1
LN_EPS = 1e-5
DEEP = 4
TAPS = 12
UPW = 74
PITCH = 80
RB = 4
TILES = H // RB
KM = 12
BLK = 2 * RB * PITCH // P
UPB = BLK * (TILES - 1) + KM
GAIN = float(np.sqrt(2.0))
SLOPE = 0.2
CLAMP = 256.0
NS = 16
D8 = P // NS
TOK = 8
GCN = C // TOK
DIN = 2 * GCN
SLOT = TOK + 1
N2 = 256
DM = C // 4
DI = 2 * DM
Q4 = 4
AMAX = 88.0


def wait(eng, sem, value):
    if isinstance(value, int) and value <= 0:
        return
    eng.wait_ge(sem, value)


def live(p, n):
    return not isinstance(p, int) or 0 <= p < n


def skewed(eng, n, unroll, peel, body):
    for s in range(peel):
        body(s, s % unroll)
    with eng.Fori(0, (n - peel) // unroll) as r:
        for u in range(unroll):
            body(r * unroll + (peel + u), u)
    for s in range(n, n + peel):
        body(s, s % unroll)


def layout(groups):
    at, out = 0, {}
    for name, width in groups:
        out[name] = (at, at + width)
        at += width
    return out, at


CONST = {
    "ln": [("center", P), ("mean", P), ("ln1_scale", 1), ("ln1_bias", 1), ("ln2_scale", 1), ("ln2_bias", 1),
           ("lnw", 1), ("lnb", 1)],
    "attn": [("wq", P), ("wk", P), ("wv", P), ("wp", P), ("ident", P), ("kmask", HEADS), ("vmask", 2 * 32),
             ("bq", 1), ("bk", 1), ("bv", 1), ("bp", 1)],
    "mlp0": [("w1", 4 * P), ("w2", 2 * C), ("b1", 2), ("b2", 1), ("l1b", 1)],
    "fir": [("ident", P)],
    "scan": [("sel", 16 * P), ("seln", 8 * P), ("ysel", 4 * 32)],
    "l2": [("wxp", 2 * P), ("wdt", P), ("wx0", 1), ("wb", P), ("wc", P), ("bdt", 1), ("alog", 2), ("dsk", 1)],
    "l2post": [("wz", 2 * P), ("wo", C), ("gavg", P), ("gnw", 1), ("gnb", 1)],
    "l3conv": [("wxi", 2 * P), ("convw", 4 * P), ("convb", 1)],
    "l3": [("xpr", P), ("dtw", P), ("wbc", P), ("dtb", 1),
           ("alog", 4), ("dp", 1)],
    "l3post": [("wz", 2 * P), ("wo", C), ("skip", 1), ("wpj", P), ("pjb", 1)],
    "mlp3": [("w1", 4 * P), ("w2", 2 * C), ("b1", 2), ("b2", 1), ("l1b", 1)],
}


def blocks(n, m):
    r, c = m.shape
    out = np.zeros((n, r, n, c), np.float32)
    for i in range(n):
        out[i, :, i, :] = m
    return out.reshape(n * r, n * c)


def halves(m):
    out = np.zeros((HALVES, P, P), np.float32)
    for h in range(HALVES):
        out[h, h * C:(h + 1) * C, :] = m
    return out.transpose(1, 0, 2).reshape(P, HALVES * P)


def mlp_pack(w1, b1, w2, b2, l1b):
    a = np.zeros((P, 2, 2, P), np.float32)
    for h in range(2):
        for k in range(2):
            a[h * C:(h + 1) * C, h, k] = w1[:, k * P:(k + 1) * P]
    return {"w1": a.reshape(P, -1), "w2": w2.reshape(2, P, C).transpose(1, 0, 2).reshape(P, -1), "b1": b1.reshape(2, P).T,
            "b2": np.tile(b2, 2)[:, None], "l1b": np.tile(l1b, 2)[:, None]}


def pack(i):
    def two(v):
        return np.tile(np.asarray(v), 2)[:, None]

    def rep(v, n):
        return np.tile(np.asarray(v), n)[:, None]

    eye = np.eye(P, dtype=np.float32)
    wqkv, bqkv = i["L0_conv_w_qkv"], i["L0_conv_b_qkv"]
    part = np.arange(P)
    kmask = ((part % C)[:, None] // HD == np.arange(HEADS)).astype(np.float32)
    c32 = np.arange(32)
    vmask = (c32[None, None, :] // HD == 2 * np.arange(2)[None, :, None] + (part // C)[:, None, None])
    v = {}
    v["ln"] = {"center": eye - blocks(2, np.full((C, C), 1.0 / C, np.float32)),
               "mean": blocks(2, np.full((C, C), 1.0 / C, np.float32)),
               "ln1_scale": two(i["L0_conv_ln1_scale"]), "ln1_bias": two(i["L0_conv_ln1_bias"]),
               "ln2_scale": two(i["L0_conv_ln2_scale"]), "ln2_bias": two(i["L0_conv_ln2_bias"]),
               "lnw": two(i["L3_conv_ln_w"]), "lnb": two(i["L3_conv_ln_b"])}
    v["attn"] = {"wq": blocks(2, wqkv[:, :C]), "wk": blocks(2, wqkv[:, C:2 * C]), "wv": blocks(2, wqkv[:, 2 * C:]),
                 "wp": blocks(2, i["L0_conv_w_proj"]), "ident": eye, "kmask": kmask,
                 "vmask": vmask.astype(np.float32).reshape(P, -1), "bq": two(bqkv[:C]), "bk": two(bqkv[C:2 * C]),
                 "bv": two(bqkv[2 * C:]), "bp": two(i["L0_conv_b_proj"])}
    v["mlp0"] = mlp_pack(i["L0_conv_w_mlp1"], i["L0_conv_b_mlp1"], i["L0_conv_w_mlp2"], i["L0_conv_b_mlp2"],
                         i["L1_conv_bias"])
    v["fir"] = {"ident": eye}
    d8n = np.arange(P)
    sel = np.zeros((P, 16, P), np.float32)
    seln = np.zeros((P, 8, P), np.float32)
    ysel = np.zeros((P, 4, 32), np.float32)
    for k in range(16):
        sel[8 * k + d8n // NS, k, d8n] = 1.0
    for t in range(8):
        seln[NS * t + d8n % NS, t, d8n] = 1.0
    for j in range(4):
        ysel[d8n, j, 8 * j + d8n // NS] = 1.0
    v["scan"] = {"sel": sel.reshape(P, -1), "seln": seln.reshape(P, -1), "ysel": ysel.reshape(P, -1)}
    wi, wx, wdt = i["L2_conv_W_in"], i["L2_conv_W_x"], i["L2_conv_W_dt"]
    v["l2"] = {"wxp": halves(blocks(TOK, wi[:, :DIN])),
               "wdt": blocks(TOK, np.repeat(wdt, DIN, axis=0)), "wx0": rep(wx[:, 0], TOK),
               "wb": blocks(TOK, wx[:, 1:1 + NS]), "wc": blocks(TOK, wx[:, 1 + NS:]),
               "bdt": rep(i["L2_conv_b_dt"], TOK), "alog": i["L2_conv_A_logs"].reshape(2, P).T,
               "dsk": rep(i["L2_conv_Ds"], TOK)}
    v["l2post"] = {"wz": halves(blocks(TOK, wi[:, DIN:])), "wo": blocks(TOK, i["L2_conv_W_out"]),
                   "gavg": blocks(8, np.full((16, 16), 1.0 / 16, np.float32)),
                   "gnw": two(i["L2_conv_gn_w"]), "gnb": two(i["L2_conv_gn_b"])}
    inw, xp, cw = i["L3_conv_in_w"], i["L3_conv_xproj_w"], i["L3_conv_conv_w"]
    xpr = np.zeros((P, P), np.float32)
    dtw = np.zeros((P, P), np.float32)
    xpr[:16] = blocks(Q4, xp[:4])
    dtw[:16] = blocks(Q4, i["L3_conv_dt_w"].T)
    v["l3conv"] = {"wxi": halves(blocks(Q4, inw[:DI].T)),
               "convw": np.broadcast_to(np.tile(cw[:, 0].T[:, None, :], (1, Q4, 1)).reshape(1, -1), (P, 4 * P)),
                   "convb": rep(i["L3_conv_conv_b"], Q4)}
    v["l3"] = {"xpr": xpr, "dtw": dtw, "wbc": blocks(Q4, xp[4:].T),
               "dtb": rep(i["L3_conv_dt_b"], Q4), "alog": i["L3_conv_A_log"].reshape(4, P).T,
               "dp": rep(i["L3_conv_Dp"], Q4)}
    v["l3post"] = {"wz": halves(blocks(Q4, inw[DI:].T)), "wo": blocks(Q4, i["L3_conv_out_w"].T),
                   "skip": np.broadcast_to(i["L3_conv_skip_scale"], (P,))[:, None],
                   "wpj": blocks(2, i["L3_conv_proj_w"].T), "pjb": two(i["L3_conv_proj_b"])}
    v["mlp3"] = mlp_pack(i["L3_conv_fc1_w"].T, i["L3_conv_fc1_b"], i["L3_conv_fc2_w"].T, i["L3_conv_fc2_b"],
                         np.zeros(C, np.float32))
    out = {}
    for group, names in CONST.items():
        at, width = layout(names)
        a = np.zeros((P, width), np.float32)
        for name, (lo, hi) in at.items():
            a[:, lo:hi] = v[group][name]
        out["pack_" + group] = a
    for name, f in (("up", i["L1_conv_up_filter"][::-1, ::-1]), ("down", i["L1_conv_down_filter"])):
        band = np.zeros((RB, W, KM * P // PITCH + 1, PITCH), np.float32)
        for r in range(RB):
            for ix in range(W):
                band[r, ix, 2 * r:2 * r + TAPS, 2 * ix:2 * ix + TAPS] = f
        band = band.reshape(P, -1)[:, :KM * P]
        if name == "down":
            band = band.reshape(P, KM, P).transpose(2, 1, 0).reshape(P, -1)
        out["fir_" + name] = band
    return out


class Scope:

    def __init__(self, nc, ctx):
        self.nc, self.ctx = nc, ctx

    def sb(self, name, shape, dt=F32):
        return self.ctx.enter_context(self.nc.sbuf_tensor(name, shape, dt))

    def banks(self, name, n, shape=(P, N), dt=F32):
        return [self.ctx.enter_context(self.nc.psum_tensor(f"{name}{k}", list(shape), dt)) for k in range(n)]

    def sem(self, name):
        return self.nc.alloc_semaphore(name=name)


def fetch(nc, ctx, dram, groups, tag=""):
    m = Scope(nc, ctx)
    found = {}
    with nc.Block() as block:
        @block.sync
        def _(sp):
            for group in groups:
                at, width = layout(CONST[group])
                t, loaded = m.sb(f"k_{group}{tag}", [P, width]), m.sem(f"k_{group}{tag}_in")
                sp.dma_start(t[:], dram["pack_" + group]).then_inc(loaded, 16)
                found[group] = {name: t[:, lo:hi] for name, (lo, hi) in at.items()}, loaded
    return found


def layernorm(nc, consts, tag, src, dst, scale_name, bias_name):
    with ExitStack() as ctx:
        m = Scope(nc, ctx)
        c, const_in = consts["ln"]
        center, square, normed = m.banks(tag + "cen", DEEP), m.sb(tag + "sq", [P, DEEP, N]), m.sb(tag + "nrm", [P, 2, N])
        var, rstd, lnv = m.banks(tag + "var", DEEP), m.sb(tag + "rstd", [P, DEEP, N]), m.sb(tag + "lnv", [P, 2, N])
        centered, squared, var_done, logged, rstd_done, norm_done, out_done = (
            m.sem(tag + x) for x in ("centered", "squared", "var", "logged", "rstd", "norm", "out"))
        block = ctx.enter_context(nc.Block())

        @block.tensor
        def _(pe):
            pe.wait_ge(const_in, 16)
            for n in range(CHUNKS + 2):
                if n < CHUNKS:
                    wait(pe, norm_done, n - DEEP + 1)
                    pe.matmul(center[n % DEEP][:], c["center"], src[:, n * N:(n + 1) * N], start=True,
                              stop=True).then_inc(centered, 1)
                if n >= 2:
                    k = n - 2
                    pe.wait_ge(squared, k + 1)
                    wait(pe, logged, k - DEEP + 1)
                    pe.matmul(var[k % DEEP][:], c["mean"], square[:, k % DEEP], start=True,
                              stop=True).then_inc(var_done, 1)

        @block.scalar
        def _(act):
            act.preload_act_table_set("natural_log_exp_and_others")
            for n in range(CHUNKS + 2):
                if n < CHUNKS:
                    act.wait_ge(centered, n + 1)
                    wait(act, var_done, n - DEEP + 1)
                    act.activation(square[:, n % DEEP], center[n % DEEP][:], ACT.Square).then_inc(squared, 1)
                if n >= 2:
                    k = n - 2
                    act.wait_ge(var_done, k + 1)
                    act.activation(lnv[:, k % 2], var[k % DEEP][:], ACT.Ln, bias=LN_EPS).then_inc(logged, 1)
                    act.wait_ge(logged, k + 1)
                    wait(act, norm_done, k - DEEP + 1)
                    act.activation(rstd[:, k % DEEP], lnv[:, k % 2], ACT.Exp, scale=-0.5).then_inc(rstd_done, 1)

        @block.vector
        def _(dve):
            dve.wait_ge(const_in, 16)
            for n in range(CHUNKS):
                dve.wait_ge(rstd_done, n + 1)
                dve.wait_ge(squared, n + 1)
                dve.tensor_tensor(normed[:, n % 2], center[n % DEEP][:], rstd[:, n % DEEP],
                                  ALU.mult).then_inc(norm_done, 1)
                dve.wait_ge(norm_done, n + 1)
                dve.tensor_scalar(dst[:, n * N:(n + 1) * N], normed[:, n % 2], c[scale_name], c[bias_name],
                                  ALU.mult, ALU.add).then_inc(out_done, 1)


def mlp(nc, consts, tag, group, src, resid, dst, out=None):
    with ExitStack() as ctx:
        m = Scope(nc, ctx)
        c, const_in = consts[group]
        hidden, act_out, total = m.banks(tag + "hid", 4), m.sb(tag + "gelu", [P, 2, 4, N]), m.banks(tag + "tot", 2)
        bias = m.sb(tag + "bias", [P, 1])
        hid_done, gelu_done, tot_done, bias_done, res_done, stored = (
            m.sem(tag + x) for x in ("hid", "gelu", "tot", "bias", "res", "stored"))
        w1 = c["w1"].rearrange("p (k n) -> p k n", n=P)
        w2 = c["w2"].rearrange("p (k n) -> p k n", n=C)
        block = ctx.enter_context(nc.Block())

        @block.sync
        def _(sp):
            if out is not None:
                for n in range(CHUNKS):
                    sp.wait_ge(res_done, n + 1)
                    bl, at = n * N // HW, n * N % HW
                    for h in range(HALVES):
                        sp.dma_start(out[h * BL + bl, :, at:at + N],
                                     dst[h * C:(h + 1) * C, n * N:(n + 1) * N]).then_inc(stored, 16)
                sp.wait_ge(stored, 16 * HALVES * CHUNKS)

        @block.tensor
        def _(pe):
            pe.wait_ge(const_in, 16)
            for n in range(CHUNKS + 1):
                if n < CHUNKS:
                    for k in range(4):
                        wait(pe, gelu_done, 4 * (n - 1) + k + 1)
                        pe.matmul(hidden[k][:], w1[:, k], src[:, n * N:(n + 1) * N], start=True,
                                  stop=True).then_inc(hid_done, 1)
                if n >= 1:
                    j = n - 1
                    wait(pe, res_done, j - 1)
                    pe.wait_ge(gelu_done, 4 * j + 4)
                    for k in range(2):
                        for h in range(HALVES):
                            mm = pe.matmul(total[j % 2][h * C:(h + 1) * C], w2[:, k], act_out[:, j % 2, 2 * h + k],
                                           start=(k == 0), stop=(k == 1), tile_position=(0, h * C))
                    mm.then_inc(tot_done, 1)

        @block.scalar
        def _(act):
            act.wait_ge(const_in, 16)
            for n in range(CHUNKS):
                wait(act, tot_done, n - 1)
                for k in range(4):
                    act.wait_ge(hid_done, 4 * n + k + 1)
                    act.activation(act_out[:, n % 2, k], hidden[k][:], ACT.Gelu,
                                   bias=c["b1"][:, k % 2:k % 2 + 1]).then_inc(gelu_done, 1)

        @block.vector
        def _(dve):
            dve.wait_ge(const_in, 16)
            dve.tensor_tensor(bias[:], c["b2"], c["l1b"], ALU.add).then_inc(bias_done, 1)
            dve.wait_ge(bias_done, 1)
            for n in range(CHUNKS):
                dve.wait_ge(tot_done, n + 1)
                cols = slice(n * N, (n + 1) * N)
                dve.scalar_tensor_tensor(out=dst[:, cols], in0=total[n % 2][:], scalar=bias[:, 0:1],
                                         in1=resid[:, cols], op0=ALU.add, op1=ALU.add).then_inc(res_done, 1)


def attention(nc, consts, dram, xn, x):
    with ExitStack() as ctx:
        m = Scope(nc, ctx)
        c, const_in = consts["attn"]
        rel = m.sb("relrow", [P, WIN, HEADS])
        bias = m.sb("relbias", [P, HEADS, WIN])
        win = m.sb("win", [P, 2, WROW, 2, WIN])
        qs, ks = m.sb("qs", [P, 2, ROWCOLS]), m.sb("ks", [P, 2, ROWCOLS])
        keys = m.sb("keys", [P, 2, HEADS, WIN])
        vals = m.sb("vals", [P, 2, WROW * HALVES, HPAIRS, 32])
        logit, prob, pnorm = (m.sb(x, [P, 2, HEADS, WIN]) for x in ("logit", "prob", "pnorm"))
        top, total, inv = (m.sb(x, [P, 2, HEADS]) for x in ("top", "total", "inv"))
        probt = m.sb("probt", [P, 2, HPAIRS, P])
        mixed = m.sb("mixed", [P, 2, ROWCOLS])
        ps_qk, ps_v, ps_o, ps_y = (m.banks(x, 1)[0] for x in ("psqk", "psv", "pso", "psy"))
        ps_s, ps_t = m.banks("pss", 2), m.banks("pst", 2)
        rel_in, bias_done = (m.sem("a_" + x) for x in ("rel", "bias"))
        win_done, qk_done, v_done, q_out, k_out, v_out, y_done, x_done, mix_done = (
            m.sem("a_" + x) for x in ("win", "qk", "v", "qout", "kout", "vout", "y", "x", "mix"))
        keys_done, s_done, added, top_done, shifted, exp_done, sum_done, inv_done, norm_done, t_done, t_out, o_done = (
            m.sem("a_" + x) for x in ("keys", "s", "added", "top", "shifted", "exp", "sum", "inv", "norm", "t",
                                      "tout", "o"))
        R = WROW
        LAG_V, LAG_K, LAG_S, LAG_E, LAG_T, LAG_TO, LAG_O, LAG_Y = 3, 3, 4, 5, 6, 6, 7, 8
        UN, PEEL = 8, 16
        block = ctx.enter_context(nc.Block())

        def image(t, base):
            return t[:, ds(base, ROWCOLS)].rearrange("p (y w x) -> p w y x", y=WS, w=R)

        @block.sync
        def _(sp):
            for half in range(HALVES):
                for ny in range(WS):
                    at = half * WIN + ny * WS
                    src = dram["rel"][0:1, 0:1]
                    src = bass.AP(src.tensor, ny * REL * HEADS, [[HEADS, WS], [REL * HEADS, WS], [1, WS * HEADS]])
                    sp.dma_start(rel[at:at + WS].rearrange("p (a b) h -> p a (b h)", a=WS), src).then_inc(rel_in, 16)

        @block.scalar
        def _(act):
            act.preload_act_table_set("natural_log_exp_and_others")
            act.wait_ge(const_in, 16)

            def body(s, u):
                if u % R == 0 and live(s, PAIRS):
                    par = u // R
                    wait(act, v_done, s - R)
                    wait(act, qk_done, s - R)
                    for twice in range(2):
                        act.activation(win[:, par, :, twice].rearrange("p w (y x) -> p w y x", y=WS),
                                       image(xn, s * WIN), ACT.Copy).then_inc(win_done, R // 2)
                p = s - LAG_E
                if live(p, PAIRS):
                    b = (u - LAG_E) % 2
                    act.wait_ge(shifted, p + 1)
                    wait(act, norm_done, p - 1)
                    wait(act, sum_done, p - 1)
                    act.activation(prob[:, b], logit[:, b], ACT.Exp).then_inc(exp_done, 1)
                p = s - LAG_TO
                if live(p, PAIRS):
                    b = (u - LAG_TO) % 2
                    act.wait_ge(t_done, p + 1)
                    wait(act, o_done, p - 1)
                    act.activation(probt[:, b].rearrange("p a b -> p (a b)"), ps_t[b][:], ACT.Copy).then_inc(t_out, 1)
                p = s - LAG_Y
                if (u - LAG_Y) % R == R - 1 and live(p, PAIRS):
                    par = (u - LAG_Y) % UN // R
                    act.wait_ge(o_done, p + 1)
                    wait(act, y_done, p + 1 - 2 * R)
                    act.activation(mixed[:, par], ps_o[:, 0:ROWCOLS], ACT.Identity,
                                   bias=c["bv"]).then_inc(mix_done, R)

            skewed(act, PAIRS, UN, PEEL, body)

        @block.tensor
        def _(pe):
            pe.wait_ge(const_in, 16)

            def body(s, u):
                if u % R == 0 and live(s, PAIRS):
                    par = u // R
                    pe.wait_ge(win_done, s + R)
                    wait(pe, q_out, s)
                    wait(pe, k_out, s)
                    once = win[:, par, :, 0]
                    pe.matmul(ps_qk[:, 0:ROWCOLS], c["wq"], once, start=True, stop=True)
                    pe.matmul(ps_qk[:, ROWCOLS:2 * ROWCOLS], c["wk"], once, start=True, stop=True).then_inc(qk_done, R)
                p = s - LAG_V
                if u % R == LAG_V and live(p, PAIRS):
                    par = u // R
                    wait(pe, v_out, p)
                    for w in range(R):
                        mm = pe.matmul(ps_v[:, w * P:(w + 1) * P], win[:, par, w].rearrange("p a b -> p (a b)"), c["wv"], start=True, stop=True)
                    mm.then_inc(v_done, R)
                p = s - LAG_S
                if live(p, PAIRS):
                    b, w, par = (u - LAG_S) % 2, (u - LAG_S) % R, (u - LAG_S) % UN // R
                    pe.wait_ge(keys_done, p + 1)
                    pe.wait_ge(q_out, p - w + R)
                    wait(pe, added, p - 1)
                    pe.matmul(ps_s[b][:, 0:1], c["ident"], c["kmask"][:, 0:1], start=True, stop=True)
                    for h in range(HALVES):
                        r = slice(h * C, (h + 1) * C)
                        mm = pe.matmul(ps_s[b][r, :], qs[r, par, w * WIN:(w + 1) * WIN],
                                       keys[r, b].rearrange("p a b -> p (a b)"), start=True, stop=True)
                    mm.then_inc(s_done, 1)
                p = s - LAG_T
                if live(p, PAIRS):
                    b = (u - LAG_T) % 2
                    pe.wait_ge(norm_done, p + 1)
                    wait(pe, t_out, p - 1)
                    for k in range(HPAIRS):
                        mm = pe.transpose(ps_t[b][:, k * P:(k + 1) * P],
                                          pnorm[:, b, 2 * k:2 * k + 2].rearrange("p a b -> p (a b)"), c["ident"])
                    mm.then_inc(t_done, 1)
                p = s - LAG_O
                if live(p, PAIRS):
                    b, w, par = (u - LAG_O) % 2, (u - LAG_O) % R, (u - LAG_O) % UN // R
                    pe.wait_ge(t_out, p + 1)
                    pe.wait_ge(v_out, p - w + R)
                    if w == 0:
                        wait(pe, mix_done, p)
                    for first in (0, 1):
                        for h in range(HALVES):
                            for k2 in range(2):
                                quad = 2 * h + k2
                                k = 2 * k2 + first
                                mm = pe.matmul(ps_o[quad * 32:(quad + 1) * 32, w * WIN:(w + 1) * WIN],
                                               vals[:, par, w * HALVES + h, k], probt[:, b, k, h * WIN:(h + 1) * WIN],
                                               start=(first == 0), stop=(first == 1), tile_position=(0, quad * 32))
                    mm.then_inc(o_done, 1)
                p = s - LAG_Y
                if (u - LAG_Y) % R == R - 1 and live(p, PAIRS):
                    par = (u - LAG_Y) % UN // R
                    pe.wait_ge(mix_done, p + 1)
                    wait(pe, x_done, p + 1 - R)
                    pe.matmul(ps_y[:, 0:ROWCOLS], c["wp"],
                              mixed[:, par].rearrange("p (w y x) -> p y w x", w=R, y=WS),
                              start=True, stop=True).then_inc(y_done, R)

            skewed(pe, PAIRS, UN, PEEL, body)

        @block.vector
        def _(dve):
            dve.wait_ge(const_in, 16)
            dve.wait_ge(rel_in, 16 * HALVES * WS)
            dve.tensor_copy(bias[:], rel[:, ::-1, :].rearrange("p j h -> p h j")).then_inc(bias_done, 1)
            dve.wait_ge(bias_done, 1)

            def body(s, u):
                if u % R == 0 and live(s, PAIRS):
                    par = u // R
                    dve.wait_ge(qk_done, s + R)
                    wait(dve, s_done, s - R)
                    dve.tensor_scalar(qs[:, par], ps_qk[:, 0:ROWCOLS], c["bq"], float(HD) ** -0.5, ALU.add,
                                      ALU.mult).then_inc(q_out, R)
                    wait(dve, keys_done, s - R)
                    dve.tensor_scalar(ks[:, par], ps_qk[:, ROWCOLS:2 * ROWCOLS], c["bk"], None,
                                      ALU.add).then_inc(k_out, R)
                p = s - LAG_V
                if u % R == LAG_V and live(p, PAIRS):
                    par = u // R
                    dve.wait_ge(v_done, p + R)
                    wait(dve, o_done, p - R)
                    v = ps_v[:].rearrange("p (a b) -> p a b", b=C)
                    mask = c["vmask"].rearrange("p (a b) -> p a b", a=2)
                    for k2 in range(2):
                        dve.tensor_tensor(vals[:, par, :, 2 * k2:2 * k2 + 2],
                                          v[:, :, None, 32 * k2:32 * k2 + 32].to_broadcast([P, R * HALVES, 2, 32]),
                                          mask[:, None].to_broadcast([P, R * HALVES, 2, 32]),
                                          ALU.mult).then_inc(v_out, R // 2)
                p = s - LAG_S
                if live(p, PAIRS):
                    b = (u - LAG_S) % 2
                    dve.wait_ge(s_done, p + 1)
                    wait(dve, exp_done, p - 1)
                    dve.tensor_tensor(logit[:, b].rearrange("p a b -> p (a b)"), ps_s[b][:],
                                      bias[:].rearrange("p a b -> p (a b)"), ALU.add).then_inc(added, 1)
                    dve.wait_ge(added, p + 1)
                    dve.tensor_reduce(top[:, b], logit[:, b], AX.X, ALU.max).then_inc(top_done, 1)
                    dve.wait_ge(top_done, p + 1)
                    dve.tensor_tensor(logit[:, b], logit[:, b], top[:, b, :, None].to_broadcast([P, HEADS, WIN]),
                                      ALU.subtract).then_inc(shifted, 1)
                p = s - LAG_E
                if live(p, PAIRS):
                    b = (u - LAG_E) % 2
                    dve.wait_ge(exp_done, p + 1)
                    dve.tensor_reduce(total[:, b], prob[:, b], AX.X, ALU.add).then_inc(sum_done, 1)
                    dve.wait_ge(sum_done, p + 1)
                    wait(dve, norm_done, p - 1)
                    dve.reciprocal(inv[:, b], total[:, b]).then_inc(inv_done, 1)
                p = s - LAG_Y
                if (u - LAG_Y) % R == R - 1 and live(p, PAIRS):
                    dve.wait_ge(y_done, p + 1)
                    cols = ds((p + 1 - R) * WIN, ROWCOLS)
                    dve.scalar_tensor_tensor(out=x[:, cols], in0=ps_y[:, 0:ROWCOLS], scalar=c["bp"], in1=x[:, cols],
                                             op0=ALU.add, op1=ALU.add).then_inc(x_done, R)

            skewed(dve, PAIRS, UN, PEEL, body)

        @block.gpsimd
        def _(pool):
            pool.wait_ge(const_in, 16)

            def body(s, u):
                p = s - LAG_K
                if live(p, PAIRS):
                    b, w, par = (u - LAG_K) % 2, (u - LAG_K) % R, (u - LAG_K) % UN // R
                    pool.wait_ge(k_out, p - w + R)
                    wait(pool, s_done, p - 1)
                    pool.tensor_tensor(keys[:, b],
                                       ks[:, par, None, w * WIN:(w + 1) * WIN].to_broadcast([P, HEADS, WIN]),
                                       c["kmask"][:, :, None].to_broadcast([P, HEADS, WIN]),
                                       ALU.mult).then_inc(keys_done, 1)
                p = s - LAG_E
                if live(p, PAIRS):
                    b = (u - LAG_E) % 2
                    pool.wait_ge(inv_done, p + 1)
                    wait(pool, t_done, p - 1)
                    pool.tensor_tensor(pnorm[:, b], prob[:, b], inv[:, b, :, None].to_broadcast([P, HEADS, WIN]),
                                       ALU.mult).then_inc(norm_done, 1)

            skewed(pool, PAIRS, UN, PEEL, body)


def antialiased(nc, consts, dram, x):
    with ExitStack() as ctx:
        m = Scope(nc, ctx)
        c, const_in = consts["fir"]
        upm = m.sb("upm", [P, KM * P])
        downt = m.sb("downt", [P, KM, P])
        pos = m.sb("pos", [P, TILES, N])
        lin, rect, act_y = (m.sb(t, [P, 2, N]) for t in ("lin", "rect", "acty"))
        tile_out = m.sb("tileout", [P, 2, N])
        ps_up, ps_down, ps_t = m.banks("psup", 3), m.banks("psdown", 3), m.banks("pstr", 2)
        band_in, tp_done, tp_out = (m.sem("f_" + t) for t in ("band", "tp", "tpout"))
        up_done, lin_done, rect_done, act_done, acc_done, tile_done, back_done, x_done = (
            m.sem("f_" + t) for t in ("up", "lin", "rect", "act", "acc", "tile", "back", "x"))

        def sources(j):
            return [(t, j - BLK * t) for t in range(TILES) if 0 <= j - BLK * t < KM]

        block = ctx.enter_context(nc.Block())

        @block.sync
        def _(sp):
            sp.dma_start(upm[:], dram["fir_up"]).then_inc(band_in, 16)
            sp.dma_start(downt[:], dram["fir_down"].rearrange("p (k n) -> p k n", n=P)).then_inc(band_in, 16)

        @block.tensor
        def _(pe):
            pe.wait_ge(const_in, 16)
            for t in range(TILES):
                wait(pe, tp_out, t - 1)
                for bl in range(BL):
                    mm = pe.transpose(ps_t[t % 2][:, bl * P:(bl + 1) * P],
                                      x[:, bl * HW + t * P:bl * HW + (t + 1) * P], c["ident"])
                mm.then_inc(tp_done, 1)
            pe.wait_ge(band_in, 16 * 2)

            def up(j):
                pe.wait_ge(tp_out, sources(j)[-1][0] + 1)
                wait(pe, lin_done, j - 2)
                src = sources(j)
                for n, (t, k) in enumerate(src):
                    mm = pe.matmul(ps_up[j % 3][:], upm[:, k * P:(k + 1) * P], pos[:, t], start=(n == 0),
                                   stop=(n == len(src) - 1))
                mm.then_inc(up_done, 1)

            def down(j):
                pe.wait_ge(act_done, j + 1)
                for t, k in sources(j):
                    if k == 0:
                        wait(pe, tile_done, t - 2)
                    mm = pe.matmul(ps_down[t % 3][:], downt[:, k], act_y[:, j % 2], start=(k == 0), stop=(k == KM - 1))
                mm.then_inc(acc_done, 1)

            def back(t):
                pe.wait_ge(tile_done, t + 1)
                wait(pe, x_done, t - 1)
                pe.wait_ge(tp_out, TILES)
                for bl in range(BL):
                    mm = pe.transpose(ps_t[t % 2][:, bl * P:(bl + 1) * P], tile_out[:, t % 2, bl * P:(bl + 1) * P],
                                      c["ident"])
                mm.then_inc(back_done, 1)

            for j in range(UPB + 4):
                if j < UPB:
                    up(j)
                if 2 <= j < UPB + 2:
                    down(j - 2)
                t, rest = divmod(j - 3 - KM, BLK)
                if rest == 0 and 0 <= t < TILES:
                    back(t)

        @block.scalar
        def _(act):
            for t in range(TILES):
                act.wait_ge(tp_done, t + 1)
                act.activation(pos[:, t], ps_t[t % 2][:], ACT.Copy).then_inc(tp_out, 1)
            def finish(t):
                act.wait_ge(acc_done, BLK * t + KM)
                wait(act, back_done, t - 1)
                act.activation(tile_out[:, t % 2], ps_down[t % 3][:], ACT.Copy).then_inc(tile_done, 1)

            for j in range(UPB):
                act.wait_ge(up_done, j + 1)
                wait(act, rect_done, j - 1)
                act.activation(lin[:, j % 2], ps_up[j % 3][:], ACT.Copy, scale=GAIN).then_inc(lin_done, 1)
                t, rest = divmod(j - KM - 1, BLK)
                if rest == 0 and t >= 0:
                    finish(t)
            finish(TILES - 1)

        @block.vector
        def _(dve):
            def put(t):
                dve.wait_ge(back_done, t + 1)
                dve.tensor_copy(x.rearrange("p (b t n) -> p t b n", b=BL, n=P)[:, t],
                                ps_t[t % 2][:].rearrange("p (b n) -> p b n", b=BL)).then_inc(x_done, 1)

            for j in range(UPB):
                dve.wait_ge(lin_done, j + 1)
                dve.scalar_tensor_tensor(out=rect[:, j % 2], in0=lin[:, j % 2], scalar=SLOPE, in1=lin[:, j % 2],
                                         op0=ALU.mult, op1=ALU.max).then_inc(rect_done, 1)
                dve.wait_ge(rect_done, j + 1)
                wait(dve, acc_done, j - 1)
                dve.tensor_scalar(act_y[:, j % 2], rect[:, j % 2], CLAMP, -CLAMP, ALU.min,
                                  ALU.max).then_inc(act_done, 1)
                t, rest = divmod(j - KM - 5, BLK)
                if rest == 0 and t >= 0:
                    put(t)
            for t in range((UPB - 1 - KM - 5) // BLK + 1, TILES):
                put(t)


STEPS = 64
UNROLL, PEEL = 8, 8


def selectors(nc, consts, selr, ysel):
    with ExitStack() as ctx:
        m = Scope(nc, ctx)
        c, const_in = consts["scan"]
        copied = m.sem("z_copied")
        block = ctx.enter_context(nc.Block())

        @block.vector
        def _(dve):
            dve.wait_ge(const_in, 16)
            dve.tensor_copy(selr[:, 0:16 * P], c["sel"]).then_inc(copied, 1)
            dve.tensor_copy(selr[:, 16 * P:], c["seln"]).then_inc(copied, 1)
            dve.tensor_copy(ysel[:], c["ysel"]).then_inc(copied, 1)


def prepare_a(m, tag, c, blocks_of_a):
    low, grown, neg = (m.sb(tag + t, [P, blocks_of_a]) for t in ("alow", "agrown", "aneg"))
    low_done, grown_done, neg_done = (m.sem(tag + t) for t in ("alowd", "agrownd", "anegd"))

    def on_vector(dve):
        dve.tensor_scalar(low[:], c["alog"], AMAX, None, ALU.min).then_inc(low_done, 1)
        dve.wait_ge(grown_done, 1)
        dve.tensor_scalar(neg[:], grown[:], -1.0, None, ALU.mult).then_inc(neg_done, 1)

    def on_scalar(act):
        act.wait_ge(low_done, 1)
        act.activation(grown[:], low[:], ACT.Exp).then_inc(grown_done, 1)
        act.wait_ge(neg_done, 1)

    return neg, on_vector, on_scalar


def scan2(nc, consts, x, y, selr, ysel):
    with ExitStack() as ctx:
        m = Scope(nc, ctx)
        c, const_in = consts["l2"]
        wdt, bdt2, dsk2 = m.sb("s_wdtb", [P, P]), m.sb("s_bdt2", [P, 1]), m.sb("s_dsk2", [P, 1])
        xp = m.sb("s_xp", [P, N])
        delta, du = m.sb("s_delta", [P, N]), m.sb("s_du", [P, N])
        relu, ex, one = (m.sb("s_" + t, [P, N]) for t in ("relu", "ex", "one"))
        parts_b, parts_c = (m.sb("s_parts" + t, [P, 2, N], F32R) for t in "bc")
        parts_d, parts_u = (m.sb("s_parts" + t, [P, 2, 2, N], F32R) for t in "du")
        decay, feed = m.sb("s_decay", [P, 2, N2, SLOT]), m.sb("s_feed", [P, N2, SLOT])
        ahead, back = m.sb("s_ahead", [P, 2, N2, SLOT]), m.sb("s_back", [P, 2, N2, SLOT])
        bs, cs = m.sb("s_bs", [P, 2, TOK, N2]), m.sb("s_cs", [P, 2, TOK, N2])
        low_prod, high_prod = m.sb("s_lprod", [P, TOK // 2, N2]), m.sb("s_hprod", [P, 2, TOK // 2, N2])
        ps_in, ps_dt, ps_y, ps_bc = (m.banks("s_p" + t, 1)[0] for t in ("in", "dt", "y", "bc"))
        ps_d, ps_u = m.banks("s_pd", 2), m.banks("s_pu", 2)
        ready, zeroed = (m.sem("s_" + t) for t in ("ready", "zeroed"))
        xp_ps, xp_done, skip_done, dt_ps, b_ps, c_ps, away_done, relu_done, ex_done, one_done, ln_done, lost_done, \
            rest_done, delta_done, du_done = (m.sem("s_" + t) for t in (
                "xpps", "xpd", "skipd", "dtps", "bps", "cps", "awayd", "relud", "exd", "oned", "lnd", "lostd",
                "restd", "deltad", "dud"))
        hi_d, hi_u, hi_b, hi_c, lo_d, lo_u, lo_b, lo_c = (
            m.sem("s_" + t) for t in ("hid", "hiu", "hib", "hic", "lod", "lou", "lob", "loc"))
        d_ps, decayed, b_rep, b_copied, c_rep, c_copied, u_rep, fed, ahead_done, back_done, summed, low_done, \
            high_done, y_part, y_done = (m.sem("s_" + t) for t in (
                "dps", "decayed", "brepd", "bcop", "crepd", "ccop", "urep", "fed", "aheadd", "backd", "summed",
                "lowp", "highp", "ypart", "ydone"))
        aneg, a_on_vector, a_on_scalar = prepare_a(m, "s_", c, 2)
        LAG_B, LAG_D, LAG_A, LAG_C, LAG_Y = 3, 4, 5, 6, 7
        block = ctx.enter_context(nc.Block())

        def place(u):
            u %= UNROLL
            return u // 4, slice(u % 4 // 2 * N2, (u % 4 // 2 + 1) * N2), u % 2

        @block.tensor
        def _(pe):
            pe.wait_ge(ready, 3)

            def spread(bank, sel, parts, cols):
                for i in range(2):
                    for part in range(2):
                        mm = pe.matmul(bank[:, i * N2:(i + 1) * N2], selr[:, sel[i] * P:(sel[i] + 1) * P],
                                       parts[:, part, cols], start=(part == 0), stop=(part == 1))
                return mm

            def body(s, u):
                par = u // 4
                if u % 4 == 0 and live(s, STEPS):
                    wait(pe, lo_b, s)
                    pe.matmul(ps_in[:], c["wxp"][:, par * P:(par + 1) * P], x[:, ds((s - u) * (N // UNROLL), N)],
                              start=True, stop=True).then_inc(xp_ps, 4)
                if u % 4 == 1 and live(s, STEPS):
                    pe.wait_ge(xp_done, s + 3)
                    pe.wait_ge(skip_done, s + 3)
                    wait(pe, lo_c, s - 1)
                    pe.matmul(ps_dt[:], wdt[:], xp[:], start=True, stop=True).then_inc(dt_ps, 4)
                    pe.matmul(ps_in[:], c["wb"], xp[:], start=True, stop=True).then_inc(b_ps, 4)
                if u % 4 == 2 and live(s, STEPS):
                    pe.wait_ge(relu_done, s + 2)
                    pe.matmul(ps_dt[:], c["wc"], xp[:], start=True, stop=True).then_inc(c_ps, 4)
                p, v = s - LAG_D, u - LAG_D
                q, w = s - LAG_B, u - LAG_B
                r, z = s - LAG_A, u - LAG_A

                def decays(tp):
                    if live(p, STEPS):
                        par, cols, g = place(v)
                        if v % 4 == 0 and tp == 0:
                            pe.wait_ge(lo_d, p + 4)
                        wait(pe, decayed, 4 * p + tp - 1)
                        spread(ps_d[tp % 2], [2 * (2 * tp + i) + g for i in range(2)], parts_d[:, par], cols).then_inc(d_ps, 1)

                def states(tp):
                    if live(q, STEPS):
                        par, cols, second = place(w)
                        if w % 4 == second and tp == 0:
                            pe.wait_ge((lo_b, lo_c)[second], q - second + 4)
                        if tp:
                            pe.wait_ge((b_copied, c_copied)[second], 4 * (q - second) + 2 * tp)
                        elif second:
                            pe.wait_ge(b_copied, 4 * (q - 1) + 8)
                        else:
                            wait(pe, c_copied, 4 * q)
                        spread(ps_bc, [16 + 2 * tp + i for i in range(2)], (parts_b, parts_c)[second],
                               cols).then_inc((b_rep, c_rep)[second], 2)

                def inputs(tp):
                    if live(r, STEPS):
                        par, cols, g = place(z)
                        if z % 4 == 0 and tp == 0:
                            pe.wait_ge(lo_u, r + 4)
                        wait(pe, fed, 4 * r + tp - 1)
                        spread(ps_u[tp % 2], [2 * (2 * tp + i) + g for i in range(2)], parts_u[:, par], cols).then_inc(u_rep, 1)

                inputs(0)
                inputs(1)
                decays(0)
                states(0)
                decays(1)
                inputs(2)
                inputs(3)
                o = s - LAG_Y
                if live(o, STEPS):
                    _, cols, g = place(u - LAG_Y)
                    if (u - LAG_Y) % 4 == 0:
                        wait(pe, y_done, o)
                    pe.wait_ge(low_done, 2 * o + 2)
                    pe.wait_ge(high_done, 2 * o + 2)
                    for odd in range(2):
                        for quad in range(4):
                            t = 2 * quad + odd
                            src = low_prod[:, t] if t < TOK // 2 else high_prod[:, (u - LAG_Y) % 2, t - TOK // 2]
                            mm = pe.matmul(ps_y[quad * 32:(quad + 1) * 32, cols],
                                           ysel[:, (2 * odd + g) * 32:(2 * odd + g + 1) * 32],
                                           src, start=(odd == 0 and g == 0),
                                           stop=(odd == 1 and g == 1), tile_position=(0, quad * 32))
                    mm.then_inc(y_part, 1)
                states(1)
                for tp in range(2, 4):
                    decays(tp)
                    states(tp)

            skewed(pe, STEPS, UNROLL, PEEL, body)

        @block.scalar
        def _(act):
            act.preload_act_table_set("natural_log_exp_and_others")
            a_on_scalar(act)
            act.wait_ge(ready, 3)
            act.wait_ge(zeroed, 3)

            def body(s, u):
                par, gi = u // 4, s - u % 4
                if u % 4 == 0 and live(s, STEPS):
                    act.wait_ge(xp_ps, gi + 4)
                    wait(act, c_ps, gi)
                    wait(act, du_done, gi)
                    act.activation(xp[:], ps_in[:], ACT.Copy).then_inc(xp_done, 4)
                    act.activation(y[:, par, ds((s - u) * (N // UNROLL), N)], ps_in[:], ACT.Copy,
                                   scale=dsk2[:, 0:1]).then_inc(skip_done, 4)
                if u % 4 == 1 and live(s, STEPS):
                    act.wait_ge(dt_ps, gi + 4)
                    wait(act, rest_done, gi)
                    act.activation(ex[:], ps_dt[:], ACT.Abs, bias=bdt2[:, 0:1]).then_inc(away_done, 4)
                    wait(act, delta_done, gi)
                    act.activation(relu[:], ps_dt[:], ACT.Relu, bias=bdt2[:, 0:1]).then_inc(relu_done, 4)
                    act.wait_ge(away_done, gi + 4)
                    act.activation(ex[:], ex[:], ACT.Exp, scale=-1.0).then_inc(ex_done, 4)
                if u % 4 == 2 and live(s, STEPS):
                    act.wait_ge(one_done, gi + 4)
                    act.wait_ge(lost_done, gi + 4)
                    act.activation(one[:], one[:], ACT.Ln).then_inc(ln_done, 4)
                if u % 4 == 3 and live(s, STEPS):
                    act.wait_ge(delta_done, gi + 4)
                    wait(act, d_ps, 4 * (gi - 4))
                    act.activation(parts_d[:, par, 0], delta[:], ACT.Copy).then_inc(hi_d, 4)
                if u % 4 == 0 and live(s - 4, STEPS):
                    act.wait_ge(du_done, s)
                    wait(act, u_rep, 4 * (s - 7))
                    act.activation(parts_u[:, 1 - par, 0], du[:], ACT.Copy).then_inc(hi_u, 4)
                p, v = s - LAG_D, u - LAG_D
                q, w = s - LAG_B, u - LAG_B
                for tp in range(4):
                    if live(p, STEPS):
                        b, g = v % 2, place(v)[2]
                        wait(act, back_done, p - 1)
                        act.wait_ge(d_ps, 4 * p + tp + 1)
                        act.activation(decay[:, b, :, 2 * tp:2 * tp + 2].rearrange("p n t -> p t n"),
                                       ps_d[tp % 2][:].rearrange("p (t n) -> p t n", t=2), ACT.Exp,
                                       scale=aneg[:, g:g + 1]).then_inc(decayed, 1)
                    if live(q, STEPS):
                        second, blk = place(w)[2], w % 4 // 2
                        act.wait_ge((b_rep, c_rep)[second], 4 * (q - second) + 2 * tp + 2)
                        if second == 0:
                            wait(act, fed, 4 * (q - 3) + tp + 1)
                        elif tp < 2:
                            wait(act, low_done, 2 * (q - 4) + tp + 1)
                        else:
                            wait(act, high_done, 2 * (q - 4) + tp - 1)
                        act.activation((bs, cs)[second][:, blk, 2 * tp:2 * tp + 2].rearrange("p t n -> p (t n)"),
                                       ps_bc[:], ACT.Copy).then_inc((b_copied, c_copied)[second], 2)
                if u % 4 == 1 and live(s, STEPS):
                    act.wait_ge(b_ps, gi + 4)
                    wait(act, b_rep, 4 * gi)
                    act.activation(parts_b[:, 0], ps_in[:], ACT.Copy).then_inc(hi_b, 4)
                if u % 4 == 2 and live(s, STEPS):
                    act.wait_ge(c_ps, gi + 4)
                    wait(act, c_rep, 4 * gi)
                    act.activation(parts_c[:, 0], ps_dt[:], ACT.Copy).then_inc(hi_c, 4)

            skewed(act, STEPS, UNROLL, PEEL, body)

        @block.vector
        def _(dve):
            dve.wait_ge(const_in, 16)
            dve.tensor_scalar(wdt[:], c["wdt"], c["wx0"], None, ALU.mult).then_inc(ready, 1)
            dve.tensor_scalar(bdt2[:], c["bdt"], 2.0, None, ALU.mult).then_inc(ready, 1)
            dve.tensor_scalar(dsk2[:], c["dsk"], 2.0, None, ALU.mult).then_inc(ready, 1)
            a_on_vector(dve)
            dve.wait_ge(zeroed, 3)

            def body(s, u):
                p, v = s - LAG_A, u - LAG_A
                if live(p, STEPS):
                    b, g, blk = v % 2, place(v)[2], v % 4 // 2
                    for tp in range(4):
                        dve.wait_ge(u_rep, 4 * p + tp + 1)
                        if g == 0:
                            dve.wait_ge(b_copied, 4 * p + 2 * tp + 2)
                        wait(dve, back_done, p)
                        dve.tensor_tensor(feed[:, :, 2 * tp:2 * tp + 2].rearrange("p n t -> p t n"),
                                          ps_u[tp % 2][:].rearrange("p (t n) -> p t n", t=2),
                                          bs[:, blk, 2 * tp:2 * tp + 2], ALU.mult).then_inc(fed, 1)
                c_step, w = s - LAG_C, u - LAG_C
                if live(c_step, STEPS):
                    wait(dve, y_part, c_step)
                    dve.wait_ge(summed, 2 * c_step + 1)
                    for tp in range(2):
                        if place(w)[2] == 0:
                            dve.wait_ge(c_copied, 4 * c_step + 2 * tp + 2)
                        dve.tensor_tensor(low_prod[:, 2 * tp:2 * tp + 2], cs[:, w % 4 // 2, 2 * tp:2 * tp + 2],
                                          ahead[:, w % 2, :, 2 * tp:2 * tp + 2].rearrange("p n t -> p t n"),
                                          ALU.mult).then_inc(low_done, 1)
                if live(p, STEPS):
                    dve.wait_ge(decayed, 4 * p + 4)
                    dve.wait_ge(fed, 4 * p + 4)
                    a, f = (t.rearrange("p n t -> p (n t)") for t in (decay[:, b], feed[:]))
                    wait(dve, low_done, 2 * (p - 1))
                    wait(dve, high_done, 2 * (p - 1))
                    dve.tensor_tensor_scan(ahead[:, b].rearrange("p n t -> p (n t)"), a, f, 0.0, ALU.mult,
                                           ALU.add).then_inc(ahead_done, 1)
                    wait(dve, summed, 2 * (p - 1))
                    dve.tensor_tensor_scan(back[:, b].rearrange("p n t -> p (n t)")[:, ::-1], a[:, ::-1], f[:, ::-1],
                                           0.0, ALU.mult, ALU.add).then_inc(back_done, 1)
                p = s - LAG_Y
                if (u - LAG_Y) % 4 == 3 and live(p, STEPS):
                    half = place(u - LAG_Y)[0]
                    dve.wait_ge(y_part, p + 1)
                    dve.wait_ge(skip_done, p + 1)
                    cols = ds((p - (u - LAG_Y) % UNROLL) * (N // UNROLL), N)
                    dve.tensor_tensor(y[:, half, cols], ps_y[:], y[:, half, cols], ALU.add).then_inc(y_done, 4)
                if not live(s, STEPS):
                    return
                par, gi = u // 4, s - u % 4
                if u % 4 == 1:
                    dve.wait_ge(ex_done, gi + 4)
                    wait(dve, delta_done, gi)
                    dve.tensor_scalar(one[:], ex[:], 1.0, None, ALU.add).then_inc(one_done, 4)
                    dve.wait_ge(one_done, gi + 4)
                    dve.scalar_tensor_tensor(out=ex[:], in0=one[:], scalar=-1.0, in1=ex[:], op0=ALU.add,
                                             op1=ALU.subtract).then_inc(lost_done, 4)
                    dve.wait_ge(hi_b, gi + 4)
                    wait(dve, b_rep, 4 * gi)
                    dve.tensor_tensor(parts_b[:, 1], ps_in[:], parts_b[:, 0].bitcast(F32),
                                      ALU.subtract).then_inc(lo_b, 4)
                if u % 4 == 2:
                    dve.wait_ge(hi_c, gi + 4)
                    wait(dve, c_rep, 4 * gi)
                    dve.tensor_tensor(parts_c[:, 1], ps_dt[:], parts_c[:, 0].bitcast(F32),
                                      ALU.subtract).then_inc(lo_c, 4)

            skewed(dve, STEPS, UNROLL, PEEL, body)

        @block.gpsimd
        def _(pool):
            for t in (decay[:, 0], decay[:, 1], feed[:]):
                pool.memset(t, 0.0).then_inc(zeroed, 1)

            def body(s, u):
                par, gi = u // 4, s - u % 4
                if u % 4 == 2 and live(s, STEPS):
                    pool.wait_ge(ln_done, gi + 4)
                    pool.wait_ge(lost_done, gi + 4)
                    pool.tensor_tensor(one[:], one[:], ex[:], ALU.subtract).then_inc(rest_done, 4)
                    pool.wait_ge(rest_done, gi + 4)
                    pool.wait_ge(relu_done, gi + 4)
                    wait(pool, hi_d, gi)
                    wait(pool, lo_d, gi)
                    pool.tensor_tensor(delta[:], relu[:], one[:], ALU.add).then_inc(delta_done, 4)
                if u % 4 == 3 and live(s, STEPS):
                    pool.wait_ge(delta_done, gi + 4)
                    wait(pool, hi_u, gi)
                    wait(pool, lo_u, gi)
                    pool.wait_ge(xp_done, gi + 4)
                    pool.tensor_tensor(du[:], delta[:], xp[:], ALU.mult).then_inc(du_done, 4)
                    pool.wait_ge(hi_d, gi + 4)
                    wait(pool, d_ps, 4 * (gi - 4))
                    pool.tensor_tensor(parts_d[:, par, 1], delta[:], parts_d[:, par, 0].bitcast(F32),
                                       ALU.subtract).then_inc(lo_d, 4)
                if u % 4 == 0 and live(s - 4, STEPS):
                    pool.wait_ge(hi_u, s)
                    wait(pool, u_rep, 4 * (s - 7))
                    pool.tensor_tensor(parts_u[:, 1 - par, 1], du[:], parts_u[:, 1 - par, 0].bitcast(F32),
                                       ALU.subtract).then_inc(lo_u, 4)
                p, v = s - LAG_A, u - LAG_A
                if live(p, STEPS):
                    b = v % 2
                    pool.wait_ge(ahead_done, p + 1)
                    pool.wait_ge(back_done, p + 1)
                    for part in range(2):
                        toks = slice(part * TOK // 2, (part + 1) * TOK // 2)
                        pool.tensor_tensor(ahead[:, b, :, toks], ahead[:, b, :, toks], back[:, b, :, toks],
                                           ALU.add).then_inc(summed, 1)
                    pool.wait_ge(summed, 2 * p + 2)
                    wait(pool, y_part, p - 1)
                    for tp in range(2, 4):
                        if place(v)[2] == 0:
                            pool.wait_ge(c_copied, 4 * p + 2 * tp + 2)
                        pool.tensor_tensor(high_prod[:, b, 2 * tp - 4:2 * tp - 2],
                                           cs[:, v % 4 // 2, 2 * tp:2 * tp + 2],
                                           ahead[:, b, :, 2 * tp:2 * tp + 2].rearrange("p n t -> p t n"),
                                           ALU.mult).then_inc(high_done, 1)

            skewed(pool, STEPS, UNROLL, PEEL, body)


def gated(nc, consts, tag, group, src, y, func, dst, sums=None):
    with ExitStack() as ctx:
        m = Scope(nc, ctx)
        c, const_in = consts[group]
        gate, gated_y = m.sb(tag + "gate", [P, 2, N]), m.sb(tag + "gy", [P, 2, HALVES, N])
        ps_z, ps_o = m.banks(tag + "psz", 3), m.banks(tag + "pso", 2)
        z_done, gate_done, gy_done, o_done, dst_done = (
            m.sem(tag + t) for t in ("zd", "gated", "gyd", "od", "dstd"))
        block = ctx.enter_context(nc.Block())
        units = [(n, h) for n in range(CHUNKS) for h in range(HALVES)]

        @block.tensor
        def _(pe):
            pe.wait_ge(const_in, 16)
            for k in range(len(units) + 2):
                if k < len(units):
                    n, h = units[k]
                    wait(pe, gate_done, k - 2)
                    pe.matmul(ps_z[k % 3][:], c["wz"][:, h * P:(h + 1) * P], src[:, n * N:(n + 1) * N], start=True,
                              stop=True).then_inc(z_done, 1)
                if k >= 2 and k % 2 == 1:
                    n = k // 2 - 1
                    pe.wait_ge(gy_done, k - 1)
                    wait(pe, dst_done, n - 1)
                    for h in range(HALVES):
                        mm = pe.matmul(ps_o[n % 2][h * C:(h + 1) * C], c["wo"], gated_y[:, n % 2, h], start=True,
                                       stop=True, tile_position=(0, h * C))
                    mm.then_inc(o_done, 1)

        @block.scalar
        def _(act):
            for k in range(len(units)):
                act.wait_ge(z_done, k + 1)
                wait(act, gy_done, k - 1)
                act.activation(gate[:, k % 2], ps_z[k % 3][:], func).then_inc(gate_done, 1)

        @block.vector
        def _(dve):
            dve.wait_ge(const_in, 16)

            def finish(n):
                dve.wait_ge(o_done, n + 1)
                cols = slice(n * N, (n + 1) * N)
                if sums is None:
                    dve.scalar_tensor_tensor(out=dst[:, cols], in0=src[:, cols], scalar=c["skip"],
                                             in1=ps_o[n % 2][:], op0=ALU.mult, op1=ALU.add).then_inc(dst_done, 1)
                else:
                    dve.tensor_scalar(dst[:, cols], ps_o[n % 2][:], 1.0, 0.0, ALU.mult, ALU.add,
                                      accum_out=sums[:, n:n + 1]).then_inc(dst_done, 1)

            for k, (n, h) in enumerate(units):
                dve.wait_ge(gate_done, k + 1)
                wait(dve, o_done, n - 1)
                dve.tensor_tensor(gated_y[:, n % 2, h], y[:, h, n * N:(n + 1) * N], gate[:, k % 2],
                                  ALU.mult).then_inc(gy_done, 1)
                if h == 1 and n >= 1:
                    finish(n - 1)
            finish(CHUNKS - 1)


def groupnorm(nc, consts, src, sums, x):
    with ExitStack() as ctx:
        m = Scope(nc, ctx)
        c, const_in = consts["l2post"]
        spread, total, scaled = m.sb("g_spread", [P, HW]), m.sb("g_total", [P, BL]), m.sb("g_scaled", [P, 2, HW])
        means, square, lnv, rstd, gain, shift, offset = (m.sb("g_" + t, [P, BL]) for t in (
            "means", "square", "lnv", "rstd", "gain", "shift", "offset"))
        ps_m, ps_v = m.banks("g_psm", 1, (P, BL))[0], m.banks("g_psv", 1, (P, BL))[0]
        total_done, mean_ps, mean_done, square_done, var_ps, logged, rstd_done, gain_done, shift_done, \
            offset_done, scaled_done, x_done = (m.sem("g_" + t) for t in (
                "totald", "meanps", "meand", "squared", "varps", "logged", "rstdd", "gaind", "shiftd",
                "offsetd", "scaledd", "xd"))
        block = ctx.enter_context(nc.Block())

        @block.tensor
        def _(pe):
            pe.wait_ge(const_in, 16)
            pe.wait_ge(total_done, 1)
            pe.matmul(ps_m[:], c["gavg"], total[:], start=True, stop=True).then_inc(mean_ps, 1)
            pe.wait_ge(square_done, BL)
            pe.matmul(ps_v[:], c["gavg"], square[:], start=True, stop=True).then_inc(var_ps, 1)

        @block.scalar
        def _(act):
            act.preload_act_table_set("natural_log_exp_and_others")
            act.wait_ge(mean_done, 1)
            for bl in range(BL):
                wait(act, square_done, bl)
                act.activation(spread[:], src[:, bl * HW:(bl + 1) * HW], ACT.Square, bias=means[:, bl:bl + 1],
                               accum_out=square[:, bl:bl + 1]).then_inc(square_done, 1)
            act.wait_ge(var_ps, 1)
            act.activation(lnv[:], ps_v[:], ACT.Ln, scale=1.0 / HW, bias=LN_EPS).then_inc(logged, 1)
            act.wait_ge(logged, 1)
            act.activation(rstd[:], lnv[:], ACT.Exp, scale=-0.5).then_inc(rstd_done, 1)
            act.wait_ge(gain_done, 1)
            act.wait_ge(offset_done, 1)
            for bl in range(BL):
                wait(act, x_done, bl - 1)
                act.activation(scaled[:, bl % 2], src[:, bl * HW:(bl + 1) * HW], ACT.Identity,
                               scale=gain[:, bl:bl + 1], bias=offset[:, bl:bl + 1]).then_inc(scaled_done, 1)

        @block.vector
        def _(dve):
            pairs = sums.rearrange("p (b k) -> p k b", k=HW // N)
            dve.tensor_tensor(total[:], pairs[:, 0], pairs[:, 1], ALU.add).then_inc(total_done, 1)
            dve.wait_ge(mean_ps, 1)
            dve.tensor_scalar(means[:], ps_m[:], -1.0 / HW, None, ALU.mult).then_inc(mean_done, 1)
            dve.wait_ge(const_in, 16)
            dve.wait_ge(rstd_done, 1)
            dve.tensor_scalar(gain[:], rstd[:], c["gnw"], None, ALU.mult).then_inc(gain_done, 1)
            dve.wait_ge(mean_done, 1)
            dve.wait_ge(gain_done, 1)
            dve.tensor_tensor(shift[:], means[:], gain[:], ALU.mult).then_inc(shift_done, 1)
            dve.wait_ge(shift_done, 1)
            dve.tensor_scalar(offset[:], shift[:], c["gnb"], None, ALU.add).then_inc(offset_done, 1)
            for bl in range(BL):
                dve.wait_ge(scaled_done, bl + 1)
                cols = slice(bl * HW, (bl + 1) * HW)
                dve.tensor_tensor(x[:, cols], x[:, cols], scaled[:, bl % 2], ALU.add).then_inc(x_done, 1)


def convolve3(nc, consts, xn, xc):
    with ExitStack() as ctx:
        m = Scope(nc, ctx)
        c, const_in = consts["l3conv"]
        taps = 4
        folded = m.sb("c_folded", [P, taps, HALVES, P])
        banks = m.banks("c_ps", 4)
        folded_done, conv_done, silu_done = (m.sem("c_" + t) for t in ("foldedd", "convd", "silud"))
        block = ctx.enter_context(nc.Block())

        @block.vector
        def _(dve):
            dve.wait_ge(const_in, 16)
            for k in range(taps):
                for h in range(HALVES):
                    dve.tensor_tensor(folded[:, k, h], c["wxi"][:, h * P:(h + 1) * P],
                                      c["convw"][:, k * P:(k + 1) * P], ALU.mult).then_inc(folded_done, 1)

        @block.tensor
        def _(pe):
            pe.wait_ge(folded_done, taps * HALVES)
            for u in range(HALVES * CHUNKS):
                h, n = divmod(u, CHUNKS)
                wait(pe, silu_done, u - 3)
                for back in range(taps):
                    lost = back if n * N % HW == 0 else 0
                    mm = pe.matmul(banks[u % 4][:, lost:N], folded[:, taps - 1 - back, h],
                                   xn[:, n * N + lost - back:(n + 1) * N - back], start=(back == 0),
                                   stop=(back == taps - 1))
                mm.then_inc(conv_done, 1)

        @block.scalar
        def _(act):
            act.wait_ge(const_in, 16)
            for u in range(HALVES * CHUNKS):
                h, n = divmod(u, CHUNKS)
                act.wait_ge(conv_done, u + 1)
                act.activation(xc[:, h, n * N:(n + 1) * N], banks[u % 4][:], ACT.Silu,
                               bias=c["convb"]).then_inc(silu_done, 1)


def project3(nc, consts, src, x, out, resid):
    with ExitStack() as ctx:
        m = Scope(nc, ctx)
        c, const_in = consts["l3post"]
        banks = m.banks("j_ps", 3)
        proj_done, out_done, resid_done = (m.sem("j_" + t) for t in ("projd", "outd", "residd"))
        block = ctx.enter_context(nc.Block())

        @block.tensor
        def _(pe):
            pe.wait_ge(const_in, 16)
            for n in range(CHUNKS):
                wait(pe, out_done, n - 2)
                pe.matmul(banks[n % 3][:], c["wpj"], src[:, n * N:(n + 1) * N], start=True,
                          stop=True).then_inc(proj_done, 1)

        @block.vector
        def _(dve):
            dve.wait_ge(const_in, 16)
            for n in range(CHUNKS):
                cols = slice(n * N, (n + 1) * N)
                dve.wait_ge(proj_done, n + 1)
                dve.scalar_tensor_tensor(out=out[:, cols], in0=banks[n % 3][:], scalar=c["pjb"], in1=x[:, cols],
                                         op0=ALU.add, op1=ALU.add).then_inc(out_done, 1)

        @block.gpsimd
        def _(pool):
            for n in range(CHUNKS):
                cols = slice(n * N, (n + 1) * N)
                pool.wait_ge(out_done, n + 1)
                pool.tensor_tensor(resid[:, cols], out[:, cols], x[:, cols], ALU.add).then_inc(resid_done, 1)


def scan3(nc, consts, xc, selr, ysel):
    with ExitStack() as ctx:
        m = Scope(nc, ctx)
        c, const_in = consts["l3"]
        wdt = m.sb("r_wdtb", [P, P])
        delta, du, rest = m.sb("r_delta", [P, N]), m.sb("r_du", [P, N]), m.sb("r_rest", [P, N])
        relu, ex, one, ln, lost = (m.sb("r_" + t, [P, N]) for t in ("relu", "ex", "one", "ln", "lost"))
        parts = m.sb("r_parts", [P, 2, 3, 2, N], F32R)
        decay, feed = m.sb("r_decay", [P, 2, Q4, N]), m.sb("r_feed", [P, Q4, N])
        state, prod = m.sb("r_state", [P, 2, Q4, N]), m.sb("r_prod", [P, 2, Q4, N])
        carry = m.sb("r_carry", [P, Q4, Q4])
        bs, cs = m.sb("r_bs", [P, 2, Q4, N]), m.sb("r_cs", [P, 2, Q4, N])
        ps_bc, ps_dt, ps_y, ps_s = (m.banks("r_p" + t, 1)[0] for t in ("bc", "dt", "y", "s"))
        ps_d, ps_u = m.banks("r_pd", 2), m.banks("r_pu", 2)
        w_ps, w_done = (m.sem("r_" + t) for t in ("wps", "wd"))
        dt_ps, bc_ps, away_done, relu_done, ex_done, one_done, ln_done, lost_done, rest_done, delta_done, \
            du_done = (m.sem("r_" + t) for t in (
                "dtps", "bcps", "awayd", "relud", "exd", "oned", "lnd", "lostd", "restd", "deltad", "dud"))
        hi_d, hi_u, hi_bc, lo_d, lo_u, lo_bc = (m.sem("r_" + t) for t in ("hid", "hiu", "hibc", "lod", "lou", "lobc"))
        d_ps, decayed, u_rep, fed, scanned, multiplied, b_rep, c_rep, b_copied, c_copied, carried, y_part, y_done = (
            m.sem("r_" + t) for t in ("dps", "decayed", "urep", "fed", "scanned", "mult", "brepd", "crepd", "bcop",
                                      "ccop", "carried", "ypart", "ydone"))
        aneg, a_on_vector, a_on_scalar = prepare_a(m, "r_", c, 4)
        LAG_B, LAG_D, LAG_U, LAG_Y = 2, 5, 6, 7
        DT, DU, BC = range(3)
        block = ctx.enter_context(nc.Block())

        def columns(s, u):
            if isinstance(s, int):
                return slice(s // 4 * N, (s // 4 + 1) * N)
            return ds((s - u % UNROLL) * (N // 4) + u % UNROLL // 4 * N, N)

        @block.tensor
        def _(pe):
            pe.wait_ge(const_in, 16)
            pe.matmul(ps_dt[:, 0:P], c["xpr"][0:16], c["dtw"][0:16], start=True, stop=True).then_inc(w_ps, 1)
            pe.wait_ge(w_done, 1)

            def spread(bank, sel, which, par):
                for part in range(2):
                    mm = pe.matmul(bank[:], selr[:, sel * P:(sel + 1) * P], parts[:, par, which, part],
                                   start=(part == 0), stop=(part == 1))
                return mm

            def body(s, u):
                par = u // 4
                if u % 4 == 0 and live(s, STEPS):
                    cols = columns(s, u)
                    wait(pe, relu_done, s)
                    pe.matmul(ps_dt[:], wdt[:], xc[:, cols], start=True, stop=True).then_inc(dt_ps, 4)
                    wait(pe, lo_bc, s)
                    pe.matmul(ps_bc[:], c["wbc"], xc[:, cols], start=True, stop=True).then_inc(bc_ps, 4)

                def decays(qs):
                    p, v = s - LAG_D, u - LAG_D
                    if not live(p, STEPS):
                        return
                    for q in qs:
                        if v % 4 == 0 and q == 0:
                            pe.wait_ge(lo_d, p + 4)
                        wait(pe, decayed, 4 * p + q - 1)
                        spread(ps_d[q % 2], 4 * q + v % 4, DT, v % UNROLL // 4).then_inc(d_ps, 1)

                def states(which):
                    p, v = s - LAG_B, u - LAG_B
                    if not live(p, STEPS):
                        return
                    if which == 0:
                        if v % 4 == 0:
                            pe.wait_ge(lo_bc, p + 4)
                        wait(pe, c_copied, p)
                    else:
                        pe.wait_ge(b_copied, p + 1)
                    spread(ps_s, 16 + 2 * (v % 4) + which, BC, v % UNROLL // 4).then_inc((b_rep, c_rep)[which], 1)

                def inputs(qs):
                    p, v = s - LAG_U, u - LAG_U
                    if not live(p, STEPS):
                        return
                    for q in qs:
                        if v % 4 == 0 and q == 0:
                            pe.wait_ge(lo_u, p + 4)
                        wait(pe, fed, 4 * p + q - 1)
                        spread(ps_u[q % 2], 4 * q + v % 4, DU, v % UNROLL // 4).then_inc(u_rep, 1)

                inputs((0, 1))
                decays((0,))
                states(0)
                decays((1,))
                inputs((2, 3))
                states(1)
                decays((2, 3))
                p, v = s - LAG_Y, u - LAG_Y
                if live(p, STEPS):
                    if v % 4 == 0:
                        wait(pe, y_done, p)
                    pe.wait_ge(multiplied, 4 * p + 4)
                    for q in range(Q4):
                        mm = pe.matmul(ps_y[q * 32:(q + 1) * 32], ysel[:, v % 4 * 32:(v % 4 + 1) * 32],
                                       prod[:, v % 2, q], start=(v % 4 == 0), stop=(v % 4 == 3),
                                       tile_position=(0, q * 32))
                    mm.then_inc(y_part, 1)

            skewed(pe, STEPS, UNROLL, PEEL, body)

        @block.scalar
        def _(act):
            act.preload_act_table_set("natural_log_exp_and_others")
            act.wait_ge(const_in, 16)
            act.wait_ge(w_ps, 1)
            act.activation(wdt[:], ps_dt[:, 0:P], ACT.Copy).then_inc(w_done, 1)
            a_on_scalar(act)

            def body(s, u):
                par, gi = u // 4, s - u % 4
                if u % 4 == 0 and live(s, STEPS):
                    act.wait_ge(dt_ps, gi + 4)
                    wait(act, lost_done, gi)
                    act.activation(ex[:], ps_dt[:], ACT.Abs, bias=c["dtb"]).then_inc(away_done, 4)
                    wait(act, delta_done, gi)
                    act.activation(relu[:], ps_dt[:], ACT.Relu, bias=c["dtb"]).then_inc(relu_done, 4)
                    act.wait_ge(away_done, gi + 4)
                    act.activation(ex[:], ex[:], ACT.Exp, scale=-1.0).then_inc(ex_done, 4)
                if u % 4 == 1 and live(s, STEPS):
                    act.wait_ge(bc_ps, gi + 4)
                    wait(act, c_rep, gi - 4)
                    act.activation(parts[:, par, BC, 0], ps_bc[:], ACT.Copy).then_inc(hi_bc, 4)
                if u % 4 == 2 and live(s, STEPS):
                    act.wait_ge(one_done, gi + 4)
                    wait(act, rest_done, gi)
                    act.activation(ln[:], one[:], ACT.Ln).then_inc(ln_done, 4)
                if u % 4 == 3 and live(s, STEPS):
                    act.wait_ge(delta_done, gi + 4)
                    wait(act, d_ps, 4 * (gi - 4))
                    act.activation(parts[:, par, DT, 0], delta[:], ACT.Copy).then_inc(hi_d, 4)
                if u % 4 == 0 and live(s - 4, STEPS):
                    act.wait_ge(du_done, s)
                    wait(act, u_rep, 4 * (s - 7))
                    act.activation(parts[:, 1 - par, DU, 0], du[:], ACT.Copy).then_inc(hi_u, 4)
                def decays(qs):
                    p, v = s - LAG_D, u - LAG_D
                    if not live(p, STEPS):
                        return
                    for q in qs:
                        act.wait_ge(d_ps, 4 * p + q + 1)
                        wait(act, scanned, 4 * (p - 2) + q + 1)
                        act.activation(decay[:, v % 2, q], ps_d[q % 2][:], ACT.Exp,
                                       scale=aneg[:, v % 4:v % 4 + 1]).then_inc(decayed, 1)

                def states(which):
                    p, v = s - LAG_B, u - LAG_B
                    if not live(p, STEPS):
                        return
                    act.wait_ge((b_rep, c_rep)[which], p + 1)
                    wait(act, (fed, multiplied)[which], 4 * (p - 5) + v % 4 + 1)
                    act.activation((bs, cs)[which][:, v % UNROLL // 4, v % 4], ps_s[:],
                                   ACT.Copy).then_inc((b_copied, c_copied)[which], 1)

                decays((0,))
                states(0)
                decays((1,))
                states(1)
                decays((2, 3))

            skewed(act, STEPS, UNROLL, PEEL, body)

        @block.vector
        def _(dve):
            dve.wait_ge(const_in, 16)
            a_on_vector(dve)

            def body(s, u):
                p, v = s - LAG_U, u - LAG_U
                if live(p, STEPS):
                    b, g, lc = v % 2, v % 4, v % UNROLL // 4
                    for q in range(Q4):
                        dve.wait_ge(u_rep, 4 * p + q + 1)
                        if g == 0:
                            dve.wait_ge(b_copied, p + q + 1)
                        wait(dve, scanned, 4 * (p - 1) + q + 1)
                        dve.tensor_tensor(feed[:, q], ps_u[q % 2][:], bs[:, lc, q], ALU.mult).then_inc(fed, 1)
                    for q in range(Q4):
                        dve.wait_ge(decayed, 4 * p + q + 1)
                        dve.wait_ge(fed, 4 * p + q + 1)
                        wait(dve, multiplied, 4 * (p - 2) + q + 1)
                        if lc == 1:
                            dve.wait_ge(carried, p - 2 + g)
                            start = carry[:, g, q:q + 1]
                        else:
                            start = 0.0
                        dve.tensor_tensor_scan(state[:, b, q], decay[:, b, q], feed[:, q], start, ALU.mult,
                                               ALU.add).then_inc(scanned, 1)
                    if lc == 0:
                        dve.wait_ge(scanned, 4 * p + 4)
                        dve.tensor_copy(carry[:, g], state[:, b, :, N - 1]).then_inc(carried, 2)
                p, v = s - LAG_Y, u - LAG_Y
                if v % 4 == 3 and live(p, STEPS):
                    dve.wait_ge(y_part, p + 1)
                    cols = columns(p, v)
                    dve.wait_ge(du_done, p + 1)
                    dve.scalar_tensor_tensor(out=xc[:, cols], in0=xc[:, cols], scalar=c["dp"], in1=ps_y[:],
                                             op0=ALU.mult, op1=ALU.add).then_inc(y_done, 4)
                if u % 4 == 0 and live(s - 4, STEPS):
                    dve.wait_ge(hi_u, s)
                    wait(dve, u_rep, 4 * (s - 7))
                    dve.tensor_tensor(parts[:, 1 - u // 4, DU, 1], du[:], parts[:, 1 - u // 4, DU, 0].bitcast(F32),
                                      ALU.subtract).then_inc(lo_u, 4)
                if not live(s, STEPS):
                    return
                par, gi = u // 4, s - u % 4
                if u % 4 == 1:
                    dve.wait_ge(ex_done, gi + 4)
                    wait(dve, ln_done, gi)
                    dve.tensor_scalar(one[:], ex[:], 1.0, None, ALU.add).then_inc(one_done, 4)
                    dve.wait_ge(one_done, gi + 4)
                    wait(dve, rest_done, gi)
                    dve.scalar_tensor_tensor(out=lost[:], in0=one[:], scalar=-1.0, in1=ex[:], op0=ALU.add,
                                             op1=ALU.subtract).then_inc(lost_done, 4)
                    dve.wait_ge(hi_bc, gi + 4)
                    wait(dve, c_rep, gi - 4)
                    dve.tensor_tensor(parts[:, par, BC, 1], ps_bc[:], parts[:, par, BC, 0].bitcast(F32),
                                      ALU.subtract).then_inc(lo_bc, 4)
                if u % 4 == 3:
                    dve.wait_ge(hi_d, gi + 4)
                    wait(dve, d_ps, 4 * (gi - 4))
                    dve.tensor_tensor(parts[:, par, DT, 1], delta[:], parts[:, par, DT, 0].bitcast(F32),
                                       ALU.subtract).then_inc(lo_d, 4)

            skewed(dve, STEPS, UNROLL, PEEL, body)

        @block.gpsimd
        def _(pool):
            def body(s, u):
                par, gi = u // 4, s - u % 4
                if u % 4 == 2 and live(s, STEPS):
                    pool.wait_ge(ln_done, gi + 4)
                    pool.wait_ge(lost_done, gi + 4)
                    pool.tensor_tensor(rest[:], ln[:], lost[:], ALU.subtract).then_inc(rest_done, 4)
                    pool.wait_ge(rest_done, gi + 4)
                    pool.wait_ge(relu_done, gi + 4)
                    wait(pool, hi_d, gi)
                    wait(pool, lo_d, gi)
                    pool.tensor_tensor(delta[:], relu[:], rest[:], ALU.add).then_inc(delta_done, 4)
                if u % 4 == 3 and live(s, STEPS):
                    pool.wait_ge(delta_done, gi + 4)
                    wait(pool, hi_u, gi)
                    wait(pool, lo_u, gi)
                    pool.tensor_tensor(du[:], delta[:], xc[:, columns(gi, u - u % 4)], ALU.mult).then_inc(du_done, 4)
                p, v = s - LAG_U, u - LAG_U
                if live(p, STEPS):
                    wait(pool, y_part, p - 1)
                    for q in range(Q4):
                        pool.wait_ge(scanned, 4 * p + q + 1)
                        if v % 4 == 0:
                            pool.wait_ge(c_copied, p + q + 1)
                        pool.tensor_tensor(prod[:, v % 2, q], state[:, v % 2, q], cs[:, v % UNROLL // 4, q],
                                           ALU.mult).then_inc(multiplied, 1)

            skewed(pool, STEPS, UNROLL, PEEL, body)


def load(nc, dram, x):
    x_in = nc.alloc_semaphore(name="x_in")
    with nc.Block() as block:
        @block.sync
        def _(sp):
            for h in range(HALVES):
                sp.dma_start(x[h * C:(h + 1) * C].rearrange("c (b n) -> c b n", b=BL),
                             dram["x"][h * BL:(h + 1) * BL].rearrange("b c n -> c b n")).then_inc(x_in, 16)
            sp.wait_ge(x_in, 16 * HALVES)


def program(nc, dram, out):
    with ExitStack() as kept:
        m = Scope(nc, kept)
        x, y = m.sb("x_act", [P, COLS]), m.sb("y_inner", [P, HALVES, COLS])
        selr, ysel = m.sb("selr", [P, 24 * P], F32R), m.sb("ysel", [P, 4 * 32])
        with ExitStack() as scan_consts:
            consts = fetch(nc, scan_consts, dram, ["l2"])
            with ExitStack() as first_consts:
                consts |= fetch(nc, first_consts, dram, ["ln", "attn", "mlp0", "fir", "scan"])
                with nc.cleanup_on_exit(), ExitStack() as layer:
                    xn = Scope(nc, layer).sb("x_norm0", [P, COLS])
                    load(nc, dram, x)
                    layernorm(nc, consts, "n1", x, xn, "ln1_scale", "ln1_bias")
                    attention(nc, consts, dram, xn, x)
                    layernorm(nc, consts, "n2", x, xn, "ln2_scale", "ln2_bias")
                    mlp(nc, consts, "m0", "mlp0", xn, x, x)
                with nc.cleanup_on_exit():
                    antialiased(nc, consts, dram, x)
                    selectors(nc, consts, selr, ysel)
            with nc.cleanup_on_exit():
                scan2(nc, consts, x, y, selr, ysel)
        xn = m.sb("x_norm3", [P, COLS])
        with ExitStack() as scan_consts:
            consts = fetch(nc, scan_consts, dram, ["l3"])
            with ExitStack() as first_consts:
                consts |= fetch(nc, first_consts, dram, ["l2post", "ln", "l3conv"], "3")
                with nc.cleanup_on_exit(), ExitStack() as layer:
                    mem = Scope(nc, layer)
                    mixed, sums = mem.sb("mixed2", [P, COLS]), mem.sb("chunk_sums", [P, CHUNKS])
                    gated(nc, consts, "o2", "l2post", x, y, ACT.Gelu, mixed, sums)
                    groupnorm(nc, consts, mixed, sums, x)
                layernorm(nc, consts, "n3", x, xn, "lnw", "lnb")
                convolve3(nc, consts, xn, y)
            scan3(nc, consts, y[:].rearrange("p h n -> p (h n)"), selr, ysel)
        mixed = m.sb("mixed3", [P, COLS])
        consts = fetch(nc, kept, dram, ["l3post", "ln", "mlp3"], "4")
        gated(nc, consts, "o3", "l3post", xn, y, ACT.Silu, mixed)
        layernorm(nc, consts, "n4", mixed, xn, "lnw", "lnb")
        project3(nc, consts, xn, x, mixed, x)
        mlp(nc, consts, "m3", "mlp3", mixed, x, x, out)


def kernel(**inputs):
    import concourse.bacc as _bacc
    from concourse import mybir as _mybir
    from concourse.bass_utils import run_bass_kernel_spmd as _run

    host = {k: np.asarray(v) for k, v in inputs.items()}
    data = pack(host)
    data["x"] = host["x"].reshape(B, C, HW)
    data["rel"] = host["L0_conv_rel_bias_table"].reshape(1, -1)
    nc = _bacc.Bacc("TRN2", target_bir_lowering=False, num_devices=1)
    arrays, dram = {}, {}
    for name, a in data.items():
        a = np.ascontiguousarray(a)
        arrays[f"in_{name}_dram"] = a
        dram[name] = nc.dram_tensor(f"in_{name}_dram", a.shape, _mybir.dt.from_np(a.dtype),
                                    kind="ExternalInput").ap()
    out = nc.dram_tensor("out_0_dram", (B, C, HW), F32, kind="ExternalOutput").ap()
    program(nc, dram, out)
    r = _run(nc, [arrays], core_ids=[0])
    return r.results[0]["out_0_dram"].reshape(B, C, H, W)
```

```python
from contextlib import ExitStack

import numpy as np

import concourse.bass as bass
from concourse import mybir

F32 = mybir.dt.float32
F32R = mybir.dt.float32r
ALU = mybir.AluOpType
ACT = mybir.ActivationFunctionType
AX = mybir.AxisListType
ds = bass.ds

B, C, H, W = 8, 64, 32, 32
P = 128
HALVES = P // C
BL = B // HALVES
HW = H * W
COLS = BL * HW
N = 512
CHUNKS = COLS // N
WS = 8
HEADS = 8
HD = C // HEADS
WIN = WS * WS
PAIRS = COLS // WIN
ROWCOLS = WS * W
WROW = W // WS
HPAIRS = HEADS // 2
REL = 2 * WS - 1
LN_EPS = 1e-5
DEEP = 4
TAPS = 12
PITCH = 80
RB = 4
TILES = H // RB
KM = 12
BLK = 2 * RB * PITCH // P
UPB = BLK * (TILES - 1) + KM
GAIN = float(np.sqrt(2.0))
SLOPE = 0.2
CLAMP = 256.0
NS = 16
TOK = 8
GCN = C // TOK
DIN = 2 * GCN
SLOT = TOK + 1
N2 = 256
DM = C // 4
DI = 2 * DM
Q4 = 4
AMAX = 88.0


def wait(eng, sem, value):
    if isinstance(value, int) and value <= 0:
        return
    eng.wait_ge(sem, value)


def live(p, n):
    return not isinstance(p, int) or 0 <= p < n


def skewed(eng, n, unroll, peel, body):
    for s in range(peel):
        body(s, s % unroll)
    with eng.Fori(0, (n - peel) // unroll) as r:
        for u in range(unroll):
            body(r * unroll + (peel + u), u)
    for s in range(n, n + peel):
        body(s, s % unroll)


def layout(groups):
    at, out = 0, {}
    for name, width in groups:
        out[name] = (at, at + width)
        at += width
    return out, at


CONST = {
    "ln": [("center", P), ("mean", P), ("ln1_scale", 1), ("ln1_bias", 1), ("ln2_scale", 1), ("ln2_bias", 1),
           ("lnw", 1), ("lnb", 1)],
    "attn": [("wq", P), ("wk", P), ("wv", P), ("wp", P), ("ident", P), ("kmask", HEADS), ("vmask", 2 * 32),
             ("bq", 1), ("bk", 1), ("bv", 1), ("bp", 1)],
    "mlp0": [("w1", 2 * P), ("w2", 2 * C), ("b1", 2), ("b2", 1), ("l1b", 1)],
    "fir": [("ident", P), ("up", KM * P), ("down", KM * P)],
    "scan": [("sel", 16 * P), ("seln", 8 * P), ("ysel", 4 * 32)],
    "l2": [("wxp", 2 * P), ("wdt", P), ("wx0", 1), ("wb", P), ("wc", P), ("bdt", 1), ("alog", 2), ("dsk", 1)],
    "l2post": [("wz", 2 * P), ("wo", C), ("gavg", P), ("gnw", 1), ("gnb", 1)],
    "l3conv": [("wxi", P), ("convw", 4 * P), ("convb", 1)],
    "l3": [("xpr", P), ("dtw", P), ("wbc", P), ("dtb", 1),
           ("alog", 4), ("dp", 1)],
    "l3post": [("wz", 2 * P), ("wo", C), ("skip", 1), ("wpj", P), ("pjb", 1)],
    "mlp3": [("w1", 2 * P), ("w2", 2 * C), ("b1", 2), ("b2", 1), ("l1b", 1)],
}


def blocks(n, m):
    r, c = m.shape
    out = np.zeros((n, r, n, c), np.float32)
    for i in range(n):
        out[i, :, i, :] = m
    return out.reshape(n * r, n * c)


def halves(m):
    out = np.zeros((HALVES, P, P), np.float32)
    for h in range(HALVES):
        out[h, h * C:(h + 1) * C, :] = m
    return out.transpose(1, 0, 2).reshape(P, HALVES * P)


def mlp_pack(w1, b1, w2, b2, l1b):
    return {"w1": np.tile(w1, (2, 1)), "w2": w2.reshape(2, P, C).transpose(1, 0, 2).reshape(P, -1),
            "b1": b1.reshape(2, P).T, "b2": np.tile(b2, 2)[:, None], "l1b": np.tile(l1b, 2)[:, None]}


def pack(i):
    def two(v):
        return np.tile(np.asarray(v), 2)[:, None]

    def rep(v, n):
        return np.tile(np.asarray(v), n)[:, None]

    eye = np.eye(P, dtype=np.float32)
    wqkv, bqkv = i["L0_conv_w_qkv"], i["L0_conv_b_qkv"]
    part = np.arange(P)
    kmask = ((part % C)[:, None] // HD == np.arange(HEADS)).astype(np.float32)
    c32 = np.arange(32)
    vmask = (c32[None, None, :] // HD == 2 * np.arange(2)[None, :, None] + (part // C)[:, None, None])
    v = {}
    v["ln"] = {"center": eye - blocks(2, np.full((C, C), 1.0 / C, np.float32)),
               "mean": blocks(2, np.full((C, C), 1.0 / C, np.float32)),
               "ln1_scale": two(i["L0_conv_ln1_scale"]), "ln1_bias": two(i["L0_conv_ln1_bias"]),
               "ln2_scale": two(i["L0_conv_ln2_scale"]), "ln2_bias": two(i["L0_conv_ln2_bias"]),
               "lnw": two(i["L3_conv_ln_w"]), "lnb": two(i["L3_conv_ln_b"])}
    v["attn"] = {"wq": blocks(2, wqkv[:, :C]), "wk": blocks(2, wqkv[:, C:2 * C]), "wv": blocks(2, wqkv[:, 2 * C:]),
                 "wp": blocks(2, i["L0_conv_w_proj"]), "ident": eye, "kmask": kmask,
                 "vmask": vmask.astype(np.float32).reshape(P, -1), "bq": two(bqkv[:C]), "bk": two(bqkv[C:2 * C]),
                 "bv": two(bqkv[2 * C:]), "bp": two(i["L0_conv_b_proj"])}
    v["mlp0"] = mlp_pack(i["L0_conv_w_mlp1"], i["L0_conv_b_mlp1"], i["L0_conv_w_mlp2"], i["L0_conv_b_mlp2"],
                         i["L1_conv_bias"])
    v["fir"] = {"ident": eye}
    d8n = np.arange(P)
    sel = np.zeros((P, 16, P), np.float32)
    seln = np.zeros((P, 8, P), np.float32)
    ysel = np.zeros((P, 4, 32), np.float32)
    for k in range(16):
        sel[8 * k + d8n // NS, k, d8n] = 1.0
    for t in range(8):
        seln[NS * t + d8n % NS, t, d8n] = 1.0
    for j in range(4):
        ysel[d8n, j, 8 * j + d8n // NS] = 1.0
    v["scan"] = {"sel": sel.reshape(P, -1), "seln": seln.reshape(P, -1), "ysel": ysel.reshape(P, -1)}
    wi, wx, wdt = i["L2_conv_W_in"], i["L2_conv_W_x"], i["L2_conv_W_dt"]
    v["l2"] = {"wxp": halves(blocks(TOK, wi[:, :DIN])),
               "wdt": blocks(TOK, np.repeat(wdt, DIN, axis=0)), "wx0": rep(wx[:, 0], TOK),
               "wb": blocks(TOK, wx[:, 1:1 + NS]), "wc": blocks(TOK, wx[:, 1 + NS:]),
               "bdt": rep(i["L2_conv_b_dt"], TOK), "alog": i["L2_conv_A_logs"].reshape(2, P).T,
               "dsk": rep(i["L2_conv_Ds"], TOK)}
    v["l2post"] = {"wz": halves(blocks(TOK, wi[:, DIN:])), "wo": blocks(TOK, i["L2_conv_W_out"]),
                   "gavg": blocks(8, np.full((16, 16), 1.0 / 16, np.float32)),
                   "gnw": two(i["L2_conv_gn_w"]), "gnb": two(i["L2_conv_gn_b"])}
    inw, xp, cw = i["L3_conv_in_w"], i["L3_conv_xproj_w"], i["L3_conv_conv_w"]
    xpr = np.zeros((P, P), np.float32)
    dtw = np.zeros((P, P), np.float32)
    xpr[:16] = blocks(Q4, xp[:4])
    dtw[:16] = blocks(Q4, i["L3_conv_dt_w"].T)
    v["l3conv"] = {"wxi": np.tile(blocks(Q4, inw[:DI].T), (2, 1)),
               "convw": np.broadcast_to(np.tile(cw[:, 0].T[:, None, :], (1, Q4, 1)).reshape(1, -1), (P, 4 * P)),
                   "convb": rep(i["L3_conv_conv_b"], Q4)}
    v["l3"] = {"xpr": xpr, "dtw": dtw, "wbc": blocks(Q4, xp[4:].T),
               "dtb": rep(i["L3_conv_dt_b"], Q4), "alog": i["L3_conv_A_log"].reshape(4, P).T,
               "dp": rep(i["L3_conv_Dp"], Q4)}
    v["l3post"] = {"wz": halves(blocks(Q4, inw[DI:].T)), "wo": blocks(Q4, i["L3_conv_out_w"].T),
                   "skip": np.broadcast_to(i["L3_conv_skip_scale"], (P,))[:, None],
                   "wpj": blocks(2, i["L3_conv_proj_w"].T), "pjb": two(i["L3_conv_proj_b"])}
    v["mlp3"] = mlp_pack(i["L3_conv_fc1_w"].T, i["L3_conv_fc1_b"], i["L3_conv_fc2_w"].T, i["L3_conv_fc2_b"],
                         np.zeros(C, np.float32))
    for name, f in (("up", i["L1_conv_up_filter"][::-1, ::-1]), ("down", i["L1_conv_down_filter"])):
        band = np.zeros((RB, W, KM * P // PITCH + 1, PITCH), np.float32)
        for r in range(RB):
            for ix in range(W):
                band[r, ix, 2 * r:2 * r + TAPS, 2 * ix:2 * ix + TAPS] = f
        band = band.reshape(P, -1)[:, :KM * P]
        if name == "down":
            band = band.reshape(P, KM, P).transpose(2, 1, 0).reshape(P, -1)
        v["fir"][name] = band
    out = {}
    for group, names in CONST.items():
        at, width = layout(names)
        a = np.zeros((P, width), np.float32)
        for name, (lo, hi) in at.items():
            a[:, lo:hi] = v[group][name]
        out["pack_" + group] = a
    return out


class Scope:

    def __init__(self, nc, ctx):
        self.nc, self.ctx = nc, ctx

    def sb(self, name, shape, dt=F32):
        return self.ctx.enter_context(self.nc.sbuf_tensor(name, shape, dt))

    def banks(self, name, n, shape=(P, N), dt=F32):
        return [self.ctx.enter_context(self.nc.psum_tensor(f"{name}{k}", list(shape), dt)) for k in range(n)]

    def sem(self, name):
        return self.nc.alloc_semaphore(name=name)


def fetch(nc, ctx, dram, groups, tag=""):
    m = Scope(nc, ctx)
    found = {}
    with nc.Block() as block:
        @block.sync
        def _(sp):
            for group in groups:
                at, width = layout(CONST[group])
                t, loaded = m.sb(f"k_{group}{tag}", [P, width]), m.sem(f"k_{group}{tag}_in")
                sp.dma_start(t[:], dram["pack_" + group]).then_inc(loaded, 16)
                found[group] = {name: t[:, lo:hi] for name, (lo, hi) in at.items()}, loaded
    return found


def layernorm(nc, consts, tag, src, dst, scale_name, bias_name, arrived=None):
    with ExitStack() as ctx:
        m = Scope(nc, ctx)
        c, const_in = consts["ln"]
        center, square = m.banks(tag + "cen", DEEP), m.sb(tag + "sq", [P, DEEP, N])
        normed = m.sb(tag + "nrm", [P, 2, N])
        var, rstd, lnv = m.banks(tag + "var", DEEP), m.sb(tag + "rstd", [P, DEEP, N]), m.sb(tag + "lnv", [P, 2, N])
        centered, squared, var_done, logged, rstd_done, norm_done, out_done = (
            m.sem(tag + x) for x in ("centered", "squared", "var", "logged", "rstd", "norm", "out"))
        block = ctx.enter_context(nc.Block())

        @block.tensor
        def _(pe):
            pe.wait_ge(const_in, 16)
            for n in range(CHUNKS + 2):
                if n < CHUNKS:
                    if arrived is not None:
                        pe.wait_ge(arrived[n * N // HW], 16 * HALVES)
                    wait(pe, norm_done, n - DEEP + 1)
                    pe.matmul(center[n % DEEP][:], c["center"], src[:, n * N:(n + 1) * N], start=True,
                              stop=True).then_inc(centered, 1)
                if n >= 2:
                    k = n - 2
                    pe.wait_ge(squared, k + 1)
                    wait(pe, logged, k - DEEP + 1)
                    pe.matmul(var[k % DEEP][:], c["mean"], square[:, k % DEEP], start=True,
                              stop=True).then_inc(var_done, 1)

        @block.scalar
        def _(act):
            act.preload_act_table_set("natural_log_exp_and_others")
            for n in range(CHUNKS + 2):
                if n < CHUNKS:
                    act.wait_ge(centered, n + 1)
                    wait(act, var_done, n - DEEP + 1)
                    act.activation(square[:, n % DEEP], center[n % DEEP][:], ACT.Square).then_inc(squared, 1)
                if n >= 2:
                    k = n - 2
                    act.wait_ge(var_done, k + 1)
                    act.activation(lnv[:, k % 2], var[k % DEEP][:], ACT.Ln, bias=LN_EPS).then_inc(logged, 1)
                    act.wait_ge(logged, k + 1)
                    wait(act, norm_done, k - DEEP + 1)
                    act.activation(rstd[:, k % DEEP], lnv[:, k % 2], ACT.Exp, scale=-0.5).then_inc(rstd_done, 1)

        @block.vector
        def _(dve):
            dve.wait_ge(const_in, 16)
            for n in range(CHUNKS):
                dve.wait_ge(rstd_done, n + 1)
                dve.wait_ge(squared, n + 1)
                dve.tensor_tensor(normed[:, n % 2], center[n % DEEP][:], rstd[:, n % DEEP],
                                  ALU.mult).then_inc(norm_done, 1)
                dve.wait_ge(norm_done, n + 1)
                dve.tensor_scalar(dst[:, n * N:(n + 1) * N], normed[:, n % 2], c[scale_name], c[bias_name],
                                  ALU.mult, ALU.add).then_inc(out_done, 1)


def split(act_or_dve, src, parts, h, low):
    own, other = slice(h * C, (h + 1) * C), slice((1 - h) * C, (2 - h) * C)
    if not low:
        return act_or_dve.activation(parts[own], src[own], ACT.Copy)
    return act_or_dve.tensor_tensor(parts[other], src[own], parts[own].bitcast(F32), ALU.subtract)


def mlp(nc, consts, tag, group, src, resid, dst, out=None):
    with ExitStack() as ctx:
        m = Scope(nc, ctx)
        c, const_in = consts[group]
        hidden, act_out, total = m.banks(tag + "hid", 4), m.sb(tag + "gelu", [P, 2, 4, N]), m.banks(tag + "tot", 2)
        bias = m.sb(tag + "bias", [P, 1])
        parts, w1 = m.sb(tag + "parts", [P, 2, HALVES, N], F32R), m.sb(tag + "w1parts", [P, 2, 2 * P], F32R)
        hid_done, gelu_done, tot_done, bias_done, res_done, stored, w1_hi, w1_lo, hi_done, lo_done = (
            m.sem(tag + x) for x in ("hid", "gelu", "tot", "bias", "res", "stored", "w1hi", "w1lo", "hi", "lo"))
        w2 = c["w2"].rearrange("p (k n) -> p k n", n=C)
        block = ctx.enter_context(nc.Block())

        @block.sync
        def _(sp):
            if out is not None:
                for n in range(CHUNKS):
                    sp.wait_ge(res_done, n + 1)
                    bl, at = n * N // HW, n * N % HW
                    for h in range(HALVES):
                        sp.dma_start(out[h * BL + bl, :, at:at + N],
                                     dst[h * C:(h + 1) * C, n * N:(n + 1) * N]).then_inc(stored, 16)
                sp.wait_ge(stored, 16 * HALVES * CHUNKS)

        @block.tensor
        def _(pe):
            pe.wait_ge(w1_lo, 1)
            for n in range(CHUNKS + 1):
                if n < CHUNKS:
                    pe.wait_ge(lo_done, 2 * n + 2)
                    for unit in range(4):
                        h, k = divmod(unit, 2)
                        wait(pe, gelu_done, 4 * (n - 1) + unit + 1)
                        for part in range(2):
                            mm = pe.matmul(hidden[unit][:], w1[:, part, k * P:(k + 1) * P], parts[:, n % 2, h],
                                           start=(part == 0), stop=(part == 1))
                        mm.then_inc(hid_done, 1)
                if n >= 1:
                    j = n - 1
                    wait(pe, res_done, j - 1)
                    pe.wait_ge(gelu_done, 4 * j + 4)
                    for k in range(2):
                        for h in range(HALVES):
                            mm = pe.matmul(total[j % 2][h * C:(h + 1) * C], w2[:, k], act_out[:, j % 2, 2 * h + k],
                                           start=(k == 0), stop=(k == 1), tile_position=(0, h * C))
                    mm.then_inc(tot_done, 1)

        @block.scalar
        def _(act):
            act.wait_ge(const_in, 16)
            act.activation(w1[:, 0], c["w1"], ACT.Copy).then_inc(w1_hi, 1)

            def high(n):
                wait(act, hid_done, 4 * (n - 1))
                for h in range(HALVES):
                    split(act, src[:, n * N:(n + 1) * N], parts[:, n % 2, h], h, False).then_inc(hi_done, 1)

            high(0)
            for n in range(CHUNKS):
                if n + 1 < CHUNKS:
                    high(n + 1)
                wait(act, tot_done, n - 1)
                for unit in range(4):
                    k = unit % 2
                    act.wait_ge(hid_done, 4 * n + unit + 1)
                    act.activation(act_out[:, n % 2, unit], hidden[unit][:], ACT.Gelu,
                                   bias=c["b1"][:, k:k + 1]).then_inc(gelu_done, 1)

        @block.vector
        def _(dve):
            dve.wait_ge(w1_hi, 1)
            dve.tensor_tensor(w1[:, 1], c["w1"], w1[:, 0].bitcast(F32), ALU.subtract).then_inc(w1_lo, 1)
            dve.tensor_tensor(bias[:], c["b2"], c["l1b"], ALU.add).then_inc(bias_done, 1)
            dve.wait_ge(bias_done, 1)

            def low(n):
                dve.wait_ge(hi_done, 2 * n + 2)
                wait(dve, hid_done, 4 * (n - 1))
                for h in range(HALVES):
                    split(dve, src[:, n * N:(n + 1) * N], parts[:, n % 2, h], h, True).then_inc(lo_done, 1)

            low(0)
            for n in range(CHUNKS + 1):
                if n + 1 < CHUNKS:
                    low(n + 1)
                if n >= 1:
                    j = n - 1
                    dve.wait_ge(tot_done, j + 1)
                    cols = slice(j * N, (j + 1) * N)
                    dve.scalar_tensor_tensor(out=dst[:, cols], in0=total[j % 2][:], scalar=bias[:, 0:1],
                                             in1=resid[:, cols], op0=ALU.add, op1=ALU.add).then_inc(res_done, 1)


def attention(nc, consts, dram, xn, x):
    with ExitStack() as ctx:
        m = Scope(nc, ctx)
        c, const_in = consts["attn"]
        rel = m.sb("relrow", [P, WIN, HEADS])
        bias = m.sb("relbias", [P, HEADS, WIN])
        win = m.sb("win", [P, 2, WROW, 2, WIN])
        qs = m.sb("qs", [P, 2, WROW, HALVES, WIN])
        ks = m.sb("ks", [P, 2, ROWCOLS])
        keys = m.sb("keys", [P, 2, HEADS, WIN])
        vals = m.sb("vals", [P, 2, WROW * HALVES, HPAIRS, 32])
        logit, prob, pnorm = (m.sb(x, [P, 2, HEADS, WIN]) for x in ("logit", "prob", "pnorm"))
        top, total, inv = (m.sb(x, [P, 2, HEADS]) for x in ("top", "total", "inv"))
        probt = m.sb("probt", [P, 2, HPAIRS, P])
        mixed = m.sb("mixed", [P, 2, ROWCOLS])
        ps_qk, ps_v, ps_o, ps_y = (m.banks(x, 1)[0] for x in ("psqk", "psv", "pso", "psy"))
        ps_s, ps_t = m.banks("pss", 2), m.banks("pst", 2)
        rel_in, bias_done, zeroed = (m.sem("a_" + x) for x in ("rel", "bias", "zeroed"))
        win_done, qk_done, v_done, q_out, k_out, v_out, y_done, x_done, mix_done = (
            m.sem("a_" + x) for x in ("win", "qk", "v", "qout", "kout", "vout", "y", "x", "mix"))
        keys_done, s_done, added, top_done, shifted, exp_done, sum_done, inv_done, norm_done, t_done, t_out, o_done = (
            m.sem("a_" + x) for x in ("keys", "s", "added", "top", "shifted", "exp", "sum", "inv", "norm", "t",
                                      "tout", "o"))
        R = WROW
        LAG_V, LAG_K, LAG_S, LAG_E, LAG_T, LAG_TO, LAG_O, LAG_Y = 3, 3, 4, 5, 7, 7, 8, 9
        UN, PEEL = 8, 16
        block = ctx.enter_context(nc.Block())

        def image(t, base):
            return t[:, ds(base, ROWCOLS)].rearrange("p (y w x) -> p w y x", y=WS, w=R)

        @block.sync
        def _(sp):
            for half in range(HALVES):
                for ny in range(WS):
                    at = half * WIN + ny * WS
                    src = dram["rel"][0:1, 0:1]
                    src = bass.AP(src.tensor, ny * REL * HEADS, [[HEADS, WS], [REL * HEADS, WS], [1, WS * HEADS]])
                    sp.dma_start(rel[at:at + WS].rearrange("p (a b) h -> p a (b h)", a=WS), src).then_inc(rel_in, 16)

        @block.scalar
        def _(act):
            act.preload_act_table_set("natural_log_exp_and_others")
            act.wait_ge(const_in, 16)

            def body(s, u):
                if u % R == 0 and live(s, PAIRS):
                    par = u // R
                    wait(act, v_done, s - R)
                    wait(act, qk_done, s - R)
                    for twice in range(2):
                        act.activation(win[:, par, :, twice].rearrange("p w (y x) -> p w y x", y=WS),
                                       image(xn, s * WIN), ACT.Copy).then_inc(win_done, R // 2)
                p = s - LAG_E
                if live(p, PAIRS):
                    b = (u - LAG_E) % 2
                    act.wait_ge(shifted, p + 1)
                    wait(act, norm_done, p - 1)
                    wait(act, sum_done, p - 1)
                    act.activation(prob[:, b], logit[:, b], ACT.Exp).then_inc(exp_done, 1)
                p = s - LAG_TO
                if live(p, PAIRS):
                    b = (u - LAG_TO) % 2
                    act.wait_ge(t_done, p + 1)
                    wait(act, o_done, p - 1)
                    act.activation(probt[:, b].rearrange("p a b -> p (a b)"), ps_t[b][:], ACT.Copy).then_inc(t_out, 1)
                p = s - LAG_Y
                if (u - LAG_Y) % R == R - 1 and live(p, PAIRS):
                    par = (u - LAG_Y) % UN // R
                    act.wait_ge(o_done, p + 1)
                    wait(act, y_done, p + 1 - 2 * R)
                    act.activation(mixed[:, par], ps_o[:, 0:ROWCOLS], ACT.Identity,
                                   bias=c["bv"]).then_inc(mix_done, R)

            skewed(act, PAIRS, UN, PEEL, body)

        @block.tensor
        def _(pe):
            pe.wait_ge(const_in, 16)

            def body(s, u):
                if u % R == 0 and live(s, PAIRS):
                    par = u // R
                    pe.wait_ge(win_done, s + R)
                    wait(pe, q_out, s)
                    wait(pe, k_out, s)
                    once = win[:, par, :, 0]
                    pe.matmul(ps_qk[:, 0:ROWCOLS], c["wq"], once, start=True, stop=True)
                    pe.matmul(ps_qk[:, ROWCOLS:2 * ROWCOLS], c["wk"], once, start=True, stop=True).then_inc(qk_done, R)
                p = s - LAG_V
                if u % R == LAG_V and live(p, PAIRS):
                    par = u // R
                    wait(pe, v_out, p)
                    for w in range(R):
                        mm = pe.matmul(ps_v[:, w * P:(w + 1) * P], win[:, par, w].rearrange("p a b -> p (a b)"),
                                       c["wv"], start=True, stop=True)
                    mm.then_inc(v_done, R)
                p = s - LAG_T
                if live(p, PAIRS):
                    b = (u - LAG_T) % 2
                    pe.wait_ge(norm_done, p + 1)
                    wait(pe, t_out, p - 1)
                    for k in range(HPAIRS):
                        mm = pe.transpose(ps_t[b][:, k * P:(k + 1) * P],
                                          pnorm[:, b, 2 * k:2 * k + 2].rearrange("p a b -> p (a b)"), c["ident"])
                    mm.then_inc(t_done, 1)
                p = s - LAG_S
                if live(p, PAIRS):
                    b, w, par = (u - LAG_S) % 2, (u - LAG_S) % R, (u - LAG_S) % UN // R
                    pe.wait_ge(keys_done, p + 1)
                    pe.wait_ge(q_out, p - w + R)
                    wait(pe, added, p - 1)
                    pe.matmul(ps_s[b][:], qs[:, par, w].rearrange("p h n -> p (h n)"),
                              keys[:, b].rearrange("p a b -> p (a b)"), start=True, stop=True).then_inc(s_done, 1)
                p = s - LAG_O
                if live(p, PAIRS):
                    b, w, par = (u - LAG_O) % 2, (u - LAG_O) % R, (u - LAG_O) % UN // R
                    pe.wait_ge(t_out, p + 1)
                    pe.wait_ge(v_out, p - w + R)
                    if w == 0:
                        wait(pe, mix_done, p)
                    for first in (0, 1):
                        for h in range(HALVES):
                            for k2 in range(2):
                                quad = 2 * h + k2
                                k = 2 * k2 + first
                                mm = pe.matmul(ps_o[quad * 32:(quad + 1) * 32, w * WIN:(w + 1) * WIN],
                                               vals[:, par, w * HALVES + h, k], probt[:, b, k, h * WIN:(h + 1) * WIN],
                                               start=(first == 0), stop=(first == 1), tile_position=(0, quad * 32))
                    mm.then_inc(o_done, 1)
                p = s - LAG_Y
                if (u - LAG_Y) % R == R - 1 and live(p, PAIRS):
                    par = (u - LAG_Y) % UN // R
                    pe.wait_ge(mix_done, p + 1)
                    wait(pe, x_done, p + 1 - R)
                    pe.matmul(ps_y[:, 0:ROWCOLS], c["wp"],
                              mixed[:, par].rearrange("p (w y x) -> p y w x", w=R, y=WS),
                              start=True, stop=True).then_inc(y_done, R)

            skewed(pe, PAIRS, UN, PEEL, body)

        @block.vector
        def _(dve):
            dve.wait_ge(const_in, 16)
            dve.wait_ge(rel_in, 16 * HALVES * WS)
            dve.tensor_copy(bias[:], rel[:, ::-1, :].rearrange("p j h -> p h j")).then_inc(bias_done, 1)
            dve.wait_ge(bias_done, 1)
            dve.wait_ge(zeroed, 1)

            def body(s, u):
                if u % R == 0 and live(s, PAIRS):
                    par = u // R
                    dve.wait_ge(qk_done, s + R)
                    wait(dve, s_done, s - R)
                    for h in range(HALVES):
                        r = slice(h * C, (h + 1) * C)
                        dve.tensor_scalar(qs[r, par, :, h], ps_qk[r, 0:ROWCOLS].rearrange("p (w n) -> p w n", n=WIN),
                                          c["bq"][r], float(HD) ** -0.5, ALU.add, ALU.mult).then_inc(q_out, R // 2)
                    wait(dve, keys_done, s - R)
                    dve.tensor_scalar(ks[:, par], ps_qk[:, ROWCOLS:2 * ROWCOLS], c["bk"], None,
                                      ALU.add).then_inc(k_out, R)
                p = s - LAG_V
                if u % R == LAG_V and live(p, PAIRS):
                    par = u // R
                    dve.wait_ge(v_done, p + R)
                    wait(dve, o_done, p - R)
                    v = ps_v[:].rearrange("p (a b) -> p a b", b=C)
                    mask = c["vmask"].rearrange("p (a b) -> p a b", a=2)
                    for k2 in range(2):
                        dve.tensor_tensor(vals[:, par, :, 2 * k2:2 * k2 + 2],
                                          v[:, :, None, 32 * k2:32 * k2 + 32].to_broadcast([P, R * HALVES, 2, 32]),
                                          mask[:, None].to_broadcast([P, R * HALVES, 2, 32]),
                                          ALU.mult).then_inc(v_out, R // 2)
                p = s - LAG_S
                if live(p, PAIRS):
                    b = (u - LAG_S) % 2
                    dve.wait_ge(s_done, p + 1)
                    wait(dve, exp_done, p - 1)
                    wait(dve, shifted, p - 1)
                    dve.tensor_tensor(logit[:, b].rearrange("p a b -> p (a b)"), ps_s[b][:],
                                      bias[:].rearrange("p a b -> p (a b)"), ALU.add).then_inc(added, 1)
                    dve.wait_ge(added, p + 1)
                    dve.tensor_reduce(top[:, b], logit[:, b], AX.X, ALU.max).then_inc(top_done, 1)
                p = s - LAG_E
                if live(p, PAIRS):
                    b = (u - LAG_E) % 2
                    dve.wait_ge(exp_done, p + 1)
                    dve.tensor_reduce(total[:, b], prob[:, b], AX.X, ALU.add).then_inc(sum_done, 1)
                    dve.wait_ge(sum_done, p + 1)
                    wait(dve, norm_done, p - 1)
                    dve.reciprocal(inv[:, b], total[:, b]).then_inc(inv_done, 1)
                p = s - LAG_Y
                if (u - LAG_Y) % R == R - 1 and live(p, PAIRS):
                    dve.wait_ge(y_done, p + 1)
                    cols = ds((p + 1 - R) * WIN, ROWCOLS)
                    dve.scalar_tensor_tensor(out=x[:, cols], in0=ps_y[:, 0:ROWCOLS], scalar=c["bp"], in1=x[:, cols],
                                             op0=ALU.add, op1=ALU.add).then_inc(x_done, R)

            skewed(dve, PAIRS, UN, PEEL, body)

        @block.gpsimd
        def _(pool):
            pool.memset(qs[:], 0.0).then_inc(zeroed, 1)
            pool.wait_ge(const_in, 16)

            def body(s, u):
                p = s - LAG_K
                if live(p, PAIRS):
                    b, w, par = (u - LAG_K) % 2, (u - LAG_K) % R, (u - LAG_K) % UN // R
                    pool.wait_ge(k_out, p - w + R)
                    wait(pool, s_done, p - 1)
                    pool.tensor_tensor(keys[:, b],
                                       ks[:, par, None, w * WIN:(w + 1) * WIN].to_broadcast([P, HEADS, WIN]),
                                       c["kmask"][:, :, None].to_broadcast([P, HEADS, WIN]),
                                       ALU.mult).then_inc(keys_done, 1)
                p = s - LAG_S
                if live(p, PAIRS):
                    b = (u - LAG_S) % 2
                    pool.wait_ge(top_done, p + 1)
                    pool.tensor_tensor(logit[:, b], logit[:, b], top[:, b, :, None].to_broadcast([P, HEADS, WIN]),
                                       ALU.subtract).then_inc(shifted, 1)
                p = s - LAG_E
                if live(p, PAIRS):
                    b = (u - LAG_E) % 2
                    pool.wait_ge(inv_done, p + 1)
                    wait(pool, t_done, p - 1)
                    pool.tensor_tensor(pnorm[:, b], prob[:, b], inv[:, b, :, None].to_broadcast([P, HEADS, WIN]),
                                       ALU.mult).then_inc(norm_done, 1)

            skewed(pool, PAIRS, UN, PEEL, body)


def antialiased(nc, consts, x):
    with ExitStack() as ctx:
        m = Scope(nc, ctx)
        c, const_in = consts["fir"]
        bands = c["up"], c["down"]
        band_parts = m.sb("bandparts", [P, 2, 2, KM * P], F32R)
        pos = m.sb("pos", [P, TILES, 2, N], F32R)
        lin, rect, act_y = (m.sb(t, [P, 2, N]) for t in ("lin", "rect", "acty"))
        act_parts = m.sb("actparts", [P, 3, 2, N], F32R)
        tile_out = m.sb("tileout", [P, 2, N])
        ps_up, ps_down, ps_t = m.banks("psup", 3), m.banks("psdown", 3), m.banks("pstr", 2)
        band_hi, band_lo, tp_done, pos_hi, tp_out, act_hi = (
            m.sem("f_" + t) for t in ("bandhi", "bandlo", "tp", "poshi", "tpout", "acthi"))
        up_done, lin_done, rect_done, clamped, act_done, acc_done, tile_done, back_done, x_done = (
            m.sem("f_" + t) for t in ("up", "lin", "rect", "clamped", "act", "acc", "tile", "back", "x"))

        LAG = 3

        def sources(j):
            return [(t, j - BLK * t) for t in range(TILES) if 0 <= j - BLK * t < KM]

        block = ctx.enter_context(nc.Block())

        @block.tensor
        def _(pe):
            pe.wait_ge(const_in, 16)
            for t in range(TILES):
                wait(pe, tp_out, t - 1)
                for bl in range(BL):
                    mm = pe.transpose(ps_t[t % 2][:, bl * P:(bl + 1) * P],
                                      x[:, bl * HW + t * P:bl * HW + (t + 1) * P], c["ident"])
                mm.then_inc(tp_done, 1)
            pe.wait_ge(band_lo, 2)

            def product(bank, way, k, parts, first, last):
                for n, (of_band, of_data) in enumerate(((0, 0), (0, 1), (1, 0))):
                    mm = pe.matmul(bank[:], band_parts[:, way, of_band, k * P:(k + 1) * P], parts[:, of_data],
                                   start=(first and n == 0), stop=(last and n == 2))
                return mm

            def up(j):
                pe.wait_ge(tp_out, sources(j)[-1][0] + 1)
                wait(pe, lin_done, j - 2)
                src = sources(j)
                for n, (t, k) in enumerate(src):
                    mm = product(ps_up[j % 3], 0, k, pos[:, t], n == 0, n == len(src) - 1)
                mm.then_inc(up_done, 1)

            def down(j):
                pe.wait_ge(act_done, j + 1)
                for t, k in sources(j):
                    if k == 0:
                        wait(pe, tile_done, t - 2)
                    mm = product(ps_down[t % 3], 1, k, act_parts[:, j % 3], k == 0, k == KM - 1)
                mm.then_inc(acc_done, 1)

            def back(t):
                pe.wait_ge(tile_done, t + 1)
                wait(pe, x_done, t - 1)
                pe.wait_ge(tp_out, TILES)
                for bl in range(BL):
                    mm = pe.transpose(ps_t[t % 2][:, bl * P:(bl + 1) * P], tile_out[:, t % 2, bl * P:(bl + 1) * P],
                                      c["ident"])
                mm.then_inc(back_done, 1)

            for j in range(UPB + LAG + 2):
                if j < UPB:
                    up(j)
                if LAG <= j < UPB + LAG:
                    down(j - LAG)
                t, rest = divmod(j - LAG - 1 - KM, BLK)
                if rest == 0 and 0 <= t < TILES:
                    back(t)

        @block.scalar
        def _(act):
            for t in range(TILES):
                act.wait_ge(tp_done, t + 1)
                act.activation(pos[:, t, 0], ps_t[t % 2][:], ACT.Copy).then_inc(pos_hi, 1)
            for way in range(2):
                act.wait_ge(const_in, 16)
                act.activation(band_parts[:, way, 0], bands[way], ACT.Copy).then_inc(band_hi, 1)
            def finish(t):
                act.wait_ge(acc_done, BLK * t + KM)
                wait(act, back_done, t - 1)
                act.activation(tile_out[:, t % 2], ps_down[t % 3][:], ACT.Copy).then_inc(tile_done, 1)

            def high(j):
                act.wait_ge(clamped, j + 1)
                wait(act, acc_done, j - 2)
                act.activation(act_parts[:, j % 3, 0], act_y[:, j % 2], ACT.Copy).then_inc(act_hi, 1)

            for j in range(UPB):
                act.wait_ge(up_done, j + 1)
                wait(act, rect_done, j - 1)
                act.activation(lin[:, j % 2], ps_up[j % 3][:], ACT.Copy, scale=GAIN).then_inc(lin_done, 1)
                if j >= 1:
                    high(j - 1)
                t, rest = divmod(j - KM - LAG + 1, BLK)
                if rest == 0 and t >= 0:
                    finish(t)
            high(UPB - 1)
            finish(TILES - 1)

        @block.vector
        def _(dve):
            def put(t):
                dve.wait_ge(back_done, t + 1)
                dve.tensor_copy(x.rearrange("p (b t n) -> p t b n", b=BL, n=P)[:, t],
                                ps_t[t % 2][:].rearrange("p (b n) -> p b n", b=BL)).then_inc(x_done, 1)

            for t in range(TILES):
                dve.wait_ge(pos_hi, t + 1)
                dve.tensor_tensor(pos[:, t, 1], ps_t[t % 2][:], pos[:, t, 0].bitcast(F32),
                                  ALU.subtract).then_inc(tp_out, 1)

            def low(j):
                dve.wait_ge(act_hi, j + 1)
                wait(dve, acc_done, j - 2)
                dve.tensor_tensor(act_parts[:, j % 3, 1], act_y[:, j % 2], act_parts[:, j % 3, 0].bitcast(F32),
                                  ALU.subtract).then_inc(act_done, 1)

            for j in range(UPB):
                dve.wait_ge(lin_done, j + 1)
                dve.scalar_tensor_tensor(out=rect[:, j % 2], in0=lin[:, j % 2], scalar=SLOPE, in1=lin[:, j % 2],
                                         op0=ALU.mult, op1=ALU.max).then_inc(rect_done, 1)
                dve.wait_ge(rect_done, j + 1)
                wait(dve, act_done, j - 1)
                dve.tensor_scalar(act_y[:, j % 2], rect[:, j % 2], CLAMP, -CLAMP, ALU.min,
                                  ALU.max).then_inc(clamped, 1)
                if j >= 1:
                    low(j - 1)
                t, rest = divmod(j - KM - LAG - 2, BLK)
                if rest == 0 and t >= 0:
                    put(t)
            low(UPB - 1)
            for t in range((UPB - 1 - KM - LAG - 2) // BLK + 1, TILES):
                put(t)

        @block.gpsimd
        def _(pool):
            for way in range(2):
                pool.wait_ge(band_hi, way + 1)
                pool.tensor_tensor(band_parts[:, way, 1], bands[way], band_parts[:, way, 0].bitcast(F32),
                                   ALU.subtract).then_inc(band_lo, 1)


STEPS = 64
UNROLL, PEEL = 8, 8


def selectors(nc, consts, selr, ysel):
    with ExitStack() as ctx:
        m = Scope(nc, ctx)
        c, const_in = consts["scan"]
        copied = m.sem("z_copied")
        block = ctx.enter_context(nc.Block())

        @block.vector
        def _(dve):
            dve.wait_ge(const_in, 16)
            dve.tensor_copy(selr[:, 0:16 * P], c["sel"]).then_inc(copied, 1)
            dve.tensor_copy(selr[:, 16 * P:], c["seln"]).then_inc(copied, 1)
            dve.tensor_copy(ysel[:], c["ysel"]).then_inc(copied, 1)


def prepare_a(m, tag, c, blocks_of_a):
    low, grown, neg = (m.sb(tag + t, [P, blocks_of_a]) for t in ("alow", "agrown", "aneg"))
    low_done, grown_done, neg_done = (m.sem(tag + t) for t in ("alowd", "agrownd", "anegd"))

    def on_vector(dve):
        dve.tensor_scalar(low[:], c["alog"], AMAX, None, ALU.min).then_inc(low_done, 1)
        dve.wait_ge(grown_done, 1)
        dve.tensor_scalar(neg[:], grown[:], -1.0, None, ALU.mult).then_inc(neg_done, 1)

    def on_scalar(act):
        act.wait_ge(low_done, 1)
        act.activation(grown[:], low[:], ACT.Exp).then_inc(grown_done, 1)
        act.wait_ge(neg_done, 1)

    return neg, on_vector, on_scalar


def scan2(nc, consts, x, y, selr, ysel):
    with ExitStack() as ctx:
        m = Scope(nc, ctx)
        c, const_in = consts["l2"]
        wdt, bdt2, dsk2 = m.sb("s_wdtb", [P, P]), m.sb("s_bdt2", [P, 1]), m.sb("s_dsk2", [P, 1])
        xp = m.sb("s_xp", [P, N])
        delta, du = m.sb("s_delta", [P, N]), m.sb("s_du", [P, N])
        relu, ex, one = (m.sb("s_" + t, [P, N]) for t in ("relu", "ex", "one"))
        parts_b, parts_c = (m.sb("s_parts" + t, [P, 2, N], F32R) for t in "bc")
        parts_d, parts_u = (m.sb("s_parts" + t, [P, 2, 2, N], F32R) for t in "du")
        decay, feed = m.sb("s_decay", [P, 2, N2, SLOT]), m.sb("s_feed", [P, N2, SLOT])
        ahead, back = m.sb("s_ahead", [P, 2, N2, SLOT]), m.sb("s_back", [P, 2, N2, SLOT])
        bs, cs = m.sb("s_bs", [P, 2, TOK, N2]), m.sb("s_cs", [P, 2, N2, TOK])
        low_prod, high_prod = m.sb("s_lprod", [P, N2, TOK // 2]), m.sb("s_hprod", [P, 2, N2, TOK // 2])
        ps_in, ps_dt, ps_y, ps_bc = (m.banks("s_p" + t, 1)[0] for t in ("in", "dt", "y", "bc"))
        ps_d, ps_u = m.banks("s_pd", 2), m.banks("s_pu", 2)
        ready, zeroed = (m.sem("s_" + t) for t in ("ready", "zeroed"))
        xp_ps, xp_done, skip_done, dt_ps, b_ps, c_ps, away_done, relu_done, ex_done, one_done, ln_done, lost_done, \
            rest_done, delta_done, du_done = (m.sem("s_" + t) for t in (
                "xpps", "xpd", "skipd", "dtps", "bps", "cps", "awayd", "relud", "exd", "oned", "lnd", "lostd",
                "restd", "deltad", "dud"))
        hi_d, hi_u, hi_b, hi_c, lo_d, lo_u, lo_b, lo_c = (
            m.sem("s_" + t) for t in ("hid", "hiu", "hib", "hic", "lod", "lou", "lob", "loc"))
        d_ps, decayed, b_rep, b_copied, c_rep, c_copied, u_rep, fed, ahead_done, back_done, summed, low_done, \
            high_done, y_part, y_done = (m.sem("s_" + t) for t in (
                "dps", "decayed", "brepd", "bcop", "crepd", "ccop", "urep", "fed", "aheadd", "backd", "summed",
                "lowp", "highp", "ypart", "ydone"))
        aneg, a_on_vector, a_on_scalar = prepare_a(m, "s_", c, 2)
        LAG_B, LAG_D, LAG_A, LAG_C, LAG_Y = 3, 4, 5, 6, 7
        block = ctx.enter_context(nc.Block())

        def place(u):
            u %= UNROLL
            return u // 4, slice(u % 4 // 2 * N2, (u % 4 // 2 + 1) * N2), u % 2

        @block.tensor
        def _(pe):
            pe.wait_ge(ready, 3)

            def spread(bank, sel, parts, cols):
                for i in range(2):
                    for part in range(2):
                        mm = pe.matmul(bank[:, i * N2:(i + 1) * N2], selr[:, sel[i] * P:(sel[i] + 1) * P],
                                       parts[:, part, cols], start=(part == 0), stop=(part == 1))
                return mm

            def body(s, u):
                par = u // 4
                if u % 4 == 0 and live(s, STEPS):
                    wait(pe, lo_b, s)
                    pe.matmul(ps_in[:], c["wxp"][:, par * P:(par + 1) * P], x[:, ds((s - u) * (N // UNROLL), N)],
                              start=True, stop=True).then_inc(xp_ps, 4)
                if u % 4 == 1 and live(s, STEPS):
                    pe.wait_ge(xp_done, s + 3)
                    pe.wait_ge(skip_done, s + 3)
                    wait(pe, lo_c, s - 1)
                    pe.matmul(ps_dt[:], wdt[:], xp[:], start=True, stop=True).then_inc(dt_ps, 4)
                    pe.matmul(ps_in[:], c["wb"], xp[:], start=True, stop=True).then_inc(b_ps, 4)
                if u % 4 == 2 and live(s, STEPS):
                    pe.wait_ge(relu_done, s + 2)
                    pe.matmul(ps_dt[:], c["wc"], xp[:], start=True, stop=True).then_inc(c_ps, 4)
                p, v = s - LAG_D, u - LAG_D
                q, w = s - LAG_B, u - LAG_B
                r, z = s - LAG_A, u - LAG_A

                def decays(tp):
                    if live(p, STEPS):
                        par, cols, g = place(v)
                        if v % 4 == 0 and tp == 0:
                            pe.wait_ge(lo_d, p + 4)
                        wait(pe, decayed, 4 * p + tp - 1)
                        spread(ps_d[tp % 2], [2 * (2 * tp + i) + g for i in range(2)], parts_d[:, par],
                               cols).then_inc(d_ps, 1)

                def states(tp):
                    if live(q, STEPS):
                        par, cols, second = place(w)
                        if w % 4 == second and tp == 0:
                            pe.wait_ge((lo_b, lo_c)[second], q - second + 4)
                        if tp:
                            pe.wait_ge((b_copied, c_copied)[second], 4 * (q - second) + 2 * tp)
                        elif second:
                            pe.wait_ge(b_copied, 4 * (q - 1) + 8)
                        else:
                            wait(pe, c_copied, 4 * q)
                        spread(ps_bc, [16 + 2 * tp + i for i in range(2)], (parts_b, parts_c)[second],
                               cols).then_inc((b_rep, c_rep)[second], 2)

                def inputs(tp):
                    if live(r, STEPS):
                        par, cols, g = place(z)
                        if z % 4 == 0 and tp == 0:
                            pe.wait_ge(lo_u, r + 4)
                        wait(pe, fed, 4 * r + tp - 1)
                        spread(ps_u[tp % 2], [2 * (2 * tp + i) + g for i in range(2)], parts_u[:, par],
                               cols).then_inc(u_rep, 1)

                inputs(0)
                inputs(1)
                decays(0)
                decays(1)
                inputs(2)
                inputs(3)
                states(0)
                o = s - LAG_Y
                if live(o, STEPS):
                    _, cols, g = place(u - LAG_Y)
                    if (u - LAG_Y) % 4 == 0:
                        wait(pe, y_done, o)
                    pe.wait_ge(low_done, 2 * o + 2)
                    pe.wait_ge(high_done, 2 * o + 2)
                    for odd in range(2):
                        for quad in range(4):
                            t = 2 * quad + odd
                            src = low_prod[:, :, t] if t < TOK // 2 else high_prod[:, (u - LAG_Y) % 2, :, t - TOK // 2]
                            mm = pe.matmul(ps_y[quad * 32:(quad + 1) * 32, cols],
                                           ysel[:, (2 * odd + g) * 32:(2 * odd + g + 1) * 32],
                                           src, start=(odd == 0 and g == 0),
                                           stop=(odd == 1 and g == 1), tile_position=(0, quad * 32))
                    mm.then_inc(y_part, 1)
                states(1)
                decays(2)
                states(2)
                decays(3)
                states(3)

            skewed(pe, STEPS, UNROLL, PEEL, body)

        @block.scalar
        def _(act):
            act.preload_act_table_set("natural_log_exp_and_others")
            a_on_scalar(act)
            act.wait_ge(ready, 3)
            act.wait_ge(zeroed, 3)

            def body(s, u):
                par, gi = u // 4, s - u % 4
                if u % 4 == 0 and live(s, STEPS):
                    act.wait_ge(xp_ps, gi + 4)
                    wait(act, c_ps, gi)
                    wait(act, du_done, gi)
                    act.activation(xp[:], ps_in[:], ACT.Copy).then_inc(xp_done, 4)
                    act.activation(y[:, par, ds((s - u) * (N // UNROLL), N)], ps_in[:], ACT.Copy,
                                   scale=dsk2[:, 0:1]).then_inc(skip_done, 4)
                if u % 4 == 1 and live(s, STEPS):
                    act.wait_ge(dt_ps, gi + 4)
                    wait(act, rest_done, gi)
                    act.activation(ex[:], ps_dt[:], ACT.Abs, bias=bdt2[:, 0:1]).then_inc(away_done, 4)
                    wait(act, delta_done, gi)
                    act.activation(relu[:], ps_dt[:], ACT.Relu, bias=bdt2[:, 0:1]).then_inc(relu_done, 4)
                    act.wait_ge(away_done, gi + 4)
                    act.activation(ex[:], ex[:], ACT.Exp, scale=-1.0).then_inc(ex_done, 4)
                if u % 4 == 2 and live(s, STEPS):
                    act.wait_ge(one_done, gi + 4)
                    act.wait_ge(lost_done, gi + 4)
                    act.activation(one[:], one[:], ACT.Ln).then_inc(ln_done, 4)
                if u % 4 == 3 and live(s, STEPS):
                    act.wait_ge(delta_done, gi + 4)
                    wait(act, d_ps, 4 * (gi - 4))
                    act.activation(parts_d[:, par, 0], delta[:], ACT.Copy).then_inc(hi_d, 4)
                if u % 4 == 0 and live(s - 4, STEPS):
                    act.wait_ge(du_done, s)
                    wait(act, u_rep, 4 * (s - 7))
                    act.activation(parts_u[:, 1 - par, 0], du[:], ACT.Copy).then_inc(hi_u, 4)
                p, v = s - LAG_D, u - LAG_D
                q, w = s - LAG_B, u - LAG_B
                for tp in range(4):
                    if live(p, STEPS):
                        b, g = v % 2, place(v)[2]
                        wait(act, back_done, p - 1)
                        act.wait_ge(d_ps, 4 * p + tp + 1)
                        act.activation(decay[:, b, :, 2 * tp:2 * tp + 2].rearrange("p n t -> p t n"),
                                       ps_d[tp % 2][:].rearrange("p (t n) -> p t n", t=2), ACT.Exp,
                                       scale=aneg[:, g:g + 1]).then_inc(decayed, 1)
                    if live(q, STEPS):
                        second, blk = place(w)[2], w % 4 // 2
                        act.wait_ge((b_rep, c_rep)[second], 4 * (q - second) + 2 * tp + 2)
                        if second == 0:
                            wait(act, fed, 4 * (q - 3) + tp + 1)
                            act.activation(bs[:, blk, 2 * tp:2 * tp + 2].rearrange("p t n -> p (t n)"), ps_bc[:],
                                           ACT.Copy).then_inc(b_copied, 2)
                        else:
                            wait(act, (low_done, high_done)[tp // 2], 2 * (q - 3))
                            act.activation(cs[:, blk, :, 2 * tp:2 * tp + 2].rearrange("p n t -> p t n"),
                                           ps_bc[:].rearrange("p (t n) -> p t n", t=2),
                                           ACT.Copy).then_inc(c_copied, 2)
                if u % 4 == 1 and live(s, STEPS):
                    act.wait_ge(b_ps, gi + 4)
                    wait(act, b_rep, 4 * gi)
                    act.activation(parts_b[:, 0], ps_in[:], ACT.Copy).then_inc(hi_b, 4)
                if u % 4 == 2 and live(s, STEPS):
                    act.wait_ge(c_ps, gi + 4)
                    wait(act, c_rep, 4 * gi)
                    act.activation(parts_c[:, 0], ps_dt[:], ACT.Copy).then_inc(hi_c, 4)

            skewed(act, STEPS, UNROLL, PEEL, body)

        @block.vector
        def _(dve):
            dve.wait_ge(const_in, 16)
            dve.tensor_scalar(wdt[:], c["wdt"], c["wx0"], None, ALU.mult).then_inc(ready, 1)
            dve.tensor_scalar(bdt2[:], c["bdt"], 2.0, None, ALU.mult).then_inc(ready, 1)
            dve.tensor_scalar(dsk2[:], c["dsk"], 2.0, None, ALU.mult).then_inc(ready, 1)
            a_on_vector(dve)
            dve.wait_ge(zeroed, 3)

            def body(s, u):
                p, v = s - LAG_A, u - LAG_A
                if live(p, STEPS):
                    b, g, blk = v % 2, place(v)[2], v % 4 // 2
                    for tp in range(4):
                        dve.wait_ge(u_rep, 4 * p + tp + 1)
                        if g == 0:
                            dve.wait_ge(b_copied, 4 * p + 2 * tp + 2)
                        wait(dve, back_done, p)
                        dve.tensor_tensor(feed[:, :, 2 * tp:2 * tp + 2].rearrange("p n t -> p t n"),
                                          ps_u[tp % 2][:].rearrange("p (t n) -> p t n", t=2),
                                          bs[:, blk, 2 * tp:2 * tp + 2], ALU.mult).then_inc(fed, 1)
                if live(p, STEPS):
                    dve.wait_ge(decayed, 4 * p + 4)
                    dve.wait_ge(fed, 4 * p + 4)
                    a, f = (t.rearrange("p n t -> p (n t)") for t in (decay[:, b], feed[:]))
                    wait(dve, low_done, 2 * (p - 1))
                    wait(dve, high_done, 2 * (p - 1))
                    dve.tensor_tensor_scan(ahead[:, b].rearrange("p n t -> p (n t)"), a, f, 0.0, ALU.mult,
                                           ALU.add).then_inc(ahead_done, 1)
                c_step, w = s - LAG_C, u - LAG_C
                if live(c_step, STEPS):
                    wait(dve, y_part, c_step)
                    dve.wait_ge(summed, 2 * c_step + 1)
                    if place(w)[2] == 0:
                        dve.wait_ge(c_copied, 4 * c_step + 4)
                    dve.tensor_tensor(low_prod[:], cs[:, w % 4 // 2, :, 0:TOK // 2],
                                      ahead[:, w % 2, :, 0:TOK // 2], ALU.mult).then_inc(low_done, 2)
                if live(p, STEPS):
                    wait(dve, summed, 2 * (p - 1))
                    dve.tensor_tensor_scan(back[:, b].rearrange("p n t -> p (n t)")[:, ::-1], a[:, ::-1], f[:, ::-1],
                                           0.0, ALU.mult, ALU.add).then_inc(back_done, 1)
                p = s - LAG_Y
                if (u - LAG_Y) % 4 == 3 and live(p, STEPS):
                    half = place(u - LAG_Y)[0]
                    dve.wait_ge(y_part, p + 1)
                    dve.wait_ge(skip_done, p + 1)
                    cols = ds((p - (u - LAG_Y) % UNROLL) * (N // UNROLL), N)
                    dve.tensor_tensor(y[:, half, cols], ps_y[:], y[:, half, cols], ALU.add).then_inc(y_done, 4)
                if not live(s, STEPS):
                    return
                par, gi = u // 4, s - u % 4
                if u % 4 == 1:
                    dve.wait_ge(ex_done, gi + 4)
                    wait(dve, delta_done, gi)
                    dve.tensor_scalar(one[:], ex[:], 1.0, None, ALU.add).then_inc(one_done, 4)
                    dve.wait_ge(one_done, gi + 4)
                    dve.scalar_tensor_tensor(out=ex[:], in0=one[:], scalar=-1.0, in1=ex[:], op0=ALU.add,
                                             op1=ALU.subtract).then_inc(lost_done, 4)
                    dve.wait_ge(hi_b, gi + 4)
                    wait(dve, b_rep, 4 * gi)
                    dve.tensor_tensor(parts_b[:, 1], ps_in[:], parts_b[:, 0].bitcast(F32),
                                      ALU.subtract).then_inc(lo_b, 4)
                if u % 4 == 2:
                    dve.wait_ge(hi_c, gi + 4)
                    wait(dve, c_rep, 4 * gi)
                    dve.tensor_tensor(parts_c[:, 1], ps_dt[:], parts_c[:, 0].bitcast(F32),
                                      ALU.subtract).then_inc(lo_c, 4)

            skewed(dve, STEPS, UNROLL, PEEL, body)

        @block.gpsimd
        def _(pool):
            for t in (decay[:, 0], decay[:, 1], feed[:]):
                pool.memset(t, 0.0).then_inc(zeroed, 1)

            def body(s, u):
                par, gi = u // 4, s - u % 4
                if u % 4 == 2 and live(s, STEPS):
                    pool.wait_ge(ln_done, gi + 4)
                    pool.wait_ge(lost_done, gi + 4)
                    pool.tensor_tensor(one[:], one[:], ex[:], ALU.subtract).then_inc(rest_done, 4)
                    pool.wait_ge(rest_done, gi + 4)
                    pool.wait_ge(relu_done, gi + 4)
                    wait(pool, hi_d, gi)
                    wait(pool, lo_d, gi)
                    pool.tensor_tensor(delta[:], relu[:], one[:], ALU.add).then_inc(delta_done, 4)
                if u % 4 == 3 and live(s, STEPS):
                    pool.wait_ge(delta_done, gi + 4)
                    wait(pool, hi_u, gi)
                    wait(pool, lo_u, gi)
                    pool.wait_ge(xp_done, gi + 4)
                    pool.tensor_tensor(du[:], delta[:], xp[:], ALU.mult).then_inc(du_done, 4)
                    pool.wait_ge(hi_d, gi + 4)
                    wait(pool, d_ps, 4 * (gi - 4))
                    pool.tensor_tensor(parts_d[:, par, 1], delta[:], parts_d[:, par, 0].bitcast(F32),
                                       ALU.subtract).then_inc(lo_d, 4)
                if u % 4 == 0 and live(s - 4, STEPS):
                    pool.wait_ge(hi_u, s)
                    wait(pool, u_rep, 4 * (s - 7))
                    pool.tensor_tensor(parts_u[:, 1 - par, 1], du[:], parts_u[:, 1 - par, 0].bitcast(F32),
                                       ALU.subtract).then_inc(lo_u, 4)
                p, v = s - LAG_A, u - LAG_A
                if live(p, STEPS):
                    b = v % 2
                    pool.wait_ge(ahead_done, p + 1)
                    pool.wait_ge(back_done, p + 1)
                    for part in range(2):
                        toks = slice(part * TOK // 2, (part + 1) * TOK // 2)
                        pool.tensor_tensor(ahead[:, b, :, toks], ahead[:, b, :, toks], back[:, b, :, toks],
                                           ALU.add).then_inc(summed, 1)
                    pool.wait_ge(summed, 2 * p + 2)
                    wait(pool, y_part, p - 1)
                    if place(v)[2] == 0:
                        pool.wait_ge(c_copied, 4 * p + 8)
                    pool.tensor_tensor(high_prod[:, b], cs[:, v % 4 // 2, :, TOK // 2:],
                                       ahead[:, b, :, TOK // 2:TOK], ALU.mult).then_inc(high_done, 2)

            skewed(pool, STEPS, UNROLL, PEEL, body)


def gated(nc, consts, tag, group, src, y, func, dst, sums=None):
    with ExitStack() as ctx:
        m = Scope(nc, ctx)
        c, const_in = consts[group]
        gate, gated_y = m.sb(tag + "gate", [P, 2, N]), m.sb(tag + "gy", [P, 2, HALVES, N])
        ps_z, ps_o = m.banks(tag + "psz", 3), m.banks(tag + "pso", 2)
        z_done, gate_done, gy_done, o_done, dst_done = (
            m.sem(tag + t) for t in ("zd", "gated", "gyd", "od", "dstd"))
        block = ctx.enter_context(nc.Block())
        units = [(n, h) for n in range(CHUNKS) for h in range(HALVES)]

        @block.tensor
        def _(pe):
            pe.wait_ge(const_in, 16)
            for k in range(len(units) + 2):
                if k < len(units):
                    n, h = units[k]
                    wait(pe, gate_done, k - 2)
                    pe.matmul(ps_z[k % 3][:], c["wz"][:, h * P:(h + 1) * P], src[:, n * N:(n + 1) * N], start=True,
                              stop=True).then_inc(z_done, 1)
                if k >= 2 and k % 2 == 1:
                    n = k // 2 - 1
                    pe.wait_ge(gy_done, k - 1)
                    wait(pe, dst_done, n - 1)
                    for h in range(HALVES):
                        mm = pe.matmul(ps_o[n % 2][h * C:(h + 1) * C], c["wo"], gated_y[:, n % 2, h], start=True,
                                       stop=True, tile_position=(0, h * C))
                    mm.then_inc(o_done, 1)

        @block.scalar
        def _(act):
            for k in range(len(units)):
                act.wait_ge(z_done, k + 1)
                wait(act, gy_done, k - 1)
                act.activation(gate[:, k % 2], ps_z[k % 3][:], func).then_inc(gate_done, 1)

        @block.vector
        def _(dve):
            dve.wait_ge(const_in, 16)

            def finish(n):
                dve.wait_ge(o_done, n + 1)
                cols = slice(n * N, (n + 1) * N)
                if sums is None:
                    dve.scalar_tensor_tensor(out=dst[:, cols], in0=src[:, cols], scalar=c["skip"],
                                             in1=ps_o[n % 2][:], op0=ALU.mult, op1=ALU.add).then_inc(dst_done, 1)
                else:
                    dve.tensor_scalar(dst[:, cols], ps_o[n % 2][:], 1.0, 0.0, ALU.mult, ALU.add,
                                      accum_out=sums[:, n:n + 1]).then_inc(dst_done, 1)

            for k, (n, h) in enumerate(units):
                dve.wait_ge(gate_done, k + 1)
                wait(dve, o_done, n - 1)
                dve.tensor_tensor(gated_y[:, n % 2, h], y[:, h, n * N:(n + 1) * N], gate[:, k % 2],
                                  ALU.mult).then_inc(gy_done, 1)
                if h == 1 and n >= 1:
                    finish(n - 1)
            finish(CHUNKS - 1)


def groupnorm(nc, consts, src, sums, x):
    with ExitStack() as ctx:
        m = Scope(nc, ctx)
        c, const_in = consts["l2post"]
        spread, total, scaled = m.sb("g_spread", [P, HW]), m.sb("g_total", [P, BL]), m.sb("g_scaled", [P, 2, HW])
        means, square, lnv, rstd, gain, shift, offset = (m.sb("g_" + t, [P, BL]) for t in (
            "means", "square", "lnv", "rstd", "gain", "shift", "offset"))
        ps_m, ps_v = m.banks("g_psm", 1, (P, BL))[0], m.banks("g_psv", 1, (P, BL))[0]
        total_done, mean_ps, mean_done, square_done, var_ps, logged, rstd_done, gain_done, shift_done, \
            offset_done, scaled_done, x_done = (m.sem("g_" + t) for t in (
                "totald", "meanps", "meand", "squared", "varps", "logged", "rstdd", "gaind", "shiftd",
                "offsetd", "scaledd", "xd"))
        block = ctx.enter_context(nc.Block())

        @block.tensor
        def _(pe):
            pe.wait_ge(const_in, 16)
            pe.wait_ge(total_done, 1)
            pe.matmul(ps_m[:], c["gavg"], total[:], start=True, stop=True).then_inc(mean_ps, 1)
            pe.wait_ge(square_done, BL)
            pe.matmul(ps_v[:], c["gavg"], square[:], start=True, stop=True).then_inc(var_ps, 1)

        @block.scalar
        def _(act):
            act.preload_act_table_set("natural_log_exp_and_others")
            act.wait_ge(mean_done, 1)
            for bl in range(BL):
                wait(act, square_done, bl)
                act.activation(spread[:], src[:, bl * HW:(bl + 1) * HW], ACT.Square, bias=means[:, bl:bl + 1],
                               accum_out=square[:, bl:bl + 1]).then_inc(square_done, 1)
            act.wait_ge(var_ps, 1)
            act.activation(lnv[:], ps_v[:], ACT.Ln, scale=1.0 / HW, bias=LN_EPS).then_inc(logged, 1)
            act.wait_ge(logged, 1)
            act.activation(rstd[:], lnv[:], ACT.Exp, scale=-0.5).then_inc(rstd_done, 1)
            act.wait_ge(gain_done, 1)
            act.wait_ge(offset_done, 1)
            for bl in range(BL):
                wait(act, x_done, bl - 1)
                act.activation(scaled[:, bl % 2], src[:, bl * HW:(bl + 1) * HW], ACT.Identity,
                               scale=gain[:, bl:bl + 1], bias=offset[:, bl:bl + 1]).then_inc(scaled_done, 1)

        @block.vector
        def _(dve):
            pairs = sums.rearrange("p (b k) -> p k b", k=HW // N)
            dve.tensor_tensor(total[:], pairs[:, 0], pairs[:, 1], ALU.add).then_inc(total_done, 1)
            dve.wait_ge(mean_ps, 1)
            dve.tensor_scalar(means[:], ps_m[:], -1.0 / HW, None, ALU.mult).then_inc(mean_done, 1)
            dve.wait_ge(const_in, 16)
            dve.wait_ge(rstd_done, 1)
            dve.tensor_scalar(gain[:], rstd[:], c["gnw"], None, ALU.mult).then_inc(gain_done, 1)
            dve.wait_ge(mean_done, 1)
            dve.wait_ge(gain_done, 1)
            dve.tensor_tensor(shift[:], means[:], gain[:], ALU.mult).then_inc(shift_done, 1)
            dve.wait_ge(shift_done, 1)
            dve.tensor_scalar(offset[:], shift[:], c["gnb"], None, ALU.add).then_inc(offset_done, 1)
            for bl in range(BL):
                dve.wait_ge(scaled_done, bl + 1)
                cols = slice(bl * HW, (bl + 1) * HW)
                dve.tensor_tensor(x[:, cols], x[:, cols], scaled[:, bl % 2], ALU.add).then_inc(x_done, 1)


def convolve3(nc, consts, xn, xc):
    with ExitStack() as ctx:
        m = Scope(nc, ctx)
        c, const_in = consts["l3conv"]
        taps = 4
        folded, w = m.sb("c_folded", [P, taps, P]), m.sb("c_w", [P, 2, taps, P], F32R)
        parts = m.sb("c_parts", [P, HALVES, BL, taps + HW], F32R)
        banks = m.banks("c_ps", 4)
        folded_done, w_hi, w_lo, zeroed, hi_done, lo_done, conv_done, silu_done = (
            m.sem("c_" + t) for t in ("foldedd", "whi", "wlo", "zeroed", "hi", "lo", "convd", "silud"))
        block = ctx.enter_context(nc.Block())
        units = [(n, h) for n in range(CHUNKS) for h in range(HALVES)]

        def place(n):
            return n * N // HW, taps + n * N % HW

        @block.tensor
        def _(pe):
            pe.wait_ge(w_lo, 1)
            pe.wait_ge(zeroed, 1)
            for u, (n, h) in enumerate(units):
                bl, at = place(n)
                wait(pe, silu_done, u - 3)
                pe.wait_ge(lo_done, u + 1)
                for back in range(taps):
                    for part in range(2):
                        mm = pe.matmul(banks[u % 4][:], w[:, part, taps - 1 - back],
                                       parts[:, h, bl, at - back:at - back + N], start=(back == 0 and part == 0),
                                       stop=(back == taps - 1 and part == 1))
                mm.then_inc(conv_done, 1)

        @block.scalar
        def _(act):
            def high(n):
                bl, at = place(n)
                for h in range(HALVES):
                    split(act, xn[:, n * N:(n + 1) * N], parts[:, h, bl, at:at + N], h, False).then_inc(hi_done, 1)

            act.wait_ge(folded_done, taps)
            act.activation(w[:, 0], folded[:], ACT.Copy).then_inc(w_hi, 1)
            high(0)
            for u, (n, h) in enumerate(units):
                if h == 0 and n + 1 < CHUNKS:
                    high(n + 1)
                act.wait_ge(conv_done, u + 1)
                act.activation(xc[:, h, n * N:(n + 1) * N], banks[u % 4][:], ACT.Silu,
                               bias=c["convb"]).then_inc(silu_done, 1)

        @block.vector
        def _(dve):
            dve.wait_ge(const_in, 16)
            for k in range(taps):
                dve.tensor_tensor(folded[:, k], c["wxi"], c["convw"][:, k * P:(k + 1) * P],
                                  ALU.mult).then_inc(folded_done, 1)
            dve.memset(parts[:, :, :, 0:taps].bitcast(F32), 0.0).then_inc(zeroed, 1)
            dve.wait_ge(w_hi, 1)
            dve.tensor_tensor(w[:, 1], folded[:], w[:, 0].bitcast(F32), ALU.subtract).then_inc(w_lo, 1)
            for u, (n, h) in enumerate(units):
                bl, at = place(n)
                dve.wait_ge(hi_done, u + 1)
                split(dve, xn[:, n * N:(n + 1) * N], parts[:, h, bl, at:at + N], h, True).then_inc(lo_done, 1)


def project3(nc, consts, src, x, out, resid):
    with ExitStack() as ctx:
        m = Scope(nc, ctx)
        c, const_in = consts["l3post"]
        banks = m.banks("j_ps", 3)
        proj_done, out_done, resid_done = (m.sem("j_" + t) for t in ("projd", "outd", "residd"))
        block = ctx.enter_context(nc.Block())

        @block.tensor
        def _(pe):
            pe.wait_ge(const_in, 16)
            for n in range(CHUNKS):
                wait(pe, out_done, n - 2)
                pe.matmul(banks[n % 3][:], c["wpj"], src[:, n * N:(n + 1) * N], start=True,
                          stop=True).then_inc(proj_done, 1)

        @block.vector
        def _(dve):
            dve.wait_ge(const_in, 16)
            for n in range(CHUNKS):
                cols = slice(n * N, (n + 1) * N)
                dve.wait_ge(proj_done, n + 1)
                dve.scalar_tensor_tensor(out=out[:, cols], in0=banks[n % 3][:], scalar=c["pjb"], in1=x[:, cols],
                                         op0=ALU.add, op1=ALU.add).then_inc(out_done, 1)

        @block.gpsimd
        def _(pool):
            for n in range(CHUNKS):
                cols = slice(n * N, (n + 1) * N)
                pool.wait_ge(out_done, n + 1)
                pool.tensor_tensor(resid[:, cols], out[:, cols], x[:, cols], ALU.add).then_inc(resid_done, 1)


def scan3(nc, consts, xc, selr, ysel):
    with ExitStack() as ctx:
        m = Scope(nc, ctx)
        c, const_in = consts["l3"]
        wdt = m.sb("r_wdtb", [P, P])
        delta, du, rest = m.sb("r_delta", [P, N]), m.sb("r_du", [P, N]), m.sb("r_rest", [P, N])
        relu, ex, one, ln, lost = (m.sb("r_" + t, [P, N]) for t in ("relu", "ex", "one", "ln", "lost"))
        parts = m.sb("r_parts", [P, 2, 3, 2, N], F32R)
        decay, feed = m.sb("r_decay", [P, 2, Q4, N]), m.sb("r_feed", [P, Q4, N])
        state, prod = m.sb("r_state", [P, 2, Q4, N]), m.sb("r_prod", [P, 2, Q4, N])
        carry = m.sb("r_carry", [P, Q4, Q4])
        bs, cs = m.sb("r_bs", [P, 2, Q4, N]), m.sb("r_cs", [P, 2, Q4, N])
        ps_bc, ps_dt, ps_y, ps_s = (m.banks("r_p" + t, 1)[0] for t in ("bc", "dt", "y", "s"))
        ps_d, ps_u = m.banks("r_pd", 2), m.banks("r_pu", 2)
        w_ps, w_done = (m.sem("r_" + t) for t in ("wps", "wd"))
        dt_ps, bc_ps, away_done, relu_done, ex_done, one_done, ln_done, lost_done, rest_done, delta_done, \
            du_done = (m.sem("r_" + t) for t in (
                "dtps", "bcps", "awayd", "relud", "exd", "oned", "lnd", "lostd", "restd", "deltad", "dud"))
        hi_d, hi_u, hi_bc, lo_d, lo_u, lo_bc = (m.sem("r_" + t) for t in ("hid", "hiu", "hibc", "lod", "lou", "lobc"))
        d_ps, decayed, u_rep, fed, scanned, multiplied, b_rep, c_rep, b_copied, c_copied, carried, y_part, y_done = (
            m.sem("r_" + t) for t in ("dps", "decayed", "urep", "fed", "scanned", "mult", "brepd", "crepd", "bcop",
                                      "ccop", "carried", "ypart", "ydone"))
        aneg, a_on_vector, a_on_scalar = prepare_a(m, "r_", c, 4)
        LAG_B, LAG_D, LAG_U, LAG_Y = 2, 5, 6, 7
        DT, DU, BC = range(3)
        block = ctx.enter_context(nc.Block())

        def columns(s, u):
            if isinstance(s, int):
                return slice(s // 4 * N, (s // 4 + 1) * N)
            return ds((s - u % UNROLL) * (N // 4) + u % UNROLL // 4 * N, N)

        @block.tensor
        def _(pe):
            pe.wait_ge(const_in, 16)
            pe.matmul(ps_dt[:, 0:P], c["xpr"][0:16], c["dtw"][0:16], start=True, stop=True).then_inc(w_ps, 1)
            pe.wait_ge(w_done, 1)

            def spread(bank, sel, which, par):
                for part in range(2):
                    mm = pe.matmul(bank[:], selr[:, sel * P:(sel + 1) * P], parts[:, par, which, part],
                                   start=(part == 0), stop=(part == 1))
                return mm

            def body(s, u):
                par = u // 4
                if u % 4 == 0 and live(s, STEPS):
                    cols = columns(s, u)
                    wait(pe, relu_done, s)
                    pe.matmul(ps_dt[:], wdt[:], xc[:, cols], start=True, stop=True).then_inc(dt_ps, 4)
                    wait(pe, lo_bc, s)
                    pe.matmul(ps_bc[:], c["wbc"], xc[:, cols], start=True, stop=True).then_inc(bc_ps, 4)

                def decays(qs):
                    p, v = s - LAG_D, u - LAG_D
                    if not live(p, STEPS):
                        return
                    for q in qs:
                        if v % 4 == 0 and q == 0:
                            pe.wait_ge(lo_d, p + 4)
                        wait(pe, decayed, 4 * p + q - 1)
                        spread(ps_d[q % 2], 4 * q + v % 4, DT, v % UNROLL // 4).then_inc(d_ps, 1)

                def states(which):
                    p, v = s - LAG_B, u - LAG_B
                    if not live(p, STEPS):
                        return
                    if which == 0:
                        if v % 4 == 0:
                            pe.wait_ge(lo_bc, p + 4)
                        wait(pe, c_copied, p)
                    else:
                        pe.wait_ge(b_copied, p + 1)
                    spread(ps_s, 16 + 2 * (v % 4) + which, BC, v % UNROLL // 4).then_inc((b_rep, c_rep)[which], 1)

                def inputs(qs, p, v):
                    if not live(p, STEPS):
                        return
                    for q in qs:
                        if v % 4 == 0 and q == 0:
                            pe.wait_ge(lo_u, p + 4)
                        wait(pe, fed, 4 * p + q - 1)
                        spread(ps_u[q % 2], 4 * q + v % 4, DU, v % UNROLL // 4).then_inc(u_rep, 1)

                inputs((0, 1), s - LAG_U, u - LAG_U)
                decays((0,))
                states(0)
                decays((1,))
                inputs((2, 3), s - LAG_U, u - LAG_U)
                states(1)
                decays((2,))
                decays((3,))
                p, v = s - LAG_Y, u - LAG_Y
                if live(p, STEPS):
                    if v % 4 == 0:
                        wait(pe, y_done, p)
                    pe.wait_ge(multiplied, 4 * p + 4)
                    for q in range(Q4):
                        mm = pe.matmul(ps_y[q * 32:(q + 1) * 32], ysel[:, v % 4 * 32:(v % 4 + 1) * 32],
                                       prod[:, v % 2, q], start=(v % 4 == 0), stop=(v % 4 == 3),
                                       tile_position=(0, q * 32))
                    mm.then_inc(y_part, 1)

            skewed(pe, STEPS, UNROLL, PEEL, body)

        @block.scalar
        def _(act):
            act.preload_act_table_set("natural_log_exp_and_others")
            act.wait_ge(const_in, 16)
            act.wait_ge(w_ps, 1)
            act.activation(wdt[:], ps_dt[:, 0:P], ACT.Copy).then_inc(w_done, 1)
            a_on_scalar(act)

            def body(s, u):
                par, gi = u // 4, s - u % 4
                if u % 4 == 0 and live(s, STEPS):
                    act.wait_ge(dt_ps, gi + 4)
                    wait(act, lost_done, gi)
                    act.activation(ex[:], ps_dt[:], ACT.Abs, bias=c["dtb"]).then_inc(away_done, 4)
                    wait(act, delta_done, gi)
                    act.activation(relu[:], ps_dt[:], ACT.Relu, bias=c["dtb"]).then_inc(relu_done, 4)
                    act.wait_ge(away_done, gi + 4)
                    act.activation(ex[:], ex[:], ACT.Exp, scale=-1.0).then_inc(ex_done, 4)
                if u % 4 == 1 and live(s, STEPS):
                    act.wait_ge(bc_ps, gi + 4)
                    wait(act, c_rep, gi - 4)
                    act.activation(parts[:, par, BC, 0], ps_bc[:], ACT.Copy).then_inc(hi_bc, 4)
                if u % 4 == 2 and live(s, STEPS):
                    act.wait_ge(one_done, gi + 4)
                    wait(act, rest_done, gi)
                    act.activation(ln[:], one[:], ACT.Ln).then_inc(ln_done, 4)
                if u % 4 == 3 and live(s, STEPS):
                    act.wait_ge(delta_done, gi + 4)
                    wait(act, d_ps, 4 * (gi - 4))
                    act.activation(parts[:, par, DT, 0], delta[:], ACT.Copy).then_inc(hi_d, 4)
                if u % 4 == 0 and live(s - 4, STEPS):
                    act.wait_ge(du_done, s)
                    wait(act, u_rep, 4 * (s - 7))
                    act.activation(parts[:, 1 - par, DU, 0], du[:], ACT.Copy).then_inc(hi_u, 4)
                def decays(qs):
                    p, v = s - LAG_D, u - LAG_D
                    if not live(p, STEPS):
                        return
                    for q in qs:
                        act.wait_ge(d_ps, 4 * p + q + 1)
                        wait(act, scanned, 4 * (p - 2) + q + 1)
                        act.activation(decay[:, v % 2, q], ps_d[q % 2][:], ACT.Exp,
                                       scale=aneg[:, v % 4:v % 4 + 1]).then_inc(decayed, 1)

                def states(which):
                    p, v = s - LAG_B, u - LAG_B
                    if not live(p, STEPS):
                        return
                    act.wait_ge((b_rep, c_rep)[which], p + 1)
                    wait(act, (fed, multiplied)[which], 4 * (p - 5) + v % 4 + 1)
                    act.activation((bs, cs)[which][:, v % UNROLL // 4, v % 4], ps_s[:],
                                   ACT.Copy).then_inc((b_copied, c_copied)[which], 1)

                decays((0,))
                states(0)
                decays((1,))
                states(1)
                decays((2, 3))

            skewed(act, STEPS, UNROLL, PEEL, body)

        @block.vector
        def _(dve):
            dve.wait_ge(const_in, 16)
            a_on_vector(dve)

            def body(s, u):
                p, v = s - LAG_U, u - LAG_U
                if live(p, STEPS):
                    b, g, lc = v % 2, v % 4, v % UNROLL // 4
                    def inflow(q):
                        dve.wait_ge(u_rep, 4 * p + q + 1)
                        if g == 0:
                            dve.wait_ge(b_copied, p + q + 1)
                        wait(dve, scanned, 4 * (p - 1) + q + 1)
                        dve.tensor_tensor(feed[:, q], ps_u[q % 2][:], bs[:, lc, q], ALU.mult).then_inc(fed, 1)

                    def scan(q):
                        dve.wait_ge(decayed, 4 * p + q + 1)
                        dve.wait_ge(fed, 4 * p + q + 1)
                        wait(dve, multiplied, 4 * (p - 2) + q + 1)
                        if lc == 1:
                            dve.wait_ge(carried, p - 2 + g)
                            start = carry[:, g, q:q + 1]
                        else:
                            start = 0.0
                        dve.tensor_tensor_scan(state[:, b, q], decay[:, b, q], feed[:, q], start, ALU.mult,
                                               ALU.add).then_inc(scanned, 1)

                    inflow(0)
                    inflow(1)
                    scan(0)
                    scan(1)
                    inflow(2)
                    inflow(3)
                    scan(2)
                    scan(3)
                    if lc == 0:
                        dve.wait_ge(scanned, 4 * p + 4)
                        dve.tensor_copy(carry[:, g], state[:, b, :, N - 1]).then_inc(carried, 2)
                p, v = s - LAG_Y, u - LAG_Y
                if v % 4 == 3 and live(p, STEPS):
                    dve.wait_ge(y_part, p + 1)
                    cols = columns(p, v)
                    dve.wait_ge(du_done, p + 1)
                    dve.scalar_tensor_tensor(out=xc[:, cols], in0=xc[:, cols], scalar=c["dp"], in1=ps_y[:],
                                             op0=ALU.mult, op1=ALU.add).then_inc(y_done, 4)
                if u % 4 == 0 and live(s - 4, STEPS):
                    dve.wait_ge(hi_u, s)
                    wait(dve, u_rep, 4 * (s - 7))
                    dve.tensor_tensor(parts[:, 1 - u // 4, DU, 1], du[:], parts[:, 1 - u // 4, DU, 0].bitcast(F32),
                                      ALU.subtract).then_inc(lo_u, 4)
                if not live(s, STEPS):
                    return
                par, gi = u // 4, s - u % 4
                if u % 4 == 1:
                    dve.wait_ge(ex_done, gi + 4)
                    wait(dve, ln_done, gi)
                    dve.tensor_scalar(one[:], ex[:], 1.0, None, ALU.add).then_inc(one_done, 4)
                    dve.wait_ge(one_done, gi + 4)
                    wait(dve, rest_done, gi)
                    dve.scalar_tensor_tensor(out=lost[:], in0=one[:], scalar=-1.0, in1=ex[:], op0=ALU.add,
                                             op1=ALU.subtract).then_inc(lost_done, 4)
                    dve.wait_ge(hi_bc, gi + 4)
                    wait(dve, c_rep, gi - 4)
                    dve.tensor_tensor(parts[:, par, BC, 1], ps_bc[:], parts[:, par, BC, 0].bitcast(F32),
                                      ALU.subtract).then_inc(lo_bc, 4)
                if u % 4 == 3:
                    dve.wait_ge(hi_d, gi + 4)
                    wait(dve, d_ps, 4 * (gi - 4))
                    dve.tensor_tensor(parts[:, par, DT, 1], delta[:], parts[:, par, DT, 0].bitcast(F32),
                                       ALU.subtract).then_inc(lo_d, 4)

            skewed(dve, STEPS, UNROLL, PEEL, body)

        @block.gpsimd
        def _(pool):
            def body(s, u):
                par, gi = u // 4, s - u % 4
                if u % 4 == 2 and live(s, STEPS):
                    pool.wait_ge(ln_done, gi + 4)
                    pool.wait_ge(lost_done, gi + 4)
                    pool.tensor_tensor(rest[:], ln[:], lost[:], ALU.subtract).then_inc(rest_done, 4)
                    pool.wait_ge(rest_done, gi + 4)
                    pool.wait_ge(relu_done, gi + 4)
                    wait(pool, hi_d, gi)
                    wait(pool, lo_d, gi)
                    pool.tensor_tensor(delta[:], relu[:], rest[:], ALU.add).then_inc(delta_done, 4)
                if u % 4 == 3 and live(s, STEPS):
                    pool.wait_ge(delta_done, gi + 4)
                    wait(pool, hi_u, gi)
                    wait(pool, lo_u, gi)
                    pool.tensor_tensor(du[:], delta[:], xc[:, columns(gi, u - u % 4)], ALU.mult).then_inc(du_done, 4)
                p, v = s - LAG_U, u - LAG_U
                if live(p, STEPS):
                    wait(pool, y_part, p - 1)
                    for q in range(Q4):
                        pool.wait_ge(scanned, 4 * p + q + 1)
                        if v % 4 == 0:
                            pool.wait_ge(c_copied, p + q + 1)
                        pool.tensor_tensor(prod[:, v % 2, q], state[:, v % 2, q], cs[:, v % UNROLL // 4, q],
                                           ALU.mult).then_inc(multiplied, 1)

            skewed(pool, STEPS, UNROLL, PEEL, body)


def load(nc, m, dram, x):
    arrived = [m.sem(f"x_in{bl}") for bl in range(BL)]
    with nc.Block() as block:
        @block.sync
        def _(sp):
            for bl in range(BL):
                for h in range(HALVES):
                    sp.dma_start(x[h * C:(h + 1) * C, bl * HW:(bl + 1) * HW],
                                 dram["x"][h * BL + bl]).then_inc(arrived[bl], 16)
    return arrived


def program(nc, dram, out):
    with ExitStack() as kept:
        m = Scope(nc, kept)
        x, y = m.sb("x_act", [P, COLS]), m.sb("y_inner", [P, HALVES, COLS])
        selr, ysel = m.sb("selr", [P, 24 * P], F32R), m.sb("ysel", [P, 4 * 32])
        arrived = load(nc, m, dram, x)
        with ExitStack() as scan_consts:
            consts = fetch(nc, scan_consts, dram, ["l2"])
            with ExitStack() as first_consts:
                consts |= fetch(nc, first_consts, dram, ["ln", "attn", "mlp0", "scan", "fir"])
                with nc.cleanup_on_exit(), ExitStack() as layer:
                    xn = Scope(nc, layer).sb("x_norm0", [P, COLS])
                    layernorm(nc, consts, "n1", x, xn, "ln1_scale", "ln1_bias", arrived)
                    attention(nc, consts, dram, xn, x)
                    layernorm(nc, consts, "n2", x, xn, "ln2_scale", "ln2_bias")
                    mlp(nc, consts, "m0", "mlp0", xn, x, x)
                with nc.cleanup_on_exit():
                    antialiased(nc, consts, x)
                    selectors(nc, consts, selr, ysel)
            with nc.cleanup_on_exit():
                scan2(nc, consts, x, y, selr, ysel)
        xn = m.sb("x_norm3", [P, COLS])
        with ExitStack() as scan_consts:
            consts = fetch(nc, scan_consts, dram, ["l3"])
            with ExitStack() as first_consts:
                consts |= fetch(nc, first_consts, dram, ["l2post", "ln", "l3conv"], "3")
                with nc.cleanup_on_exit(), ExitStack() as layer:
                    mem = Scope(nc, layer)
                    mixed, sums = mem.sb("mixed2", [P, COLS]), mem.sb("chunk_sums", [P, CHUNKS])
                    gated(nc, consts, "o2", "l2post", x, y, ACT.Gelu, mixed, sums)
                    groupnorm(nc, consts, mixed, sums, x)
                layernorm(nc, consts, "n3", x, xn, "lnw", "lnb")
                convolve3(nc, consts, xn, y)
            scan3(nc, consts, y[:].rearrange("p h n -> p (h n)"), selr, ysel)
        mixed = m.sb("mixed3", [P, COLS])
        consts = fetch(nc, kept, dram, ["l3post", "ln", "mlp3"], "4")
        gated(nc, consts, "o3", "l3post", xn, y, ACT.Silu, mixed)
        layernorm(nc, consts, "n4", mixed, xn, "lnw", "lnb")
        project3(nc, consts, xn, x, mixed, x)
        mlp(nc, consts, "m3", "mlp3", mixed, x, x, out)


def kernel(**inputs):
    import concourse.bacc as _bacc
    from concourse import mybir as _mybir
    from concourse.bass_utils import run_bass_kernel_spmd as _run

    host = {k: np.asarray(v) for k, v in inputs.items()}
    data = pack(host)
    data["x"] = host["x"].reshape(B, C, HW)
    data["rel"] = host["L0_conv_rel_bias_table"].reshape(1, -1)
    nc = _bacc.Bacc("TRN2", target_bir_lowering=False, num_devices=1)
    arrays, dram = {}, {}
    for name, a in data.items():
        a = np.ascontiguousarray(a)
        arrays[f"in_{name}_dram"] = a
        dram[name] = nc.dram_tensor(f"in_{name}_dram", a.shape, _mybir.dt.from_np(a.dtype),
                                    kind="ExternalInput").ap()
    out = nc.dram_tensor("out_0_dram", (B, C, HW), F32, kind="ExternalOutput").ap()
    program(nc, dram, out)
    r = _run(nc, [arrays], core_ids=[0])
    return r.results[0]["out_0_dram"].reshape(B, C, H, W)
```
